# Optimizing a Trainium2 kernel written in Bass

```python
import numpy as np
import jax
import jax.numpy as jnp

def _softmax(x, axis=-1):
    return jax.nn.softmax(x, axis=axis)

def _gelu(x):
    return jax.nn.gelu(x, approximate=True)

def _silu(x):
    return jax.nn.silu(x)

def _sigmoid(x):
    return jax.nn.sigmoid(x)

def _layernorm(x, axis=-1, eps=1e-05):
    m = jnp.mean(x, axis=axis, keepdims=True)
    v = jnp.var(x, axis=axis, keepdims=True)
    return (x - m) / jnp.sqrt(v + eps)

def _scatter_add(tgt, idx, src, axis=0):
    return tgt.at[idx].add(src)

def _segment_sum(src, seg, n):
    return jax.ops.segment_sum(src, seg, n)
kernel_name = 'mk_macaron_d1_jaxref_r8_69cd41'

def setup_inputs(seed: int=0):
    np.random.seed(seed)
    _w = jnp.asarray

    def _L0_attn_setup():
        import jax, jax.numpy as jnp
        import numpy as np
        D = 128
        H = 16
        HD = D // H
        K = 4
        B = 8
        S = 256
        SIZES = [D, D // 2, D, D, D, D, H, H, D]
        OFF = np.cumsum([0] + SIZES)

        def _dwconv_silu(x, w):
            s = x.shape[1]
            xp = jnp.pad(x, ((0, 0), (K - 1, 0), (0, 0)))
            y = sum((xp[:, j:j + s, :] * w[:, j] for j in range(K)))
            return jax.nn.silu(y)

        def _rmsnorm(x, w, eps=1e-06):
            return x * jax.lax.rsqrt(jnp.mean(x * x, axis=-1, keepdims=True) + eps) * w

        def _forward(hidden, W_ctrl, b_ctrl, W_block, qconv_w, kconv_w, vconv_w, rms_m_w, rms_v_w, W_out, b_out):
            b, s, _ = hidden.shape
            ctrl = hidden @ W_ctrl + b_ctrl
            parts = [ctrl[..., OFF[i]:OFF[i + 1]] for i in range(9)]
            ug_in, ang_in, cand_in, q_in, k_in, v_in, a_in, be_in, og_in = parts

            def heads(t):
                return t.reshape(b, s, H, HD)
            q = heads(_dwconv_silu(q_in, qconv_w))
            k = heads(_dwconv_silu(k_in, kconv_w))
            v = heads(_dwconv_silu(v_in, vconv_w))
            q = q * jax.lax.rsqrt(jnp.sum(q * q, axis=-1, keepdims=True) + 1e-12)
            k = k * jax.lax.rsqrt(jnp.sum(k * k, axis=-1, keepdims=True) + 1e-12)
            upd = jax.nn.sigmoid(ug_in)
            ret = 1.0 - upd
            cand = jax.nn.silu(cand_in)
            cos_a = jnp.cos(ang_in)
            sin_a = jnp.sin(ang_in)
            alpha = jax.nn.sigmoid(a_in)
            beta = jax.nn.sigmoid(be_in)
            tm = lambda t: jnp.moveaxis(t, 1, 0)
            xs = (tm(upd), tm(ret), tm(cand), tm(cos_a), tm(sin_a), tm(q), tm(k), tm(v), tm(alpha), tm(beta))
            vec0 = jnp.zeros((b, D), dtype=hidden.dtype)
            S0 = jnp.zeros((b, H, HD, HD), dtype=hidden.dtype)

            def step(carry, x):
                vec, St = carry
                u, r, c, ca, sa, qt, kt, vt, at, bt = x
                vp = jnp.einsum('bpi,pij->bpj', vec.reshape(b, D // 2, 2), W_block)
                x1, x2 = (vp[..., 0], vp[..., 1])
                rot = jnp.stack([x1 * ca - x2 * sa, x1 * sa + x2 * ca], axis=-1).reshape(b, D)
                vec_new = u * rot + r * c
                pred = jnp.einsum('bhij,bhi->bhj', St, kt)
                delta = vt - pred
                S_new = at[..., None, None] * St + bt[..., None, None] * (kt[..., :, None] * delta[..., None, :])
                read = jnp.einsum('bhij,bhi->bhj', S_new, qt)
                return ((vec_new, S_new), (vec_new, read))
            _, (vec_states, reads) = jax.lax.scan(step, (vec0, S0), xs)
            vec_states = jnp.moveaxis(vec_states, 0, 1)
            reads = jnp.moveaxis(reads, 0, 1)
            m = _rmsnorm(reads, rms_m_w).reshape(b, s, D)
            vread = _rmsnorm(vec_states, rms_v_w)
            gate = jax.nn.sigmoid(og_in)
            return (jnp.concatenate([m, vread], axis=-1) @ W_out + b_out) * gate
        key = jax.random.key(seed)
        ks = jax.random.split(key, 10)
        tot = int(OFF[-1])
        W_ctrl = jax.random.normal(ks[0], (D, tot), dtype=jnp.float32) / np.sqrt(D)
        b = np.zeros(tot, np.float32)
        b[OFF[6]:OFF[7]] = 1.5
        b[OFF[7]:OFF[8]] = -2.0
        b[OFF[8]:OFF[9]] = -1.5
        b_ctrl = jnp.asarray(b)
        W_block = jax.random.normal(ks[1], (D // 2, 2, 2), dtype=jnp.float32) * 0.1

        def conv_w(k):
            w = jax.random.normal(k, (D, K), dtype=jnp.float32) * 0.02
            return w.at[:, -1].add(1.0)
        qconv_w = conv_w(ks[2])
        kconv_w = conv_w(ks[3])
        vconv_w = conv_w(ks[4])
        rms_m_w = jnp.ones((HD,), dtype=jnp.float32)
        rms_v_w = jnp.ones((D,), dtype=jnp.float32)
        W_out = jax.random.normal(ks[5], (2 * D, D), dtype=jnp.float32) * 0.02
        b_out = jnp.zeros((D,), dtype=jnp.float32)
        hidden = jax.random.normal(ks[6], (B, S, D), dtype=jnp.float32)
        return {'hidden': hidden, 'W_ctrl': W_ctrl, 'b_ctrl': b_ctrl, 'W_block': W_block, 'qconv_w': qconv_w, 'kconv_w': kconv_w, 'vconv_w': vconv_w, 'rms_m_w': rms_m_w, 'rms_v_w': rms_v_w, 'W_out': W_out, 'b_out': b_out}
    _L0_attn_in = _L0_attn_setup()

    def _L0_ffn_setup():
        import jax, jax.numpy as jnp
        import numpy as np
        TOP_K = 2
        key = jax.random.key(seed)
        ks = jax.random.split(key, 5)
        B, S, H, I, E = (4, 256, 128, 512, 8)
        scale_hi = (2.0 / (H + I)) ** 0.5
        scale_he = (2.0 / (H + E)) ** 0.5
        return {'x': jax.random.normal(ks[0], (B, S, H), dtype=jnp.float32), 'router_w': jax.random.normal(ks[1], (E, H), dtype=jnp.float32) * scale_he, 'gate_w': jax.random.normal(ks[2], (E, I, H), dtype=jnp.float32) * scale_hi, 'up_w': jax.random.normal(ks[3], (E, I, H), dtype=jnp.float32) * scale_hi, 'down_w': jax.random.normal(ks[4], (E, H, I), dtype=jnp.float32) * scale_hi}
    _L0_ffn_in = _L0_ffn_setup()
    _d = {'L0_attn_hidden': _L0_attn_in['hidden'], 'L0_attn_W_ctrl': _L0_attn_in['W_ctrl'], 'L0_attn_b_ctrl': _L0_attn_in['b_ctrl'], 'L0_attn_W_block': _L0_attn_in['W_block'], 'L0_attn_qconv_w': _L0_attn_in['qconv_w'], 'L0_attn_kconv_w': _L0_attn_in['kconv_w'], 'L0_attn_vconv_w': _L0_attn_in['vconv_w'], 'L0_attn_rms_m_w': _L0_attn_in['rms_m_w'], 'L0_attn_rms_v_w': _L0_attn_in['rms_v_w'], 'L0_attn_W_out': _L0_attn_in['W_out'], 'L0_attn_b_out': _L0_attn_in['b_out'], 'L0_ffn_router_w': _L0_ffn_in['router_w'], 'L0_ffn_gate_w': _L0_ffn_in['gate_w'], 'L0_ffn_up_w': _L0_ffn_in['up_w'], 'L0_ffn_down_w': _L0_ffn_in['down_w']}
    _x0 = _d['L0_attn_hidden']
    _d['L0_attn_hidden'] = jax.random.normal(jax.random.fold_in(jax.random.key(seed), 1), (8, 512, 128), dtype=_x0.dtype)
    del _x0
    return _d

def reference(L0_attn_hidden, L0_attn_W_ctrl, L0_attn_b_ctrl, L0_attn_W_block, L0_attn_qconv_w, L0_attn_kconv_w, L0_attn_vconv_w, L0_attn_rms_m_w, L0_attn_rms_v_w, L0_attn_W_out, L0_attn_b_out, L0_ffn_router_w, L0_ffn_gate_w, L0_ffn_up_w, L0_ffn_down_w):

    def _L0_attn_ref(hidden, W_ctrl, b_ctrl, W_block, qconv_w, kconv_w, vconv_w, rms_m_w, rms_v_w, W_out, b_out):
        import jax, jax.numpy as jnp
        import numpy as np
        D = 128
        H = 16
        HD = D // H
        K = 4
        B = 8
        S = 256
        SIZES = [D, D // 2, D, D, D, D, H, H, D]
        OFF = np.cumsum([0] + SIZES)

        def _dwconv_silu(x, w):
            s = x.shape[1]
            xp = jnp.pad(x, ((0, 0), (K - 1, 0), (0, 0)))
            y = sum((xp[:, j:j + s, :] * w[:, j] for j in range(K)))
            return jax.nn.silu(y)

        def _rmsnorm(x, w, eps=1e-06):
            return x * jax.lax.rsqrt(jnp.mean(x * x, axis=-1, keepdims=True) + eps) * w

        def _forward(hidden, W_ctrl, b_ctrl, W_block, qconv_w, kconv_w, vconv_w, rms_m_w, rms_v_w, W_out, b_out):
            b, s, _ = hidden.shape
            ctrl = hidden @ W_ctrl + b_ctrl
            parts = [ctrl[..., OFF[i]:OFF[i + 1]] for i in range(9)]
            ug_in, ang_in, cand_in, q_in, k_in, v_in, a_in, be_in, og_in = parts

            def heads(t):
                return t.reshape(b, s, H, HD)
            q = heads(_dwconv_silu(q_in, qconv_w))
            k = heads(_dwconv_silu(k_in, kconv_w))
            v = heads(_dwconv_silu(v_in, vconv_w))
            q = q * jax.lax.rsqrt(jnp.sum(q * q, axis=-1, keepdims=True) + 1e-12)
            k = k * jax.lax.rsqrt(jnp.sum(k * k, axis=-1, keepdims=True) + 1e-12)
            upd = jax.nn.sigmoid(ug_in)
            ret = 1.0 - upd
            cand = jax.nn.silu(cand_in)
            cos_a = jnp.cos(ang_in)
            sin_a = jnp.sin(ang_in)
            alpha = jax.nn.sigmoid(a_in)
            beta = jax.nn.sigmoid(be_in)
            tm = lambda t: jnp.moveaxis(t, 1, 0)
            xs = (tm(upd), tm(ret), tm(cand), tm(cos_a), tm(sin_a), tm(q), tm(k), tm(v), tm(alpha), tm(beta))
            vec0 = jnp.zeros((b, D), dtype=hidden.dtype)
            S0 = jnp.zeros((b, H, HD, HD), dtype=hidden.dtype)

            def step(carry, x):
                vec, St = carry
                u, r, c, ca, sa, qt, kt, vt, at, bt = x
                vp = jnp.einsum('bpi,pij->bpj', vec.reshape(b, D // 2, 2), W_block)
                x1, x2 = (vp[..., 0], vp[..., 1])
                rot = jnp.stack([x1 * ca - x2 * sa, x1 * sa + x2 * ca], axis=-1).reshape(b, D)
                vec_new = u * rot + r * c
                pred = jnp.einsum('bhij,bhi->bhj', St, kt)
                delta = vt - pred
                S_new = at[..., None, None] * St + bt[..., None, None] * (kt[..., :, None] * delta[..., None, :])
                read = jnp.einsum('bhij,bhi->bhj', S_new, qt)
                return ((vec_new, S_new), (vec_new, read))
            _, (vec_states, reads) = jax.lax.scan(step, (vec0, S0), xs)
            vec_states = jnp.moveaxis(vec_states, 0, 1)
            reads = jnp.moveaxis(reads, 0, 1)
            m = _rmsnorm(reads, rms_m_w).reshape(b, s, D)
            vread = _rmsnorm(vec_states, rms_v_w)
            gate = jax.nn.sigmoid(og_in)
            return (jnp.concatenate([m, vread], axis=-1) @ W_out + b_out) * gate
        return _forward(hidden, W_ctrl, b_ctrl, W_block, qconv_w, kconv_w, vconv_w, rms_m_w, rms_v_w, W_out, b_out)

    def _L0_ffn_ref(x, router_w, gate_w, up_w, down_w):
        import jax, jax.numpy as jnp
        import numpy as np
        TOP_K = 2
        B, S, H = x.shape
        E = router_w.shape[0]
        xf = x.reshape(-1, H)
        logits = xf @ router_w.T
        probs = jax.nn.softmax(logits, axis=-1)
        topk_p, topk_i = jax.lax.top_k(probs, TOP_K)
        topk_p = topk_p / topk_p.sum(axis=-1, keepdims=True)

        def body(out, inputs):
            e, gw, uw, dw = inputs
            sel = topk_i == e
            mask = sel.any(axis=-1)
            w_tok = (topk_p * sel).sum(axis=-1)
            cnt = mask.sum().astype(xf.dtype)
            mean_w = jnp.where(cnt > 0, w_tok.sum() / jnp.maximum(cnt, 1.0), 0.0)
            h = jax.nn.silu(xf @ gw.T) * (xf @ uw.T)
            eo = h @ dw.T
            out = out + mask[:, None].astype(xf.dtype) * eo * mean_w
            return (out, None)
        out0 = jnp.zeros_like(xf)
        out, _ = jax.lax.scan(body, out0, (jnp.arange(E), gate_w, up_w, down_w))
        return out.reshape(B, S, H)
    x = L0_attn_hidden
    x = x + 0.5 * _L0_ffn_ref(_layernorm(x, axis=-1), L0_ffn_router_w, L0_ffn_gate_w, L0_ffn_up_w, L0_ffn_down_w)
    x = x + _L0_attn_ref(_layernorm(x, axis=-1), L0_attn_W_ctrl, L0_attn_b_ctrl, L0_attn_W_block, L0_attn_qconv_w, L0_attn_kconv_w, L0_attn_vconv_w, L0_attn_rms_m_w, L0_attn_rms_v_w, L0_attn_W_out, L0_attn_b_out)
    x = x + 0.5 * _L0_ffn_ref(_layernorm(x, axis=-1), L0_ffn_router_w, L0_ffn_gate_w, L0_ffn_up_w, L0_ffn_down_w)
    return x

_drawn_inputs = setup_inputs


def setup_inputs(seed=0):
    import zlib

    import numpy as np

    out = dict(_drawn_inputs(seed))
    spreads = {'L0_attn_rms_m_w': (1.0, 0.6), 'L0_attn_rms_v_w': (1.0, 0.6), 'L0_attn_b_out': (0.0, 0.1)}
    factors = {'L0_attn_W_block': 7.24}
    for name, (base, spread) in spreads.items():
        noise = np.random.default_rng([zlib.crc32(name.encode()), seed]).standard_normal(out[name].shape)
        drawn = base * np.exp(spread * noise) if base else spread * noise
        out[name] = jnp.asarray(drawn.astype(out[name].dtype))
    for name, factor in factors.items():
        out[name] = (out[name] * factor).astype(out[name].dtype)
    return out
```

```python
from contextlib import ExitStack

import numpy as np
import concourse.bass as bass
from concourse import mybir

P = 128
B, S, D = 8, 512, 128
H, HD, KT = 16, 8, 4
E, I = 8, 512
CH = I // P
NB = S // P
TILES = NB * B
G = TILES // 4
NPAIR = D // 2
BB = B // 2
C_UG, C_ANG, C_CAND, C_Q, C_K, C_V, C_A, C_BE, C_OG, C_END = np.cumsum(
    [0, D, D // 2, D, D, D, D, H, H, D]).tolist()
PAIR_ROWS = 5
HEAD_ROWS = 3 * HD + 2
FIRST = PAIR_ROWS * NPAIR + D
SECOND = HEAD_ROWS * H
HT = 32
RD = 32

L_BQKV, L_BAB, L_CONV = 0, 24, 26
L_BU = L_CONV + 3 * HD * KT
L_BC = L_BU + 2
L_BANG = L_BC + 2
L_WB = L_BANG + 1
L_RMSV = L_WB + 4
L_RMSM = L_RMSV + 2
L_BOG = L_RMSM + HD
L_BOUT = L_BOG + D
L_ID = L_BOUT + D
L_PAIR = L_ID + P
L_END = L_PAIR + 2

LN_EPS, RMS_EPS, NORM_EPS = 1e-5, 1e-6, 1e-12
TWO_PI = 2 * np.pi
TWO_PI_HI = 6.28125
TWO_PI_LO = TWO_PI - TWO_PI_HI
ROUND = 1.5 * 2 ** 23
PI_DOWN = 3.1415925
VEC_DOWN = 2.0 ** -20
VEC_CUT = 1e23
VEC_OVER = 2.0 ** 128 * VEC_DOWN ** 2
SCORE_FLOOR = -87.0

ALU = mybir.AluOpType
ACT = mybir.ActivationFunctionType
F32 = mybir.dt.float32
AX = mybir.AxisListType
ds = bass.ds

RING_CREDIT, H_CREDIT, DOWN_CREDIT, ACC_CREDIT, COPY_CREDIT = 2, 2, 4, 2, 1

ROUTER_USES = 4 * NB + 1
BLOCK_USES = 2 + 16 + 12 + 2 + 4
RING_ROUTER1 = 0
RING_ATT = ROUTER_USES
RING_ROUTER2 = RING_ATT + NB * BLOCK_USES


def over(ap, axis, n):
    a = ap.unsqueeze(axis)
    shape = list(a.shape)
    shape[axis] = n
    return a.broadcast_to(shape)


class Chain:

    def __init__(self, eng, sem):
        self.eng, self.sem, self.base, self.k, self.saved = eng, sem, 0, 0, []

    def link(self, ins):
        ins.then_inc(self.sem, 1)
        self.k += 1
        self.eng.wait_ge(self.sem, self.base + self.k)

    def enter(self, i, per):
        self.saved.append((self.base, self.k))
        self.base, self.k = self.base + self.k + i * per, 0

    def leave(self, rounds, per):
        assert self.k == per, (self.k, per)
        self.base, k = self.saved.pop()
        self.k = k + rounds * per


def macaron_kernel(nc, hidden, w_ctrl, lane_consts, w_mem, w_vec, router_wt, gate_wt, up_wt, down_wt, out):
    ctx = ExitStack()
    with ctx:
        def sb(name, shape):
            return ctx.enter_context(nc.sbuf_tensor(name, shape, F32))

        def sem(name):
            return ctx.enter_context(nc.semaphore(name))

        X = sb("X", [P, TILES, D])
        gate_w = sb("gate_w", [P, E, I])
        up_w = sb("up_w", [P, E, I])
        down_w = sb("down_w", [P, E, CH, D])
        ctrl_w = sb("ctrl_w", [P, C_END])
        mem_w = sb("mem_w", [P, HD, 2 * D])
        vec_w = sb("vec_w", [P, 2, 2 * D])
        rout_w = sb("rout_w", [P, E])
        lc = sb("lc", [P, L_END])
        ident = lc[:, L_ID:L_ID + P]
        ones = sb("ones", [P, P])
        xnT_all = sb("xnT_all", [P, TILES * P])
        xnT_cur = sb("xnT_cur", [P, B * P])
        stats = sb("stats", [P, 4, B])
        tok_w = sb("tok_w", [P, TILES, E])
        sums = sb("sums", [P, 4, 2 * E])
        silu = sb("silu", [P, 2, 4 * P])
        hT = sb("hT", [P, 4, 4 * P])
        region = sb("region", [P, B * C_OG])
        pair_rows = region[:, 0:PAIR_ROWS * B * NPAIR].rearrange("p (r b m) -> p r b m", b=B, m=NPAIR)
        head_rows = region[:, PAIR_ROWS * B * NPAIR:].rearrange("p (r b h) -> p r b h", b=B, h=H)
        qkv = region[:, 0:3 * HD * P].rearrange("p (s i t) -> p s i t", s=3, i=HD)
        reads = region[:, 0:HD * P].rearrange("p (t j) -> p t j", j=HD)
        memT = region[:, HD * P:2 * HD * P].rearrange("p (j t) -> p j t", j=HD)
        X0 = 3 * HD * P
        prod_q = region[:, X0:X0 + RD * 64].rearrange("p (t i j) -> p t i j", i=HD, j=HD)
        reads_sq = region[:, X0:X0 + HD * P].rearrange("p (t j) -> p t j", j=HD)
        ym = region[:, X0:X0 + B * D].rearrange("p (b d) -> p b d", d=D)
        yv = region[:, X0 + B * D - 0:X0 + 2 * B * D].rearrange("p (b d) -> p b d", d=D)
        router_tmp = region[:, 0:10 * TILES * E].rearrange("p (k m e) -> p k m e", k=10, e=E)
        gate = sb("gate", [P, B, D])
        raw_f = sb("raw_f", [P, 3 * HD * (P + KT - 1)])
        raw = raw_f[:, :].rearrange("p (s i t) -> p s i t", s=3, i=HD)
        qn = raw_f[:, 0:P * HD].rearrange("p (t i) -> p t i", i=HD)
        kb = raw_f[:, P * HD:2 * P * HD].rearrange("p (t i) -> p t i", i=HD)
        tail = sb("tail", [P, 3, HD, KT - 1])
        kx = sb("kx", [P, P, HD + 1])
        ab = sb("ab", [P, 2, P])
        states = sb("states", [P, HT + 1, HD + 1, HD])
        prod_k = sb("prod_k", [P, (HD + 1) * HD])
        delta = sb("delta", [P, HD])
        outer = sb("outer", [P, HD * HD])
        upd = sb("upd", [P, 2, BB, P])
        xc = upd[:, :, :, :].rearrange("p c b t -> p (c b t)").rearrange("p (b d) -> p b d", d=D)
        cand = sb("cand", [P, 2, BB, P])
        ang = sb("ang", [P, BB * P])
        sin_a = sb("sin_a", [P, BB * P])
        cos_a = sb("cos_a", [P, BB * P])
        rot = sb("rot", [P, 2, 2, BB, P])
        qk_sq = rot[:, :, :, :, :].rearrange("p a c b t -> p (a c b t)").rearrange(
            "p (s i t) -> p s i t", s=2, i=HD)
        norms = sb("norms", [P, 2, P])
        vec = sb("vec", [P, P + 1, 2 * BB])
        vprod = sb("vprod", [P, 2, 2 * BB])
        vsum = sb("vsum", [P, 2, BB])
        scr = sb("scr", [P, 2 * BB * P])
        sq = scr[:, :].rearrange("p (b d) -> p b d", d=D)
        part = scr[:, :].rearrange("p (k n) -> p k n", k=2)
        vec_sq = scr[:, :].rearrange("p (c t) -> p c t", t=P)
        rv = sb("rv", [P, B])
        vec_ss = sb("vec_ss", [P, B])
        vec_cut = sb("vec_cut", [P, 2 * BB, P])
        epsv = sb("epsv", [P, 4])
        order = sb("order", [P, E])

        gate_ps = ctx.enter_context(nc.psum_tensor("gate_ps", [P, 2, 4 * P], F32))
        up_ps = ctx.enter_context(nc.psum_tensor("up_ps", [P, 2, 4 * P], F32))
        eo_ps = ctx.enter_context(nc.psum_tensor("eo_ps", [P, 2, 4, D], F32))
        turn = ctx.enter_context(nc.psum_tensor("turn", [P, 2, 4 * P], F32))

        x_in, c_in, w_in, e_in, x_out = sem("x_in"), sem("c_in"), sem("w_in"), sem("e_in"), sem("x_out")
        consts_ready = sem("consts_ready")
        dve_step, pool_step = sem("dve_step"), sem("pool_step")
        centered, squared, var_ready, std_ready, xn_ready = (
            sem(n) for n in ("centered", "squared", "var_ready", "std_ready", "xn_ready"))
        turned, turn_free = sem("turned"), sem("turn_free")
        xnT_ready, xnT_copied = sem("xnT_ready"), sem("xnT_copied")
        logits_ready, shifted, exps_ready, colsums_ready, tokw_ready = (
            sem(n) for n in ("logits_ready", "shifted", "exps_ready", "colsums_ready", "tokw_ready"))
        sums_seen = sem("sums_seen")
        gate_ready, up_ready, silu_ready, h_ready, down_done, acc_done, group_done = (
            sem(n) for n in ("gate_ready", "up_ready", "silu_ready", "h_ready", "down_done", "acc_done", "group_done"))
        att_free, ctrl_ready, og_biased, gate_sig = (
            sem(n) for n in ("att_free", "ctrl_ready", "og_biased", "gate_sig"))
        lanes_ready, ang_reduced, sincos_ready, conv_ready, conv_act, qk_squared, qk_ssq, qk_std = (
            sem(n) for n in ("lanes_ready", "ang_reduced", "sincos_ready", "conv_ready", "conv_act",
                             "qk_squared", "qk_ssq", "qk_std"))
        rot_ready, vec_ready, vec_squared = sem("rot_ready"), sem("vec_ready"), sem("vec_squared")
        reads_ready, reads_squared, reads_ssq, reads_std, mem_ready = (
            sem(n) for n in ("reads_ready", "reads_squared", "reads_ssq", "reads_std", "mem_ready"))
        vstd_ready, rv_ready, y_ready = sem("vstd_ready"), sem("rv_ready"), sem("y_ready")

        block = ctx.enter_context(nc.Block())

        hid = hidden.rearrange("b (n t) d -> t n b d", t=P)
        res = out.rearrange("b (n t) d -> t n b d", t=P)

        @block.sync
        def _(sp):
            sp.dma_start(lc[:, :], lane_consts).then_inc(c_in, 16)
            sp.dma_start(rout_w[:, :], router_wt).then_inc(c_in, 16)
            for n in range(NB):
                sp.dma_start(X[:, n * B:(n + 1) * B, :], hid[:, n]).then_inc(x_in, 16)
            sp.dma_start(gate_w[:, :, :], gate_wt).then_inc(e_in, 16)
            sp.dma_start(up_w[:, :, :], up_wt).then_inc(e_in, 16)
            sp.dma_start(down_w[:, :, :, :], down_wt).then_inc(e_in, 16)
            sp.dma_start(ctrl_w[:, :], w_ctrl).then_inc(w_in, 16)
            sp.dma_start(mem_w[:, :, :], w_mem).then_inc(w_in, 16)
            sp.dma_start(vec_w[:, :, :], w_vec).then_inc(w_in, 16)
            for g in range(G):
                sp.wait_ge(group_done, G + g + 1)
                b0 = 4 * (g % 2)
                sp.dma_start(res[:, g // 2, b0:b0 + 4], X[:, 4 * g:4 * g + 4, :]).then_inc(x_out, 16)
            sp.wait_ge(x_out, 16 * G)

        @block.tensor
        def _(pe):
            def bank(u):
                return turn[:, u % 2, :]

            def ln_turns(u, layer):
                pe.wait_ge(xn_ready, layer + 1)
                for half in range(2):
                    pe.wait_ge(turn_free, u[0] + half + 1)
                    for b in range(4):
                        last = pe.transpose(turn[:, (u[1] + half) % 2, b * P:(b + 1) * P],
                                            xc[:, 4 * half + b, :], ident)
                    last.then_inc(turned, 1)

            def router(u0, layer0, phase):
                with pe.Fori(0, NB) as n:
                    ln_turns((u0 + 4 * n, u0), layer0 + n)
                    pe.wait_ge(xnT_ready, 2 * (layer0 + n + 1))
                    for half in range(2):
                        pe.wait_ge(turn_free, u0 + 4 * n + 2 + half + 1)
                        for b in range(4):
                            t0 = (4 * half + b) * P
                            last = pe.matmul(turn[:, (u0 + half) % 2, b * E:(b + 1) * E],
                                             xnT_cur[:, t0:t0 + P], rout_w[:, :], start=True, stop=True)
                        last.then_inc(turned, 1)
                u = u0 + 4 * NB
                pe.wait_ge(turn_free, u + 1)
                pe.wait_ge(colsums_ready, phase + 1)
                pe.matmul(turn[:, u % 2, 0:2 * E], ones[:, :], sums[:, 0, :],
                          start=True, stop=True).then_inc(turned, 1)

            def experts(phase):
                pe.wait_ge(e_in, 48)
                pe.wait_ge(xnT_copied, NB * (phase + 1) + COPY_CREDIT)
                with pe.Fori(0, G) as g:
                    toks = xnT_all[:, ds(g * 4 * P, 4 * P)]
                    q0 = (phase * G + g) * E * CH
                    k0 = (phase * G + g) * E

                    def down(q):
                        e, c = q // CH, q % CH
                        pe.wait_ge(h_ready, q0 + q + 1 + H_CREDIT)
                        if c == 0:
                            pe.wait_ge(acc_done, k0 + e + 1)
                        for t in range(4):
                            last = pe.matmul(eo_ps[:, e % 2, t, :], hT[:, q % 4, t * P:(t + 1) * P],
                                             down_w[:, e, c, :], start=(c == 0 and t == 0),
                                             stop=(c == CH - 1), skip_group_check=True)
                        last.then_inc(down_done, 1)

                    for q in range(E * CH):
                        e, c = q // CH, q % CH
                        pe.wait_ge(h_ready, q0 + q + 1)
                        pe.matmul(gate_ps[:, q % 2, :], gate_w[:, e, c * P:(c + 1) * P], toks,
                                  start=True, stop=True).then_inc(gate_ready, 1)
                        pe.matmul(up_ps[:, q % 2, :], up_w[:, e, c * P:(c + 1) * P], toks,
                                  start=True, stop=True).then_inc(up_ready, 1)
                        if q:
                            down(q - 1)
                    down(E * CH - 1)

            def attention():
                pe.wait_ge(w_in, 48)
                with pe.Fori(0, NB) as n:
                    U = RING_ATT + n * BLOCK_USES
                    ln_turns((U, RING_ATT), NB + n)
                    pe.wait_ge(xnT_ready, 2 * (NB + n + 1))
                    s = RING_ATT + 2
                    for b in range(B):
                        for half in range(2):
                            pe.wait_ge(turn_free, U + 2 + 2 * b + half + 1)
                            c0, width = ((0, FIRST), (FIRST, SECOND))[half]
                            pe.matmul(turn[:, (s + half) % 2, 0:width], xnT_cur[:, b * P:(b + 1) * P],
                                      ctrl_w[:, c0:c0 + width], start=True, stop=True).then_inc(turned, 1)
                    pe.wait_ge(ctrl_ready, 2 * B * (n + 1))
                    u = 2 + 2 * B

                    def lane_group(u, cols):
                        pe.wait_ge(turn_free, U + u + 1)
                        for k, col in enumerate(cols):
                            last = pe.transpose(turn[0:P, (RING_ATT + u) % 2, k * P:(k + 1) * P], col, ident)
                        last.then_inc(turned, 1)

                    def heads(r):
                        return head_rows[:, r].rearrange("p b h -> p (b h)")

                    def pairs(r, bb):
                        return pair_rows[:, r, 2 * bb:2 * bb + 2, :].rearrange("p b m -> p (b m)")

                    for r0 in range(0, 3 * HD, 4):
                        lane_group(u, [heads(r0 + r) for r in range(4)])
                        u += 1
                    for r in (0, 1):
                        lane_group(u, [pairs(r, bb) for bb in range(BB)])
                        u += 1
                    lane_group(u, [heads(3 * HD), heads(3 * HD + 1)])
                    u += 1
                    for r in (2, 3, 4):
                        lane_group(u, [pairs(r, bb) for bb in range(BB)])
                        u += 1
                    pe.wait_ge(vec_squared, n + 1)
                    for half in range(2):
                        pe.wait_ge(turn_free, U + u + 1)
                        for k in range(2):
                            for c in range(2):
                                last = pe.matmul(turn[:, (RING_ATT + u) % 2, 2 * k:2 * k + 2],
                                                 vec_sq[:, c * BB + 2 * half + k, :],
                                                 lc[:, L_PAIR:L_PAIR + 2], start=(c == 0), stop=(c == 1))
                        last.then_inc(turned, 1)
                        u += 1
                    pe.wait_ge(mem_ready, n + 1)
                    for bp in range(BB):
                        pe.wait_ge(turn_free, U + u + 1)
                        bk = (RING_ATT + u) % 2
                        for j in range(HD):
                            pe.matmul(turn[:, bk, 0:2 * D], memT[32 * bp:32 * bp + 32, j, :],
                                      mem_w[32 * bp:32 * bp + 32, j, :], start=(j == 0), stop=(j == HD - 1),
                                      tile_position=(32 * bp, 0))
                        for c in range(2):
                            last = pe.matmul(turn[:, bk, 2 * D:4 * D], vec_cut[:, c * BB + bp, :],
                                             vec_w[:, c, :], start=(c == 0), stop=(c == 1))
                        last.then_inc(turned, 1)
                        u += 1
                    assert u == BLOCK_USES

            pe.wait_ge(c_in, 32)
            pe.wait_ge(consts_ready, 1)
            router(RING_ROUTER1, 0, 0)
            experts(0)
            attention()
            router(RING_ROUTER2, 2 * NB, 1)
            experts(1)

        @block.scalar
        def _(act):
            def ln_part(layer, n8):
                act.wait_ge(centered, layer + 1)
                act.activation(sq, xc, ACT.Square).then_inc(squared, 1)
                act.wait_ge(var_ready, layer + 1)
                act.activation(stats[:, 1, :], stats[:, 0, :], ACT.Sqrt, bias=eps_ln,
                               scale=1.0 / D).then_inc(std_ready, 1)

            def router(u0, layer0, phase):
                with act.Fori(0, NB) as n:
                    ln_part(layer0 + n, None)
                    for half in range(2):
                        act.wait_ge(turned, u0 + 4 * n + half + 1)
                        if half == 0:
                            act.wait_ge(xnT_copied, phase * NB + n + 1)
                        act.activation(xnT_cur[:, half * 4 * P:(half + 1) * 4 * P],
                                       turn[:, (u0 + half) % 2, :], ACT.Copy).then_inc(xnT_ready, 1)
                        act.wait_ge(xnT_ready, 2 * (layer0 + n) + half + 1)
                        act.sem_inc(turn_free, 1)
                    for half in range(2):
                        act.wait_ge(turned, u0 + 4 * n + 2 + half + 1)
                        act.activation(router_tmp[:, 0, ds(n * B + half * 4, 4), :],
                                       turn[:, (u0 + half) % 2, 0:4 * E].rearrange("p (b e) -> p b e", e=E),
                                       ACT.Copy).then_inc(turn_free, 1)
                act.wait_ge(shifted, phase + 1)
                act.activation(router_tmp[:, 2], router_tmp[:, 1], ACT.Exp).then_inc(exps_ready, 1)
                act.wait_ge(turned, u0 + 4 * NB + 1)
                act.activation(sums[:, 1, :], turn[:, (u0 + 4 * NB) % 2, 0:2 * E], ACT.Copy).then_inc(turn_free, 1)

            def experts(phase):
                with act.Fori(0, G) as g:
                    q0 = (phase * G + g) * E * CH
                    for q in range(E * CH):
                        act.wait_ge(gate_ready, q0 + q + 1)
                        act.wait_ge(h_ready, q0 + q + 1)
                        act.activation(silu[:, q % 2, :], gate_ps[:, q % 2, :], ACT.Silu).then_inc(silu_ready, 1)

            def attention():
                with act.Fori(0, NB) as n:
                    U = RING_ATT + n * BLOCK_USES
                    ln_part(NB + n, None)
                    for half in range(2):
                        act.wait_ge(turned, U + half + 1)
                        act.activation(xnT_cur[:, half * 4 * P:(half + 1) * 4 * P],
                                       turn[:, (RING_ATT + half) % 2, :], ACT.Copy).then_inc(xnT_ready, 1)
                        act.wait_ge(xnT_ready, 2 * (NB + n) + half + 1)
                        act.sem_inc(turn_free, 1)
                    act.wait_ge(att_free, n + 1)
                    for b in range(B):
                        for half in range(2):
                            act.wait_ge(turned, U + 2 + 2 * b + half + 1)
                            src = turn[:, (RING_ATT + half) % 2, :]
                            if half == 0:
                                act.activation(pair_rows[:, :, b, :], src[:, 0:FIRST - D].rearrange(
                                    "p (r m) -> p r m", m=NPAIR), ACT.Copy)
                                last = act.activation(gate[:, b, :], src[:, FIRST - D:FIRST], ACT.Copy)
                            else:
                                last = act.activation(head_rows[:, :, b, :], src[:, 0:SECOND].rearrange(
                                    "p (r h) -> p r h", h=H), ACT.Copy)
                            last.then_inc(ctrl_ready, 1)
                            act.wait_ge(ctrl_ready, 2 * (B * n + b) + half + 1)
                            act.sem_inc(turn_free, 1)
                    u = 2 + 2 * B

                    def src(u, k0, k1):
                        return turn[:, (RING_ATT + u) % 2, k0 * P:k1 * P]

                    for part3 in range(3):
                        for i0 in (0, 4):
                            act.wait_ge(turned, U + u + 1)
                            for i in range(4):
                                col = L_BQKV + part3 * HD + i0 + i
                                last = act.activation(raw[:, part3, i0 + i, KT - 1:], src(u, i, i + 1), ACT.Identity,
                                                      bias=lc[:, col:col + 1])
                            last.then_inc(turn_free, 1)
                            u += 1
                    for c in range(2):
                        act.wait_ge(turned, U + u + 1)
                        act.activation(upd[:, c].rearrange("p b t -> p (b t)"), src(u, 0, 4), ACT.Sigmoid,
                                       bias=lc[:, L_BU + c:L_BU + c + 1]).then_inc(turn_free, 1)
                        u += 1
                    act.wait_ge(turned, U + u + 1)
                    act.activation(ab[:, 0, :], src(u, 0, 1), ACT.Sigmoid, bias=lc[:, L_BAB:L_BAB + 1])
                    act.activation(ab[:, 1, :], src(u, 1, 2), ACT.Sigmoid,
                                   bias=lc[:, L_BAB + 1:L_BAB + 2]).then_inc(turn_free, 1)
                    u += 1
                    act.wait_ge(og_biased, n + 1)
                    act.activation(gate[:, :, :], gate[:, :, :], ACT.Sigmoid).then_inc(gate_sig, 1)
                    act.wait_ge(turned, U + u + 1)
                    act.activation(ang[:, :], src(u, 0, 4), ACT.Identity,
                                   bias=lc[:, L_BANG:L_BANG + 1]).then_inc(turn_free, 1)
                    u += 1
                    for c in range(2):
                        act.wait_ge(turned, U + u + 1)
                        act.activation(cand[:, c].rearrange("p b t -> p (b t)"), src(u, 0, 4), ACT.Silu,
                                       bias=lc[:, L_BC + c:L_BC + c + 1]).then_inc(turn_free, 1)
                        u += 1
                    act.wait_ge(conv_ready, n + 1)
                    act.activation(qkv, qkv, ACT.Silu).then_inc(conv_act, 1)
                    act.wait_ge(conv_act, n + 1)
                    act.activation(qk_sq, qkv[:, 0:2], ACT.Square).then_inc(qk_squared, 1)
                    act.wait_ge(ang_reduced, n + 1)
                    act.activation(sin_a[:, :], ang[:, :], ACT.Sin)
                    act.activation(cos_a[:, :], cos_a[:, :], ACT.Sin).then_inc(sincos_ready, 1)
                    act.wait_ge(qk_ssq, n + 1)
                    act.activation(norms[:, :, :], norms[:, :, :], ACT.Sqrt, bias=eps_norm).then_inc(qk_std, 1)
                    act.wait_ge(vec_ready, n + 1)
                    act.activation(vec_sq, vec_cut[:, :, :], ACT.Square, scale=VEC_DOWN).then_inc(vec_squared, 1)
                    for half in range(2):
                        act.wait_ge(turned, U + u + 1)
                        act.activation(vec_ss[:, 4 * half:4 * half + 4], src(u, 0, 4)[:, 0:4], ACT.Copy)
                        act.activation(rv[:, 4 * half:4 * half + 4], src(u, 0, 4)[:, 0:4], ACT.Sqrt, bias=eps_vec,
                                       scale=1.0 / D).then_inc(vstd_ready, 1)
                        act.wait_ge(vstd_ready, 2 * n + half + 1)
                        act.sem_inc(turn_free, 1)
                        u += 1
                    act.wait_ge(reads_ready, n + 1)
                    act.activation(reads_sq, reads, ACT.Square).then_inc(reads_squared, 1)
                    act.wait_ge(reads_ssq, n + 1)
                    act.activation(norms[:, 0, :], norms[:, 0, :], ACT.Sqrt, bias=eps_rms,
                                   scale=1.0 / HD).then_inc(reads_std, 1)
                    act.wait_ge(rv_ready, n + 1)
                    for bp in range(BB):
                        act.wait_ge(turned, U + u + 1)
                        act.activation(ym[:, 2 * bp:2 * bp + 2, :],
                                       src(u, 0, 2).rearrange("p (b d) -> p b d", d=D), ACT.Copy)
                        for b2 in range(2):
                            last = act.activation(yv[:, 2 * bp + b2, :], src(u, 2 + b2, 3 + b2), ACT.Copy,
                                                  scale=rv[:, 2 * bp + b2:2 * bp + b2 + 1])
                        last.then_inc(y_ready, 1)
                        act.wait_ge(y_ready, BB * n + bp + 1)
                        act.sem_inc(turn_free, 1)
                        u += 1

            eps_ln, eps_rms, eps_norm, eps_vec = (epsv[:, k:k + 1] for k in range(4))
            act.wait_ge(c_in, 32)
            act.wait_ge(consts_ready, 1)
            router(RING_ROUTER1, 0, 0)
            experts(0)
            attention()
            router(RING_ROUTER2, 2 * NB, 1)
            experts(1)

        @block.vector
        def _(dve):
            chain = Chain(dve, dve_step)
            link = chain.link

            def layernorm(layer, x_block):
                link(dve.tensor_reduce(stats[:, 0, :], x_block, AX.X, ALU.add))
                link(dve.tensor_scalar(stats[:, 2, :], stats[:, 0, :], 1.0 / D, None, ALU.mult))
                dve.tensor_tensor(xc, x_block, over(stats[:, 2, :], 2, D), ALU.subtract).then_inc(centered, 1)
                dve.wait_ge(squared, layer + 1)
                dve.tensor_reduce(stats[:, 0, :], sq, AX.X, ALU.add).then_inc(var_ready, 1)
                dve.wait_ge(std_ready, layer + 1)
                link(dve.reciprocal(stats[:, 3, :], stats[:, 1, :]))
                dve.tensor_tensor(xc, xc, over(stats[:, 3, :], 2, D), ALU.mult).then_inc(xn_ready, 1)

            def router(u0, layer0, phase):
                chain_per = 3
                with dve.Fori(0, NB) as n:
                    chain.enter(n, chain_per)
                    layernorm(layer0 + n, X[:, ds(n * B, B), :])
                    dve.wait_ge(xnT_ready, 2 * (layer0 + n + 1))
                    dve.tensor_copy(xnT_all[:, ds(n * B * P, B * P)], xnT_cur[:, :]).then_inc(xnT_copied, 1)
                chain.leave(NB, chain_per)
                dve.wait_ge(turn_free, u0 + 4 * NB + RING_CREDIT)
                lg, z, ex, m1, m2, rank, z2, w = (router_tmp[:, k] for k in range(8))
                top = sums[:, 2:4, :].rearrange("p a e -> p (a e)")

                def per_tile(a):
                    return over(a, 2, E)

                link(dve.tensor_reduce(top, lg, AX.X, ALU.max))
                link(dve.tensor_tensor(z, lg, per_tile(top), ALU.subtract))
                dve.tensor_scalar(z, z, SCORE_FLOOR, None, ALU.max).then_inc(shifted, 1)
                dve.wait_ge(shifted, phase + 1)

                def pick(m, scores):
                    link(dve.tensor_reduce(top, scores, AX.X, ALU.max))
                    link(dve.tensor_tensor(m, scores, per_tile(top), ALU.is_equal))
                    link(dve.tensor_tensor(m, m, over(order[:, :], 1, TILES), ALU.mult))
                    link(dve.tensor_reduce(top, m, AX.X, ALU.max))
                    link(dve.tensor_tensor(m, m, per_tile(top), ALU.is_equal))

                pick(m1, z)
                link(dve.scalar_tensor_tensor(z2, m1, -1e4, z, ALU.mult, ALU.add))
                pick(m2, z2)
                link(dve.tensor_tensor(m1, m1, m2, ALU.add))
                dve.wait_ge(exps_ready, phase + 1)
                link(dve.tensor_tensor(w, m1, ex, ALU.mult))
                link(dve.tensor_reduce(top, w, AX.X, ALU.add))
                link(dve.reciprocal(top, top))
                link(dve.tensor_tensor(w, w, per_tile(top), ALU.mult))
                link(dve.tensor_reduce(sums[:, 0, 0:E], w.rearrange("p m e -> p e m"), AX.X, ALU.add))
                dve.tensor_reduce(sums[:, 0, E:2 * E], m1.rearrange("p m e -> p e m"), AX.X,
                                  ALU.add).then_inc(colsums_ready, 1)
                dve.wait_ge(turn_free, u0 + ROUTER_USES + RING_CREDIT)
                cnt, tot = sums[:, 1, E:2 * E], sums[:, 1, 0:E]
                link(dve.tensor_scalar(cnt, cnt, 1.0, None, ALU.max))
                link(dve.reciprocal(cnt, cnt))
                link(dve.scalar_tensor_tensor(tot, tot, 0.5, cnt, ALU.mult, ALU.mult))
                link(dve.tensor_tensor(tok_w[:, :, :], m1, over(tot, 1, TILES), ALU.mult))

            def experts(phase):
                with dve.Fori(0, G) as g:
                    q0 = (phase * G + g) * E * CH
                    k0 = (phase * G + g) * E
                    for q in range(E * CH):
                        e, c = q // CH, q % CH
                        dve.wait_ge(silu_ready, q0 + q + 1)
                        dve.wait_ge(up_ready, q0 + q + 1)
                        dve.wait_ge(down_done, q0 + q + 1)
                        dve.tensor_tensor(hT[:, q % 4, :], silu[:, q % 2, :], up_ps[:, q % 2, :],
                                          ALU.mult).then_inc(h_ready, 1)
                        if c == 1 and e > 0:
                            accumulate(g, k0, q0, e - 1)
                    accumulate(g, k0, q0, E - 1)
                    dve.wait_ge(acc_done, k0 + E + ACC_CREDIT)
                    dve.sem_inc(group_done, 1)

            def accumulate(g, k0, q0, e):
                dve.wait_ge(down_done, q0 + (e + 1) * CH + DOWN_CREDIT)
                dve.wait_ge(acc_done, k0 + e + ACC_CREDIT)
                for t in range(4):
                    x = X[:, ds(g * 4 + t, 1), :].rearrange("p a d -> p (a d)")
                    last = dve.scalar_tensor_tensor(x, eo_ps[:, e % 2, t, :],
                                                    tok_w[:, ds(g * 4 + t, 1), e], x, ALU.mult, ALU.add)
                last.then_inc(acc_done, 1)

            def att_block(n):
                U = RING_ATT + n * BLOCK_USES
                layernorm(NB + n, X[:, ds(n * B, B), :])
                dve.wait_ge(ctrl_ready, 2 * B * (n + 1))
                dve.tensor_tensor(gate[:, :, :], gate[:, :, :], over(lc[:, L_BOG:L_BOG + D], 1, B),
                                  ALU.add).then_inc(og_biased, 1)
                link(dve.tensor_copy(raw[:, :, :, 0:KT - 1], tail[:, :, :, :]))
                u = 2 + 2 * B + 6
                dve.wait_ge(turn_free, U + u + RING_CREDIT)
                for j in range(KT):
                    for s in range(3):
                        for i in range(HD):
                            col = L_CONV + (s * HD + i) * KT + j
                            w = lc[:, col:col + 1]
                            src = raw[:, s, i, j:j + P]
                            dst = qkv[:, s, i, :]
                            if j == 0:
                                if s == 0 and i == 0:
                                    dve.wait_ge(turned, U + 2 + 2 * B + 12)
                                last = dve.tensor_scalar(dst, src, w, None, ALU.mult)
                            else:
                                last = dve.scalar_tensor_tensor(dst, src, w, dst, ALU.mult, ALU.add)
                    if j < KT - 1:
                        link(last)
                    else:
                        last.then_inc(conv_ready, 1)
                link(dve.tensor_copy(tail[:, :, :, :], raw[:, :, :, P:P + KT - 1]))
                dve.wait_ge(turn_free, U + 2 + 2 * B + 12 + RING_CREDIT)
                link(dve.tensor_scalar(cos_a[:, :], ang[:, :], 1.0 / TWO_PI, ROUND, ALU.mult, ALU.add))
                link(dve.tensor_scalar(cos_a[:, :], cos_a[:, :], ROUND, None, ALU.subtract))
                link(dve.scalar_tensor_tensor(ang[:, :], cos_a[:, :], -TWO_PI_HI, ang[:, :], ALU.mult, ALU.add))
                link(dve.scalar_tensor_tensor(ang[:, :], cos_a[:, :], -TWO_PI_LO, ang[:, :], ALU.mult, ALU.add))
                link(dve.tensor_scalar(ang[:, :], ang[:, :], PI_DOWN, -PI_DOWN, ALU.min, ALU.max))
                link(dve.scalar_tensor_tensor(cos_a[:, :], ang[:, :], -1.0, ang[:, :], ALU.mult, ALU.min))
                dve.tensor_scalar(cos_a[:, :], cos_a[:, :], np.pi / 2, None, ALU.add).then_inc(ang_reduced, 1)
                dve.wait_ge(qk_squared, n + 1)
                dve.tensor_reduce(norms[:, :, :], qk_sq.rearrange("p s i t -> p s t i"), AX.X,
                                  ALU.add).then_inc(qk_ssq, 1)
                U_, C_ = (a[:, :, :, :].rearrange("p c b t -> p (c b t)") for a in (upd, cand))
                link(dve.tensor_tensor(scr[:, :], U_, C_, ALU.mult))
                link(dve.tensor_tensor(C_, C_, scr[:, :], ALU.subtract))
                dve.wait_ge(qk_std, n + 1)
                link(dve.reciprocal(norms[:, :, :], norms[:, :, :]))
                dve.tensor_tensor(qn.rearrange("p t i -> p i t"), qkv[:, 0], over(norms[:, 0, :], 1, HD), ALU.mult)
                link(dve.scalar_tensor_tensor(kx[:, :, 0:HD].rearrange("p t i -> p i t"), qkv[:, 1], -1.0,
                                              over(norms[:, 1, :], 1, HD), ALU.mult, ALU.mult))
                link(dve.scalar_tensor_tensor(kb, kx[:, :, 0:HD], -1.0, over(ab[:, 1, :], 2, HD),
                                              ALU.mult, ALU.mult))
                dve.wait_ge(sincos_ready, n + 1)
                for c in range(2):
                    w0, w1 = (lc[:, L_WB + 2 * c + k:L_WB + 2 * c + k + 1] for k in range(2))
                    dve.tensor_scalar(part[:, 0, :], cos_a[:, :], w0, None, ALU.mult)
                    link(dve.tensor_scalar(part[:, 1, :], sin_a[:, :], w0, None, ALU.mult))
                    dve.scalar_tensor_tensor(part[:, 0, :], sin_a[:, :], w1, part[:, 0, :], ALU.mult, ALU.subtract)
                    link(dve.scalar_tensor_tensor(part[:, 1, :], cos_a[:, :], w1, part[:, 1, :], ALU.mult, ALU.add))
                    r0, r1 = (rot[:, k, c].rearrange("p b t -> p (b t)") for k in range(2))
                    u0, u1 = (upd[:, k].rearrange("p b t -> p (b t)") for k in range(2))
                    dve.scalar_tensor_tensor(r0, part[:, 0, :], -1.0, u0, ALU.mult, ALU.mult)
                    last = dve.tensor_tensor(r1, part[:, 1, :], u1, ALU.mult)
                    if c == 0:
                        link(last)
                    else:
                        last.then_inc(rot_ready, 1)
                for half in range(P // HT):
                    t0 = half * HT
                    link(dve.tensor_copy(states[:, 0:HT, HD, :],
                                         qkv[:, 2, :, t0:t0 + HT].rearrange("p j t -> p t j")))
                    per = 4
                    dve.nop(nofuse=True)
                    with dve.Fori(0, HT) as t:
                        chain.enter(t, per)
                        st = states[:, ds(t, 1), :, :].rearrange("p a i j -> p (a i) j")
                        nx = states[:, ds(t + 1, 1), 0:HD, :].rearrange("p a i j -> p (a i) j")
                        k_t = kx[:, ds(t + t0, 1), :].rearrange("p a i -> p (a i)")
                        kb_t = kb[:, ds(t + t0, 1), :].rearrange("p a i -> p (a i)")
                        pk = prod_k[:, :].rearrange("p (i j) -> p i j", j=HD)
                        ou = outer[:, :].rearrange("p (i j) -> p i j", j=HD)
                        link(dve.tensor_tensor(pk, st, over(k_t, 2, HD), ALU.mult))
                        link(dve.tensor_reduce(delta[:, :], pk.rearrange("p i j -> p j i"), AX.X, ALU.add))
                        link(dve.tensor_tensor(ou, over(kb_t, 2, HD), over(delta[:, :], 1, HD), ALU.mult))
                        link(dve.scalar_tensor_tensor(nx, st[:, 0:HD, :], ab[:, 0, ds(t + t0, 1)], ou,
                                                      ALU.mult, ALU.add))
                    chain.leave(HT, per)
                    for r in range(HT // RD):
                        q_r = qn[:, t0 + r * RD:t0 + (r + 1) * RD, :]
                        for a in range(1):
                            link(dve.tensor_tensor(prod_q, states[:, 1 + r * RD:1 + (r + 1) * RD, 0:HD, :],
                                                   over(q_r, 3, HD), ALU.mult))
                        link(dve.tensor_reduce(reads[:, t0 + r * RD:t0 + (r + 1) * RD, :],
                                               prod_q.rearrange("p t i j -> p t j i"), AX.X, ALU.add))
                    link(dve.tensor_copy(states[:, 0, 0:HD, :], states[:, HT, 0:HD, :]))
                dve.sem_inc(reads_ready, 1)
                dve.wait_ge(reads_squared, n + 1)
                dve.tensor_reduce(norms[:, 0, :], reads_sq, AX.X, ALU.add).then_inc(reads_ssq, 1)
                dve.wait_ge(reads_std, n + 1)
                link(dve.reciprocal(norms[:, 0, :], norms[:, 0, :]))
                dve.tensor_tensor(memT.rearrange("p j t -> p t j"), reads, over(norms[:, 0, :], 2, HD),
                                  ALU.mult).then_inc(mem_ready, 1)
                dve.wait_ge(vstd_ready, 2 * (n + 1))
                link(dve.reciprocal(rv[:, :], rv[:, :]))
                link(dve.tensor_scalar(vec_ss[:, :], vec_ss[:, :], VEC_OVER, VEC_DOWN, ALU.is_lt, ALU.mult))
                dve.tensor_tensor(rv[:, :], rv[:, :], vec_ss[:, :], ALU.mult).then_inc(rv_ready, 1)
                dve.wait_ge(y_ready, BB * (n + 1))
                link(dve.tensor_tensor(ym, ym, yv, ALU.add))
                link(dve.tensor_tensor(ym, ym, over(lc[:, L_BOUT:L_BOUT + D], 1, B), ALU.add))
                dve.wait_ge(gate_sig, n + 1)
                link(dve.tensor_tensor(ym, ym, gate[:, :, :], ALU.mult))
                xb = X[:, ds(n * B, B), :]
                link(dve.tensor_tensor(xb, xb, ym, ALU.add))
                dve.sem_inc(att_free, 1)

            dve.memset(ones[:, :], 1.0)
            for k, v in enumerate((LN_EPS, RMS_EPS, NORM_EPS, RMS_EPS * VEC_DOWN ** 2)):
                dve.memset(epsv[:, k:k + 1], v)
            for e in range(E):
                dve.memset(order[:, e:e + 1], float(E - e))
            dve.memset(tail[:, :, :, :], 0.0)
            dve.memset(states[:, 0, 0:HD, :], 0.0)
            dve.memset(kx[:, :, HD], 1.0)
            link(dve.memset(delta[:, :], 0.0))
            dve.sem_inc(consts_ready, 1)
            dve.sem_inc(turn_free, RING_CREDIT)
            dve.sem_inc(h_ready, H_CREDIT)
            dve.sem_inc(down_done, DOWN_CREDIT)
            dve.sem_inc(acc_done, ACC_CREDIT)
            dve.sem_inc(xnT_copied, COPY_CREDIT)

            dve.wait_ge(x_in, 16 * NB)
            router(RING_ROUTER1, 0, 0)
            dve.wait_ge(w_in, 48)
            for j in range(HD):
                dve.tensor_scalar(mem_w[:, j, :], mem_w[:, j, :], lc[:, L_RMSM + j:L_RMSM + j + 1], None, ALU.mult)
            for c in range(2):
                last = dve.tensor_scalar(vec_w[:, c, :], vec_w[:, c, :], lc[:, L_RMSV + c:L_RMSV + c + 1], None,
                                         ALU.mult)
            link(last)
            dve.sem_inc(att_free, 1)
            experts(0)
            PER = 3 + 1 + 3 + 1 + 6 + 2 + 3 + 5 + (P // HT) * (1 + 4 * HT + 2 * (HT // RD) + 1) + 1 + 2 + 4
            with dve.Fori(0, NB) as n:
                chain.enter(n, PER)
                att_block(n)
            chain.leave(NB, PER)
            router(RING_ROUTER2, 2 * NB, 1)
            experts(1)

        @block.gpsimd
        def _(pool):
            chain = Chain(pool, pool_step)
            link = chain.link
            link(pool.memset(vec[:, P, :], 0.0))
            PER = 1 + 3 * P
            with pool.Fori(0, NB) as n:
                pool.wait_ge(rot_ready, n + 1)
                pool.wait_ge(att_free, n + 1)
                pool.nop(nofuse=True)
                chain.enter(n, PER)
                link(pool.tensor_copy(vec[:, 0, :], vec[:, P, :]))
                pool.nop(nofuse=True)
                with pool.Fori(0, P) as t:
                    chain.enter(t, 3)
                    now = vec[:, ds(t, 1), :].rearrange("p a c -> p (a c)")
                    A = rot[:, :, :, :, ds(t, 1)].rearrange("p r c b t -> p r (c b t)")
                    link(pool.tensor_tensor(vprod[:, :, :], A, over(now, 1, 2), ALU.mult))
                    link(pool.tensor_tensor(vsum[:, :, :], vprod[:, :, 0:BB], vprod[:, :, BB:2 * BB], ALU.add))
                    nxt = vec[:, ds(t + 1, 1), :].rearrange("p a (c b) -> p (a c) b", b=BB)
                    c_t = cand[:, :, :, ds(t, 1)].rearrange("p c b t -> p c (b t)")
                    link(pool.tensor_tensor(nxt, vsum[:, :, :], c_t, ALU.add))
                chain.leave(P, 3)
                pool.tensor_scalar(vec_cut[:, :, :], vec[:, 1:P + 1, :].rearrange("p t c -> p c t"),
                                   VEC_CUT, -VEC_CUT, ALU.min, ALU.max).then_inc(vec_ready, 1)
            chain.leave(NB, PER)


def lane_constants(x):
    bc = x["L0_attn_b_ctrl"]
    lc = np.zeros((P, L_END), np.float32)
    lanes_bh = lambda a: np.tile(a, (B, 1))
    lanes_bp = lambda a: np.tile(a, (2, 1))
    q = bc[C_Q:C_A].reshape(3, H, HD).transpose(1, 0, 2).reshape(H, 3 * HD)
    lc[:, L_BQKV:L_BAB] = lanes_bh(q)
    lc[:, L_BAB:L_CONV] = lanes_bh(bc[C_A:C_OG].reshape(2, H).T)
    w = np.stack([x[f"L0_attn_{k}conv_w"] for k in "qkv"]).reshape(3, H, HD * KT)
    lc[:, L_CONV:L_BU] = lanes_bh(w.transpose(1, 0, 2).reshape(H, -1))
    lc[:, L_BU:L_BC] = lanes_bp(bc[C_UG:C_ANG].reshape(NPAIR, 2))
    lc[:, L_BC:L_BANG] = lanes_bp(bc[C_CAND:C_Q].reshape(NPAIR, 2))
    lc[:, L_BANG:L_WB] = lanes_bp(bc[C_ANG:C_CAND].reshape(NPAIR, 1))
    lc[:, L_WB:L_RMSV] = lanes_bp(x["L0_attn_W_block"].reshape(NPAIR, 4))
    lc[:, L_RMSV:L_RMSM] = lanes_bp(x["L0_attn_rms_v_w"].reshape(NPAIR, 2))
    lc[:, L_RMSM:L_BOG] = x["L0_attn_rms_m_w"]
    lc[:, L_BOG:L_BOUT] = bc[C_OG:C_END]
    lc[:, L_BOUT:L_ID] = x["L0_attn_b_out"]
    lc[:, L_ID:L_PAIR] = np.eye(P, dtype=np.float32)
    lc[:, L_PAIR:L_END] = np.repeat(np.eye(2, dtype=np.float32), NPAIR, axis=0)
    return lc


def control_columns():
    by_pair = lambda c0: c0 + np.arange(D).reshape(NPAIR, 2).T.ravel()
    by_head = lambda c0: c0 + np.arange(D).reshape(H, HD).T.ravel()
    return np.concatenate([by_pair(C_UG), np.arange(C_ANG, C_CAND), by_pair(C_CAND), np.arange(C_OG, C_END),
                           by_head(C_Q), by_head(C_K), by_head(C_V), np.arange(C_A, C_OG)])


def kernel(**inputs):
    import concourse.bacc as bacc
    from concourse.bass_utils import run_bass_kernel_spmd

    x = {k: np.asarray(v) for k, v in inputs.items()}
    w_out = x["L0_attn_W_out"]
    mem = w_out[:D].reshape(H, HD, D)
    w_mem = np.zeros((B, H, HD, 2, D), np.float32)
    for b in range(B):
        w_mem[b, :, :, b % 2] = mem
    w_vec = np.zeros((2, NPAIR, 2, 2, D), np.float32)
    for b in range(2):
        w_vec[b, :, :, b] = w_out[D:].reshape(NPAIR, 2, D)
    arrays = {
        "hidden": x["L0_attn_hidden"],
        "w_ctrl": x["L0_attn_W_ctrl"][:, control_columns()],
        "lane_consts": lane_constants(x),
        "w_mem": w_mem.reshape(P, HD, 2 * D),
        "w_vec": w_vec.reshape(P, 2, 2 * D),
        "router_wt": x["L0_ffn_router_w"].T,
        "gate_wt": x["L0_ffn_gate_w"].transpose(2, 0, 1),
        "up_wt": x["L0_ffn_up_w"].transpose(2, 0, 1),
        "down_wt": x["L0_ffn_down_w"].reshape(E, D, CH, P).transpose(3, 0, 2, 1),
    }
    arrays = {k: np.ascontiguousarray(v) for k, v in arrays.items()}
    nc = bacc.Bacc("TRN2", target_bir_lowering=False, num_devices=1)
    args = [nc.dram_tensor(k, v.shape, F32, kind="ExternalInput").ap() for k, v in arrays.items()]
    out = nc.dram_tensor("out", (B, S, D), F32, kind="ExternalOutput").ap()
    macaron_kernel(nc, *args, out)
    r = run_bass_kernel_spmd(nc, [arrays], core_ids=[0])
    return r.results[0]["out"]
```

```python
from contextlib import ExitStack

import numpy as np
import concourse.bass as bass
from concourse import mybir

P = 128
B, S, D = 8, 512, 128
H, HD, KT = 16, 8, 4
E, I = 8, 512
CH = I // P
NB = S // P
TILES = NB * B
TOP_K = 2
TOK = TILES * P
SLOT_TILES = TOK * TOP_K // P + E
R = 8
GATHER_LOOPS = SLOT_TILES // R
ADD_TILES = R // TOP_K
ADD_LOOPS = TILES // ADD_TILES
NPAIR = D // 2
BB = B // 2
C_UG, C_ANG, C_CAND, C_Q, C_K, C_V, C_A, C_BE, C_OG, C_END = np.cumsum(
    [0, D, D // 2, D, D, D, D, H, H, D]).tolist()
PAIR_ROWS = 5
HEAD_ROWS = 3 * HD + 2
FIRST = PAIR_ROWS * NPAIR + D
SECOND = HEAD_ROWS * H
QKV = 3 * D
CK = 4
NC = P // CK
SEG = 8
NG = P // SEG

L_BU = 0
L_BC = L_BU + 2
L_BANG = L_BC + 2
L_WB = L_BANG + 1
L_RMSV = L_WB + 4
L_RMSM = L_RMSV + 2
L_BOG = L_RMSM + HD
L_BOUT = L_BOG + D
L_ID = L_BOUT + D
L_PAIR = L_ID + P
L_IOTA = L_PAIR + 2
L_TOK = L_IOTA + P
L_TRI = L_TOK + TILES
L_TAPS = L_TRI + P
L_END = L_TAPS + P

LN_EPS, RMS_EPS, NORM_EPS = 1e-5, 1e-6, 1e-12
TWO_PI = 2 * np.pi
TWO_PI_HI = 6.28125
TWO_PI_LO = TWO_PI - TWO_PI_HI
ROUND = 1.5 * 2 ** 23
PI_DOWN = 3.1415925
VEC_DOWN = 2.0 ** -20
VEC_CUT = 1e23
VEC_OVER = 2.0 ** 128 * VEC_DOWN ** 2
SCORE_FLOOR = -87.0

ALU = mybir.AluOpType
ACT = mybir.ActivationFunctionType
F32 = mybir.dt.float32
U32 = mybir.dt.uint32
I32 = mybir.dt.int32
AX = mybir.AxisListType
ds = bass.ds

RING_CREDIT = 2
ROWS_CREDIT = R
X_CREDIT, UP_CREDIT, SILU_CREDIT, H_CREDIT, TURN_CREDIT, HT_CREDIT, DOWN_CREDIT, EO_CREDIT = 1, 2, 2, 2, 2, 2, 2, 1
ARENA = 36000
STORES = 4

ROUTER_USES = 4 * NB + 3
BLOCK_USES = 2 + 16 + 12 + 2 + 4
RING_ROUTER1 = 0
RING_ATT = ROUTER_USES
STAGE_USES = 2 + 16 + 12
RING_ROUTER2 = RING_ATT + NB * BLOCK_USES


def over(ap, axis, n):
    a = ap.unsqueeze(axis)
    shape = list(a.shape)
    shape[axis] = n
    return a.broadcast_to(shape)


class Chain:

    def __init__(self, eng, sem):
        self.eng, self.sem, self.base, self.k, self.saved = eng, sem, 0, 0, []

    def link(self, ins):
        ins.then_inc(self.sem, 1)
        self.k += 1
        self.eng.wait_ge(self.sem, self.base + self.k)

    def restart(self):
        self.eng.sem_clear(self.sem)
        self.base, self.k = 0, 0

    def mark(self, ins):
        ins.then_inc(self.sem, 1)
        self.k += 1
        return self.k

    def reached(self, k):
        self.eng.wait_ge(self.sem, k)

    def enter(self, i, per):
        self.saved.append((self.base, self.k))
        self.base, self.k = self.base + self.k + i * per, 0

    def leave(self, rounds, per):
        assert self.k == per, (self.k, per)
        self.base, k = self.saved.pop()
        self.k = k + rounds * per


def macaron_kernel(nc, hidden, w_first, w_second, taps, tap_rows_in, bias_second, lane_consts, w_mem, w_vec, router_wt, gate_wt, up_wt, down_wt, out):
    ctx = ExitStack()
    with ctx:
        def sb(name, shape):
            return ctx.enter_context(nc.sbuf_tensor(name, shape, F32))

        def sem(name):
            return ctx.enter_context(nc.semaphore(name))

        X = sb("X", [P, TILES, D])
        first_w = sb("first_w", [P, FIRST])
        second_w = sb("second_w", [P, KT, SECOND])
        second_b = sb("second_b", [KT, SECOND])
        tap_rows = sb("tap_rows", [KT, SECOND])
        tap_in = sb("tap_in", [KT, P])
        mem_w = sb("mem_w", [P, HD, 2 * D])
        vec_w = sb("vec_w", [P, 2, 2 * D])
        rout_w = sb("rout_w", [P, E])
        lc = sb("lc", [P, L_END])
        ident = lc[:, L_ID:L_ID + P]
        ones = sb("ones", [P, P])
        arena = sb("arena", [P, ARENA])

        class Space:
            def __init__(self, at):
                self.at = at

            def take(self, size):
                self.at += size
                assert self.at <= ARENA, self.at
                return arena[:, self.at - size:self.at]

        ffn = Space(0)
        gate_w = ffn.take(E * I).rearrange("p (e i) -> p e i", e=E)
        up_w = ffn.take(E * I).rearrange("p (e i) -> p e i", e=E)
        down_w = ffn.take(E * CH * D).rearrange("p (e c d) -> p e c d", e=E, c=CH)
        rows = ffn.take(R * D).rearrange("p (r d) -> p r d", d=D)
        xsT = ffn.take(2 * P).rearrange("p (k t) -> p k t", k=2)
        silu = ffn.take(2 * I).rearrange("p (k t) -> p k t", k=2)
        hid = ffn.take(2 * I).rearrange("p (k t) -> p k t", k=2)
        hT = ffn.take(2 * I).rearrange("p (k t) -> p k t", k=2)
        eo = ffn.take(STORES * D).rearrange("p (k t) -> p k t", k=STORES)
        onehot = ffn.take(4 * (P + SLOT_TILES)).rearrange("p (k t) -> p k t", k=4)
        second_tmp = ffn.take(SECOND)
        router_tmp = ffn.take(13 * TILES * E).rearrange("p (k m e) -> p k m e", k=13, e=E)
        att = Space(0)
        region = att.take(B * C_OG)
        pair_rows = region[:, 0:PAIR_ROWS * B * NPAIR].rearrange("p (r b m) -> p r b m", b=B, m=NPAIR)
        head_rows = region[:, PAIR_ROWS * B * NPAIR:].rearrange("p (r b h) -> p r b h", b=B, h=H)
        qkv = att.take(3 * HD * P).rearrange("p (s i t) -> p s i t", s=3, i=HD)
        gate_raw = att.take(B * D).rearrange("p (b d) -> p b d", d=D)
        gate = att.take(B * D).rearrange("p (b d) -> p b d", d=D)
        upd = att.take(2 * BB * P)
        cand = att.take(2 * BB * P)
        ang = att.take(BB * P)
        pre = Space(att.at)
        kn = pre.take(P * HD).rearrange("p (t i) -> p t i", i=HD)
        qn = pre.take(P * HD).rearrange("p (t i) -> p t i", i=HD)
        kb = pre.take(P * HD).rearrange("p (t i) -> p t i", i=HD)
        score = pre.take(10 * NC * HD)
        fwd = pre.take(3 * NC * 2 * HD)
        sin_a = pre.take(BB * P)
        cos_a = pre.take(BB * P)
        sq = score[:, 0:B * D].rearrange("p (b d) -> p b d", d=D)
        qk_sq = score[:, 0:2 * HD * P].rearrange("p (s i t) -> p s i t", s=2, i=HD)
        during = Space(att.at)
        pred = during.take(2 * CK * HD * (HD + 1)).rearrange("p (k t j i) -> p k t j i", k=2, t=CK, j=HD)
        outer = during.take(HD * HD * (CK + 1)).rearrange("p (x s) -> p x s", s=CK + 1)
        post = Space(att.at)
        terms = post.take(2 * NC * HD * 3 * CK).rearrange("p (k c j x) -> p k c j x", k=2, j=HD, x=3 * CK)
        reads = post.take(HD * P).rearrange("p (t j) -> p t j", j=HD)
        reads_sq = post.take(HD * P).rearrange("p (t j) -> p t j", j=HD)
        late = Space(att.at)
        memT = late.take(HD * P).rearrange("p (j t) -> p j t", j=HD)
        ym = late.take(B * D).rearrange("p (b d) -> p b d", d=D)
        yv = late.take(B * D).rearrange("p (b d) -> p b d", d=D)
        att.at = max(pre.at, post.at, late.at)
        z = att.take(P * 2 * HD).rearrange("p (t x) -> p t x", x=2 * HD)
        kb_end = att.take(P * HD).rearrange("p (t i) -> p t i", i=HD)
        q_state = att.take(P * HD).rearrange("p (t i) -> p t i", i=HD)
        kk = att.take(3 * (P + 1) + 1)
        qk = att.take(CK * P).rearrange("p (d t) -> p d t", d=CK)
        delta = att.take(P * HD).rearrange("p (t j) -> p t j", j=HD)
        rot = att.take(4 * BB * P).rearrange("p (r c n t) -> p r c n t", r=2, c=2, n=BB)
        run = att.take(SEG * 6 * BB * NG).rearrange("p (l r c n) -> p l r c n", l=SEG, r=2, c=3)
        vprod = att.take(4 * BB * P)
        vec_cut = att.take(2 * BB * P).rearrange("p (c t) -> p c t", t=P)
        vec_sq = vprod[:, 0:2 * BB * P].rearrange("p (c t) -> p c t", t=P)
        part = vprod[:, 0:2 * BB * P].rearrange("p (k n) -> p k n", k=2)
        states = sb("states", [P, NC + 1, HD * HD])
        decay = sb("decay", [P, 3, P + 1])
        decay4 = sb("decay4", [P, NC])
        beta = sb("beta", [P, P])
        norms = sb("norms", [P, 2, P])
        vec = sb("vec", [P, NG + 1, 2 * BB])
        vec_ss = sb("vec_ss", [P, B])
        rv = sb("rv", [P, B])
        epsv = sb("epsv", [P, 4])
        order = sb("order", [P, E])
        xn = sb("xn", [P, B, D])
        xnT = sb("xnT", [P, B, KT - 1 + P])
        stats = sb("stats", [P, 4, B])
        tok_w = sb("tok_w", [P, TOP_K, TILES])
        place = sb("place", [P, 3, TOP_K, TILES])
        base_tile = sb("base_tile", [P, 4, E])
        slot_of = ctx.enter_context(nc.sbuf_tensor("slot_of", [P, TOP_K, TILES], U32))
        token_of = ctx.enter_context(nc.sbuf_tensor("token_of", [P, SLOT_TILES], U32))
        ids_now = ctx.enter_context(nc.sbuf_tensor("ids_now", [P, R], U32))
        expert_f = sb("expert_f", [P, SLOT_TILES])
        expert_of = ctx.enter_context(nc.sbuf_tensor("expert_of", [P, SLOT_TILES], I32))
        sums = sb("sums", [P, 4, 2 * E])
        gate_ps = ctx.enter_context(nc.psum_tensor("gate_ps", [P, 2, I], F32))
        up_ps = ctx.enter_context(nc.psum_tensor("up_ps", [P, 2, I], F32))
        xt_ps = ctx.enter_context(nc.psum_tensor("xt_ps", [P, 4 * P], F32))
        eo_ps = ctx.enter_context(nc.psum_tensor("eo_ps", [P, 4 * P], F32))
        turn = ctx.enter_context(nc.psum_tensor("turn", [P, 2, 4 * P], F32))

        x_in, c_in, w_in, e_in, x_out = sem("x_in"), sem("c_in"), sem("w_in"), sem("e_in"), sem("x_out")
        consts_ready = sem("consts_ready")
        dve_step, pool_step = sem("dve_step"), sem("pool_step")
        centered, squared, var_ready, std_ready, xn_ready = (
            sem(n) for n in ("centered", "squared", "var_ready", "std_ready", "xn_ready"))
        turned, turn_free = sem("turned"), sem("turn_free")
        xnT_ready = sem("xnT_ready")
        logits_ready, shifted, exps_ready, colsums_ready, tokw_ready = (
            sem(n) for n in ("logits_ready", "shifted", "exps_ready", "colsums_ready", "tokw_ready"))
        sums_seen = sem("sums_seen")
        masks_ready, prefix_ready, onehot_ready, onehot_used, token_of_ready, slots_ready = (
            sem(n) for n in ("masks_ready", "prefix_ready", "onehot_ready", "onehot_used", "token_of_ready",
                             "slots_ready"))
        x_turned, xsT_ready, gate_ready, up_ready, silu_ready, h_ready, h_turned, hT_ready, down_done, eo_ready = (
            sem(n) for n in ("x_turned", "xsT_ready", "gate_ready", "up_ready", "silu_ready", "h_ready", "h_turned",
                             "hT_ready", "down_done", "eo_ready"))
        xn_stored = sem("xn_stored")
        rows_in = [sem(f"rows_in{k}") for k in range(R)]
        eo_stored = [sem(f"eo_stored{k}") for k in range(STORES)]
        rows_added, group_done = sem("rows_added"), sem("group_done")
        att_free, ctrl_ready, og_biased, gate_sig = (
            sem(n) for n in ("att_free", "ctrl_ready", "og_biased", "gate_sig"))
        ang_reduced, sincos_ready, qk_squared, qk_ssq, qk_std, pre_done = (
            sem(n) for n in ("ang_reduced", "sincos_ready", "qk_squared", "qk_ssq", "qk_std", "pre_done"))
        halo_ready, pairs_used, vec_ready, vec_squared, chain_done = (
            sem(n) for n in ("halo_ready", "pairs_used", "vec_ready", "vec_squared", "chain_done"))
        terms_ready, terms_used = sem("terms_ready"), sem("terms_used")
        lanes_in, ang_in = sem("lanes_in"), sem("ang_in")
        reads_ready, reads_squared, reads_ssq, reads_std, mem_ready = (
            sem(n) for n in ("reads_ready", "reads_squared", "reads_ssq", "reads_std", "mem_ready"))
        vstd_ready, rv_ready, y_ready = sem("vstd_ready"), sem("rv_ready"), sem("y_ready")

        block = ctx.enter_context(nc.Block())

        xn_dram = nc.dram_tensor("xn_dram", [TOK, D], F32).ap()
        eo_dram = nc.dram_tensor("eo_dram", [SLOT_TILES * P, D], F32).ap()
        x_src = hidden.rearrange("b (n t) d -> t n b d", t=P)
        res = out.rearrange("b (n t) d -> t n b d", t=P)

        @block.sync
        def _(sp):
            def load_experts():
                sp.dma_start(gate_w, gate_wt).then_inc(e_in, 16)
                sp.dma_start(up_w, up_wt).then_inc(e_in, 16)
                sp.dma_start(down_w, down_wt).then_inc(e_in, 16)

            sp.dma_start(lc[:, :], lane_consts).then_inc(c_in, 16)
            sp.dma_start(rout_w[:, :], router_wt).then_inc(c_in, 16)
            for n in range(NB):
                sp.dma_start(X[:, n * B:(n + 1) * B, :], x_src[:, n]).then_inc(x_in, 16)
            load_experts()
            sp.dma_start(first_w[:, :], w_first).then_inc(w_in, 16)
            sp.dma_start(second_w[:, :, :], taps).then_inc(w_in, 16)
            sp.dma_start(second_tmp, w_second).then_inc(w_in, 16)
            sp.dma_start(tap_rows[:, :], tap_rows_in).then_inc(w_in, 16)
            sp.dma_start(second_b[:, :], bias_second).then_inc(w_in, 16)
            sp.dma_start(mem_w[:, :, :], w_mem).then_inc(w_in, 16)
            sp.dma_start(vec_w[:, :, :], w_vec).then_inc(w_in, 16)

            def experts(phase):
                for n in range(NB):
                    sp.wait_ge(xn_ready, 2 * NB * phase + n + 1)
                    sp.dma_start(xn_dram[n * B * P:(n + 1) * B * P, :].rearrange("(b t) d -> t b d", t=P),
                                 xn[:, :, :]).then_inc(xn_stored, 16)
                with sp.Fori(0, GATHER_LOOPS) as i:
                    for k in range(R):
                        sp.wait_ge(eo_ready, phase * SLOT_TILES + i * R + k + 1 + EO_CREDIT)
                        sp.dma_start(eo_dram[ds(i * (R * P) + k * P, P), :],
                                     eo[:, k % STORES, :]).then_inc(eo_stored[k % STORES], 16)

            experts(0)
            sp.wait_ge(att_free, NB + 1)
            load_experts()
            experts(1)
            for g in range(ADD_LOOPS):
                sp.wait_ge(group_done, ADD_LOOPS + g + 1)
                n, b0 = g * ADD_TILES // B, g * ADD_TILES % B
                sp.dma_start(res[:, n, b0:b0 + ADD_TILES],
                             X[:, g * ADD_TILES:(g + 1) * ADD_TILES, :]).then_inc(x_out, 16)
            sp.wait_ge(x_out, 16 * ADD_LOOPS)

        @block.tensor
        def _(pe):
            def bank(u):
                return turn[:, u % 2, :]

            def ln_turns(u, layer):
                pe.wait_ge(xn_ready, layer + 1)
                for half in range(2):
                    pe.wait_ge(turn_free, u[0] + half + 1)
                    for b in range(4):
                        last = pe.transpose(turn[:, (u[1] + half) % 2, b * P:(b + 1) * P],
                                            xn[:, 4 * half + b, :], ident)
                    last.then_inc(turned, 1)

            def router(u0, layer0, phase):
                with pe.Fori(0, NB) as n:
                    ln_turns((u0 + 4 * n, u0), layer0 + n)
                    pe.wait_ge(xnT_ready, 2 * (layer0 + n + 1))
                    for half in range(2):
                        pe.wait_ge(turn_free, u0 + 4 * n + 2 + half + 1)
                        for b in range(4):
                            last = pe.matmul(turn[:, (u0 + half) % 2, b * E:(b + 1) * E],
                                             xnT[:, 4 * half + b, KT - 1:], rout_w[:, :], start=True, stop=True)
                        last.then_inc(turned, 1)
                u = u0 + 4 * NB
                pe.wait_ge(turn_free, u + 1)
                pe.wait_ge(masks_ready, phase + 1)
                masks = router_tmp[:, 5].rearrange("p m e -> p (m e)")
                pe.matmul(turn[:, u % 2, 0:TILES * E], lc[:, L_TRI:L_TRI + P], masks, start=True, stop=True)
                pe.matmul(turn[:, u % 2, TILES * E:2 * TILES * E], ones[:, :], masks,
                          start=True, stop=True).then_inc(turned, 1)
                u += 1
                pe.wait_ge(turn_free, u + 1)
                pe.wait_ge(colsums_ready, phase + 1)
                pe.matmul(turn[:, u % 2, 0:2 * E], ones[:, :], sums[:, 0, :],
                          start=True, stop=True).then_inc(turned, 1)
                u += 1
                pe.wait_ge(turn_free, u + 1)

                def tokens(i, start=False, stop=False):
                    for k in range(4):
                        pe.wait_ge(onehot_ready, phase * TOP_K * TILES + i * 4 + k + 1)
                        pe.matmul(turn[:, u % 2, 0:SLOT_TILES], onehot[:, k, 0:P], onehot[:, k, P:],
                                  start=start and k == 0, stop=stop and k == 3,
                                  skip_group_check=True).then_inc(onehot_used, 1)

                loops = TOP_K * TILES // 4
                tokens(0, start=True)
                with pe.Fori(1, loops - 1) as i:
                    tokens(i)
                tokens(loops - 1, stop=True)
                pe.wait_ge(onehot_used, (phase + 1) * TOP_K * TILES + 4)
                pe.sem_inc(turned, 1)

            def experts(phase):
                j0 = phase * SLOT_TILES
                pe.wait_ge(e_in, 48 * (phase + 1))
                pe.wait_ge(slots_ready, phase + 1)
                pe.wait_ge(turn_free, phase * (RING_ROUTER2 - RING_ROUTER1) + ROUTER_USES + RING_CREDIT)

                def turn_rows(i, k):
                    pe.wait_ge(rows_in[k % R], 16 * (phase * (GATHER_LOOPS + ADD_LOOPS) + i + k // R + 1))
                    pe.wait_ge(xsT_ready, j0 + i * R + k + X_CREDIT)
                    pe.transpose(xt_ps[:, 0:P], rows[:, k % R, :], ident).then_inc(x_turned, 1)

                def expert(i, k):
                    return pe.value_load(expert_of[0:1, ds(i * R + k, 1)], min_val=0, max_val=E - 1)

                def gate_up(i, k, e):
                    pe.wait_ge(xsT_ready, j0 + i * R + k + 1 + X_CREDIT)
                    pe.wait_ge(silu_ready, j0 + i * R + k + 1)
                    pe.matmul(gate_ps[:, k % 2, :], xsT[:, k % 2, :],
                              gate_w[:, ds(e, 1), :].rearrange("p a i -> p (a i)"),
                              start=True, stop=True).then_inc(gate_ready, 1)
                    pe.wait_ge(h_ready, j0 + i * R + k + 1)
                    pe.matmul(up_ps[:, k % 2, :], xsT[:, k % 2, :],
                              up_w[:, ds(e, 1), :].rearrange("p a i -> p (a i)"),
                              start=True, stop=True).then_inc(up_ready, 1)

                def turn_hidden(i, k):
                    pe.wait_ge(h_ready, j0 + i * R + k + 1 + H_CREDIT)
                    pe.wait_ge(hT_ready, j0 + i * R + k + 1)
                    for c in range(CH):
                        last = pe.transpose(turn[:, k % 2, c * P:(c + 1) * P], hid[:, k % 2, c * P:(c + 1) * P], ident)
                    last.then_inc(h_turned, 1)

                def down(i, k, e):
                    pe.wait_ge(hT_ready, j0 + i * R + k + 1 + HT_CREDIT)
                    pe.wait_ge(eo_ready, j0 + i * R + k + EO_CREDIT)
                    for c in range(CH):
                        last = pe.matmul(eo_ps[:, 0:D], hT[:, k % 2, c * P:(c + 1) * P],
                                         down_w[:, ds(e, 1), c, :].rearrange("p a d -> p (a d)"),
                                         start=(c == 0), stop=(c == CH - 1))
                    last.then_inc(down_done, 1)

                turn_rows(0, 0)
                turn_rows(0, 1)
                gate_up(0, 0, expert(0, 0))

                def body(i, last=False):
                    e_now, e_next = expert(i, 0), expert(i, 1)
                    for k in range(R):
                        if not last or k + 2 < R:
                            turn_rows(i, k + 2)
                        if not last or k + 1 < R:
                            gate_up(i, k + 1, e_next)
                        turn_hidden(i, k)
                        e_then = expert(i, k + 2) if k + 2 < R or (k + 2 == R and not last) else e_next
                        if k > 0:
                            down(i, k - 1, e_before)
                        e_before, e_now, e_next = e_now, e_next, e_then
                    down(i, R - 1, e_before)

                with pe.Fori(0, GATHER_LOOPS - 1) as i:
                    body(i)
                body(GATHER_LOOPS - 1, last=True)
                pe.wait_ge(hT_ready, j0 + SLOT_TILES + HT_CREDIT)

            def stage(n, U):
                par = (RING_ATT + STAGE_USES) % 2
                assert STAGE_USES % 2 == 0 and BLOCK_USES % 2 == 0 and RING_ATT % 2 == par
                ln_turns((U, RING_ATT), NB + n)
                pe.wait_ge(xnT_ready, 2 * (NB + n + 1))
                pe.wait_ge(halo_ready, n + 1)
                for b in range(B):
                    for half in range(2):
                        pe.wait_ge(turn_free, U + 2 + 2 * b + half + 1)
                        out_ps = turn[:, (par + half) % 2, :]
                        if half == 0:
                            pe.matmul(out_ps[:, 0:FIRST], xnT[:, b, KT - 1:], first_w[:, :],
                                      start=True, stop=True).then_inc(turned, 1)
                        else:
                            for j in range(KT):
                                pe.matmul(out_ps[:, 0:SECOND], xnT[:, b, j:j + P], second_w[:, j, :],
                                          start=(j == 0), stop=False)
                            pe.matmul(out_ps[:, 0:SECOND], tap_in[:, :], second_b[:, :],
                                      start=False, stop=True).then_inc(turned, 1)
                pe.wait_ge(ctrl_ready, 2 * B * (n + 1))
                u = 2 + 2 * B

                def lane_group(u, cols):
                    pe.wait_ge(turn_free, U + u + 1)
                    for k, col in enumerate(cols):
                        last = pe.transpose(turn[0:P, (par + u) % 2, k * P:(k + 1) * P], col, ident)
                    last.then_inc(turned, 1)

                def heads(r):
                    return head_rows[:, r].rearrange("p b h -> p (b h)")

                def pairs(r, bb):
                    return pair_rows[:, r, 2 * bb:2 * bb + 2, :].rearrange("p b m -> p (b m)")

                for r0 in range(0, 3 * HD, 4):
                    lane_group(u, [heads(r0 + r) for r in range(4)])
                    u += 1
                lane_group(u, [heads(3 * HD), heads(3 * HD + 1)])
                u += 1
                for r in (2, 0, 1, 3, 4):
                    lane_group(u, [pairs(r, bb) for bb in range(BB)])
                    u += 1
                assert u == STAGE_USES

            def project(n, U):
                par = RING_ATT % 2
                u = 0
                pe.wait_ge(vec_squared, n + 1)
                for half in range(2):
                    pe.wait_ge(turn_free, U + u + 1)
                    for k in range(2):
                        for c in range(2):
                            last = pe.matmul(turn[:, (par + u) % 2, 2 * k:2 * k + 2],
                                             vec_sq[:, c * BB + 2 * half + k, :],
                                             lc[:, L_PAIR:L_PAIR + 2], start=(c == 0), stop=(c == 1))
                    last.then_inc(turned, 1)
                    u += 1
                pe.wait_ge(mem_ready, n + 1)
                for bp in range(BB):
                    pe.wait_ge(turn_free, U + u + 1)
                    bk = (par + u) % 2
                    for j in range(HD):
                        pe.matmul(turn[:, bk, 0:2 * D], memT[32 * bp:32 * bp + 32, j, :],
                                  mem_w[32 * bp:32 * bp + 32, j, :], start=(j == 0), stop=(j == HD - 1),
                                  tile_position=(32 * bp, 0))
                    for c in range(2):
                        last = pe.matmul(turn[:, bk, 2 * D:4 * D], vec_cut[:, c * BB + bp, :],
                                         vec_w[:, c, :], start=(c == 0), stop=(c == 1))
                    last.then_inc(turned, 1)
                    u += 1
                assert u == BLOCK_USES - STAGE_USES

            def attention():
                pe.wait_ge(att_free, 1)
                stage(0, RING_ATT)
                with pe.Fori(0, NB - 1) as n:
                    stage(n + 1, RING_ATT + STAGE_USES + n * BLOCK_USES)
                    project(n, RING_ATT + 2 * STAGE_USES + n * BLOCK_USES)
                project(NB - 1, RING_ATT + STAGE_USES + (NB - 1) * BLOCK_USES)

            pe.wait_ge(c_in, 32)
            pe.wait_ge(consts_ready, 1)
            router(RING_ROUTER1, 0, 0)
            experts(0)
            attention()
            router(RING_ROUTER2, 2 * NB, 1)
            experts(1)

        @block.scalar
        def _(act):
            def ln_part(layer, n8):
                act.wait_ge(centered, layer + 1)
                act.activation(sq, xn[:, :, :], ACT.Square).then_inc(squared, 1)
                act.wait_ge(var_ready, layer + 1)
                act.activation(stats[:, 1, :], stats[:, 0, :], ACT.Sqrt, bias=eps_ln,
                               scale=1.0 / D).then_inc(std_ready, 1)

            def router(u0, layer0, phase):
                with act.Fori(0, NB) as n:
                    ln_part(layer0 + n, None)
                    for half in range(2):
                        act.wait_ge(turned, u0 + 4 * n + half + 1)
                        act.activation(xnT[:, 4 * half:4 * half + 4, KT - 1:],
                                       turn[:, (u0 + half) % 2, :].rearrange("p (b t) -> p b t", t=P),
                                       ACT.Copy).then_inc(xnT_ready, 1)
                        act.wait_ge(xnT_ready, 2 * (layer0 + n) + half + 1)
                        act.sem_inc(turn_free, 1)
                    for half in range(2):
                        act.wait_ge(turned, u0 + 4 * n + 2 + half + 1)
                        act.activation(router_tmp[:, 0, ds(n * B + half * 4, 4), :],
                                       turn[:, (u0 + half) % 2, 0:4 * E].rearrange("p (b e) -> p b e", e=E),
                                       ACT.Copy).then_inc(turn_free, 1)
                act.wait_ge(shifted, phase + 1)
                act.activation(router_tmp[:, 2], router_tmp[:, 1], ACT.Exp).then_inc(exps_ready, 1)
                u = u0 + 4 * NB
                act.wait_ge(turned, u + 1)
                act.activation(router_tmp[:, 8:10].rearrange("p k m e -> p (k m e)"), turn[:, u % 2, :],
                               ACT.Copy).then_inc(turn_free, 1)
                act.wait_ge(turned, u + 2)
                act.activation(sums[:, 1, :], turn[:, (u + 1) % 2, 0:2 * E], ACT.Copy).then_inc(turn_free, 1)
                act.wait_ge(turned, u + 3)
                act.activation(token_of[:, :], turn[:, u % 2, 0:SLOT_TILES], ACT.Copy).then_inc(token_of_ready, 1)
                act.wait_ge(token_of_ready, phase + 1)
                act.sem_inc(turn_free, 1)

            def experts(phase):
                j0 = phase * SLOT_TILES

                def gate_silu(i, k):
                    act.wait_ge(gate_ready, j0 + i * R + k + 1)
                    act.wait_ge(h_ready, j0 + i * R + k + 1)
                    act.activation(silu[:, k % 2, :], gate_ps[:, k % 2, :], ACT.Silu).then_inc(silu_ready, 1)

                def copy_hidden(i, k):
                    act.wait_ge(h_turned, j0 + i * R + k + 1 + TURN_CREDIT)
                    act.wait_ge(down_done, j0 + i * R + k + 1)
                    act.activation(hT[:, k % 2, :], turn[:, k % 2, :], ACT.Copy).then_inc(hT_ready, 1)

                def body(i, last=False):
                    for k in range(R):
                        if not last or k + 1 < R:
                            gate_silu(i, k + 1)
                        copy_hidden(i, k)

                gate_silu(0, 0)
                with act.Fori(0, GATHER_LOOPS - 1) as i:
                    body(i)
                body(GATHER_LOOPS - 1, last=True)

            def src(par, u, k0, k1):
                return turn[:, (par + u) % 2, k0 * P:k1 * P]

            def stage(n, U, first=False):
                par = RING_ATT % 2
                ln_part(NB + n, None)
                for half in range(2):
                    act.wait_ge(turned, U + half + 1)
                    if half == 0:
                        act.wait_ge(halo_ready, n + 1)
                    act.activation(xnT[:, 4 * half:4 * half + 4, KT - 1:],
                                   src(par, half, 0, 4).rearrange("p (b t) -> p b t", t=P),
                                   ACT.Copy).then_inc(xnT_ready, 1)
                    act.wait_ge(xnT_ready, 2 * (NB + n) + half + 1)
                    act.sem_inc(turn_free, 1)
                for b in range(B):
                    for half in range(2):
                        act.wait_ge(turned, U + 2 + 2 * b + half + 1)
                        ps = turn[:, (par + half) % 2, :]
                        if half == 0:
                            act.activation(pair_rows[:, :, b, :], ps[:, 0:FIRST - D].rearrange(
                                "p (r m) -> p r m", m=NPAIR), ACT.Copy)
                            last = act.activation(gate_raw[:, b, :], ps[:, FIRST - D:FIRST], ACT.Copy)
                        else:
                            last = act.activation(head_rows[:, :, b, :], ps[:, 0:SECOND].rearrange(
                                "p (r h) -> p r h", h=H), ACT.Copy)
                        last.then_inc(ctrl_ready, 1)
                        act.wait_ge(ctrl_ready, 2 * (B * n + b) + half + 1)
                        act.sem_inc(turn_free, 1)
                if not first:
                    act.wait_ge(pre_done, n)
                u = 2 + 2 * B
                for g in range(6):
                    act.wait_ge(turned, U + u + 1)
                    act.activation(qkv[:, g // 2, 4 * (g % 2):4 * (g % 2) + 4, :],
                                   src(par, u, 0, 4).rearrange("p (i t) -> p i t", t=P),
                                   ACT.Silu).then_inc(turn_free, 1)
                    u += 1
                act.wait_ge(turned, U + u + 1)
                act.activation(decay[:, 0, 1:], src(par, u, 0, 1), ACT.Sigmoid)
                act.activation(beta[:, :], src(par, u, 1, 2), ACT.Sigmoid).then_inc(lanes_in, 1)
                act.wait_ge(lanes_in, n + 1)
                act.sem_inc(turn_free, 1)
                u += 1
                if not first:
                    act.wait_ge(pairs_used, n)
                act.wait_ge(turned, U + u + 1)
                act.activation(ang, src(par, u, 0, 4), ACT.Identity,
                               bias=lc[:, L_BANG:L_BANG + 1]).then_inc(ang_in, 1)
                act.wait_ge(ang_in, n + 1)
                act.sem_inc(turn_free, 1)
                u += 1
                for c in range(2):
                    act.wait_ge(turned, U + u + 1)
                    act.activation(upd[:, c * BB * P:(c + 1) * BB * P], src(par, u, 0, 4), ACT.Sigmoid,
                                   bias=lc[:, L_BU + c:L_BU + c + 1]).then_inc(turn_free, 1)
                    u += 1
                for c in range(2):
                    act.wait_ge(turned, U + u + 1)
                    act.activation(cand[:, c * BB * P:(c + 1) * BB * P], src(par, u, 0, 4), ACT.Silu,
                                   bias=lc[:, L_BC + c:L_BC + c + 1]).then_inc(turn_free, 1)
                    u += 1

            def prepare(n):
                act.wait_ge(att_free, n + 1)
                act.activation(qk_sq, qkv[:, 0:2], ACT.Square).then_inc(qk_squared, 1)
                act.wait_ge(ang_reduced, n + 1)
                act.activation(sin_a, ang, ACT.Sin)
                act.activation(cos_a, cos_a, ACT.Sin).then_inc(sincos_ready, 1)
                act.wait_ge(og_biased, n + 1)
                act.activation(gate, gate_raw, ACT.Sigmoid).then_inc(gate_sig, 1)
                act.wait_ge(qk_ssq, n + 1)
                act.activation(norms[:, :, :], norms[:, :, :], ACT.Sqrt, bias=eps_norm).then_inc(qk_std, 1)

            def read_out(n, U):
                par = RING_ATT % 2
                u = 0
                act.wait_ge(vec_ready, n + 1)
                act.activation(vec_sq, vec_cut, ACT.Square, scale=VEC_DOWN).then_inc(vec_squared, 1)
                for half in range(2):
                    act.wait_ge(turned, U + u + 1)
                    act.activation(vec_ss[:, 4 * half:4 * half + 4], src(par, u, 0, 4)[:, 0:4], ACT.Copy)
                    act.activation(rv[:, 4 * half:4 * half + 4], src(par, u, 0, 4)[:, 0:4], ACT.Sqrt, bias=eps_vec,
                                   scale=1.0 / D).then_inc(vstd_ready, 1)
                    act.wait_ge(vstd_ready, 2 * n + half + 1)
                    act.sem_inc(turn_free, 1)
                    u += 1
                act.wait_ge(reads_ready, n + 1)
                act.activation(reads_sq, reads, ACT.Square).then_inc(reads_squared, 1)
                act.wait_ge(reads_ssq, n + 1)
                act.activation(norms[:, 0, :], norms[:, 0, :], ACT.Sqrt, bias=eps_rms,
                               scale=1.0 / HD).then_inc(reads_std, 1)
                act.wait_ge(rv_ready, n + 1)
                for bp in range(BB):
                    act.wait_ge(turned, U + u + 1)
                    act.activation(ym[:, 2 * bp:2 * bp + 2, :],
                                   src(par, u, 0, 2).rearrange("p (b d) -> p b d", d=D), ACT.Copy)
                    for b2 in range(2):
                        last = act.activation(yv[:, 2 * bp + b2, :], src(par, u, 2 + b2, 3 + b2), ACT.Copy,
                                              scale=rv[:, 2 * bp + b2:2 * bp + b2 + 1])
                    last.then_inc(y_ready, 1)
                    act.wait_ge(y_ready, BB * n + bp + 1)
                    act.sem_inc(turn_free, 1)
                    u += 1

            def attention():
                stage(0, RING_ATT, first=True)
                with act.Fori(0, NB - 1) as n:
                    prepare(n)
                    stage(n + 1, RING_ATT + STAGE_USES + n * BLOCK_USES)
                    read_out(n, RING_ATT + 2 * STAGE_USES + n * BLOCK_USES)
                prepare(NB - 1)
                read_out(NB - 1, RING_ATT + STAGE_USES + (NB - 1) * BLOCK_USES)

            eps_ln, eps_rms, eps_norm, eps_vec = (epsv[:, k:k + 1] for k in range(4))
            act.wait_ge(c_in, 32)
            act.wait_ge(consts_ready, 1)
            router(RING_ROUTER1, 0, 0)
            experts(0)
            attention()
            router(RING_ROUTER2, 2 * NB, 1)
            experts(1)

        @block.vector
        def _(dve):
            chain = Chain(dve, dve_step)
            link = chain.link

            def layernorm(layer, x_block, stored=None):
                link(dve.tensor_reduce(stats[:, 0, :], x_block, AX.X, ALU.add))
                link(dve.tensor_scalar(stats[:, 2, :], stats[:, 0, :], 1.0 / D, None, ALU.mult))
                if stored is not None:
                    dve.wait_ge(xn_stored, 16 * (stored + 1))
                dve.tensor_tensor(xn[:, :, :], x_block, over(stats[:, 2, :], 2, D), ALU.subtract).then_inc(centered, 1)
                dve.wait_ge(squared, layer + 1)
                dve.tensor_reduce(stats[:, 0, :], sq, AX.X, ALU.add).then_inc(var_ready, 1)
                dve.wait_ge(std_ready, layer + 1)
                link(dve.reciprocal(stats[:, 3, :], stats[:, 1, :]))
                dve.tensor_tensor(xn[:, :, :], xn[:, :, :], over(stats[:, 3, :], 2, D), ALU.mult).then_inc(xn_ready, 1)

            def router(u0, layer0, phase):
                chain_per = 3
                with dve.Fori(0, NB) as n:
                    chain.enter(n, chain_per)
                    layernorm(layer0 + n, X[:, ds(n * B, B), :], stored=phase * NB + n)
                    dve.wait_ge(xnT_ready, 2 * (layer0 + n + 1))
                chain.leave(NB, chain_per)
                dve.wait_ge(turn_free, u0 + 4 * NB + RING_CREDIT)
                lg, z, ex, m1, m2, both, z2, w, before, whole, pos, ping, tmp = (router_tmp[:, k] for k in range(13))
                top = sums[:, 2:4, :].rearrange("p a e -> p (a e)")

                def per_tile(a):
                    return over(a, 2, E)

                link(dve.tensor_reduce(top, lg, AX.X, ALU.max))
                link(dve.tensor_tensor(z, lg, per_tile(top), ALU.subtract))
                dve.tensor_scalar(z, z, SCORE_FLOOR, None, ALU.max).then_inc(shifted, 1)
                dve.wait_ge(shifted, phase + 1)

                def pick(m, scores):
                    link(dve.tensor_reduce(top, scores, AX.X, ALU.max))
                    link(dve.tensor_tensor(m, scores, per_tile(top), ALU.is_equal))
                    link(dve.tensor_tensor(m, m, over(order[:, :], 1, TILES), ALU.mult))
                    link(dve.tensor_reduce(top, m, AX.X, ALU.max))
                    link(dve.tensor_tensor(m, m, per_tile(top), ALU.is_equal))

                pick(m1, z)
                link(dve.scalar_tensor_tensor(z2, m1, -1e4, z, ALU.mult, ALU.add))
                pick(m2, z2)
                dve.tensor_tensor(both, m1, m2, ALU.add).then_inc(masks_ready, 1)
                dve.wait_ge(masks_ready, phase + 1)
                dve.wait_ge(exps_ready, phase + 1)
                link(dve.tensor_tensor(w, both, ex, ALU.mult))
                link(dve.tensor_reduce(top, w, AX.X, ALU.add))
                link(dve.reciprocal(top, top))
                link(dve.tensor_tensor(w, w, per_tile(top), ALU.mult))
                link(dve.tensor_reduce(sums[:, 0, 0:E], w.rearrange("p m e -> p e m"), AX.X, ALU.add))
                dve.tensor_reduce(sums[:, 0, E:2 * E], both.rearrange("p m e -> p e m"), AX.X,
                                  ALU.add).then_inc(colsums_ready, 1)
                dve.wait_ge(turn_free, u0 + 4 * NB + 1 + RING_CREDIT)
                link(dve.tensor_tensor(pos, before, whole, ALU.subtract))
                src, dst = whole, ping
                step = 1
                while step < TILES:
                    dve.tensor_copy(dst[:, 0:step, :], src[:, 0:step, :])
                    link(dve.tensor_tensor(dst[:, step:, :], src[:, step:, :], src[:, 0:TILES - step, :], ALU.add))
                    src, dst = dst, (tmp if dst is ping else ping)
                    step *= 2
                link(dve.tensor_tensor(pos, pos, src, ALU.add))
                dve.wait_ge(turn_free, u0 + 4 * NB + 2 + RING_CREDIT)
                cnt, tot = sums[:, 1, E:2 * E], sums[:, 1, 0:E]
                need, first, acc, _ = (base_tile[:, k, :] for k in range(4))
                link(dve.tensor_scalar(need, cnt, P / 2 - 0.5, 1.0 / P, ALU.add, ALU.mult))
                link(dve.tensor_scalar(need, need, ROUND, None, ALU.add))
                link(dve.tensor_scalar(need, need, ROUND, None, ALU.subtract))
                link(dve.memset(first, 0.0))
                for e in range(1, E):
                    link(dve.tensor_tensor(first[:, e:e + 1], first[:, e - 1:e], need[:, e - 1:e], ALU.add))
                link(dve.tensor_scalar(acc, first, float(P), None, ALU.mult))
                link(dve.tensor_tensor(pos, pos, over(acc, 1, TILES), ALU.add))
                link(dve.tensor_scalar(cnt, cnt, 1.0, None, ALU.max))
                link(dve.reciprocal(cnt, cnt))
                link(dve.scalar_tensor_tensor(tot, tot, 0.5, cnt, ALU.mult, ALU.mult))
                for k, m in enumerate((m1, m2)):
                    link(dve.tensor_tensor(tmp, m, pos, ALU.mult))
                    link(dve.tensor_reduce(place[:, 0, k, :], tmp, AX.X, ALU.add))
                    link(dve.tensor_tensor(tmp, m, over(tot, 1, TILES), ALU.mult))
                    link(dve.tensor_reduce(tok_w[:, k, :], tmp, AX.X, ALU.add))
                num, tile, row = (place[:, k] for k in range(3))
                link(dve.tensor_scalar(tile, num, P / 2 - 0.5, 1.0 / P, ALU.subtract, ALU.mult))
                link(dve.tensor_scalar(tile, tile, ROUND, None, ALU.add))
                link(dve.tensor_scalar(tile, tile, ROUND, None, ALU.subtract))
                link(dve.scalar_tensor_tensor(row, tile, -float(P), num, ALU.mult, ALU.add))
                dve.tensor_copy(slot_of[:, :, :], num)
                tiles = lc[:, L_IOTA:L_IOTA + SLOT_TILES]
                link(dve.tensor_scalar(expert_f[:, :], tiles, first[:, 1:2], None, ALU.is_ge))
                for e in range(2, E):
                    link(dve.scalar_tensor_tensor(expert_f[:, :], tiles, first[:, e:e + 1], expert_f[:, :],
                                                  ALU.is_ge, ALU.add))
                dve.tensor_copy(expert_of[:, :], expert_f[:, :]).then_inc(slots_ready, 1)
                with dve.Fori(0, TILES // 2) as i:
                    for k in range(4):
                        m, c = i * 2 + k // TOP_K, k % TOP_K
                        dve.wait_ge(onehot_used, phase * TOP_K * TILES + i * 4 + k + 1)
                        dve.tensor_scalar(onehot[:, k, 0:P], lc[:, L_IOTA:L_IOTA + P], row[:, c, ds(m, 1)], None,
                                          ALU.is_equal)
                        dve.tensor_scalar(onehot[:, k, P:], tiles, tile[:, c, ds(m, 1)],
                                          lc[:, ds(m + L_TOK, 1)], ALU.is_equal, ALU.mult).then_inc(onehot_ready, 1)

            def experts(phase):
                j0 = phase * SLOT_TILES

                def copy_rows(i, k):
                    dve.wait_ge(x_turned, j0 + i * R + k + 1 + ROWS_CREDIT)
                    dve.wait_ge(up_ready, j0 + i * R + k + 1)
                    dve.tensor_copy(xsT[:, k % 2, :], xt_ps[:, 0:P]).then_inc(xsT_ready, 1)

                def hidden_product(i, k):
                    dve.wait_ge(silu_ready, j0 + i * R + k + 1 + SILU_CREDIT)
                    dve.wait_ge(up_ready, j0 + i * R + k + 1 + UP_CREDIT)
                    dve.wait_ge(h_turned, j0 + i * R + k + 1)
                    dve.tensor_tensor(hid[:, k % 2, :], silu[:, k % 2, :], up_ps[:, k % 2, :],
                                      ALU.mult).then_inc(h_ready, 1)

                def copy_out(i, k):
                    dve.wait_ge(down_done, j0 + i * R + k + 1 + DOWN_CREDIT)
                    dve.wait_ge(eo_stored[k % STORES], 16 * ((j0 + i * R + k) // STORES + 1)
                                if isinstance(i, int) else i * (16 * R // STORES) + 16 * ((j0 + k) // STORES + 1))
                    dve.tensor_copy(eo[:, k % STORES, :], eo_ps[:, 0:D]).then_inc(eo_ready, 1)

                def body(i, last=False):
                    for k in range(R):
                        if not last or k + 2 < R:
                            copy_rows(i, k + 2)
                        if not last or k + 1 < R:
                            hidden_product(i, k + 1)
                        if k > 0:
                            copy_out(i, k - 1)
                    copy_out(i, R - 1)

                copy_rows(0, 0)
                copy_rows(0, 1)
                hidden_product(0, 0)
                with dve.Fori(0, GATHER_LOOPS - 1) as i:
                    body(i)
                body(GATHER_LOOPS - 1, last=True)
                per = 2
                with dve.Fori(0, ADD_LOOPS) as i:
                    chain.enter(i, per)
                    for k in range(R):
                        c, t = k // ADD_TILES, k % ADD_TILES
                        dve.wait_ge(rows_in[k], 16 * (phase * (GATHER_LOOPS + ADD_LOOPS) + GATHER_LOOPS + i + 1))
                        x = X[:, ds(i * ADD_TILES + t, 1), :].rearrange("p a d -> p (a d)")
                        last = dve.scalar_tensor_tensor(x, rows[:, k, :], tok_w[:, c, ds(i * ADD_TILES + t, 1)], x,
                                                        ALU.mult, ALU.add)
                        if t == ADD_TILES - 1:
                            link(last)
                            dve.sem_inc(rows_added, ADD_TILES)
                    dve.sem_inc(group_done, 1)
                chain.leave(ADD_LOOPS, per)

            def block_layernorm(n):
                layernorm(NB + n, X[:, ds(n * B, B), :])

            def by_step(a):
                if len(a.shape) == 2:
                    return a.rearrange("p (c r) -> p c r", r=CK)
                return a.rearrange("p (c r) x -> p c r x", r=CK)

            def before_recurrence(n):
                dve.wait_ge(lanes_in, n + 1)
                a1, a2, a3 = (decay[:, d, 1:] for d in range(3))
                link(dve.tensor_tensor(decay[:, 1, 1:], a1, decay[:, 0, 0:P], ALU.mult))
                link(dve.tensor_tensor(decay[:, 2, 2:], decay[:, 1, 2:], decay[:, 0, 0:P - 1], ALU.mult))
                link(dve.tensor_tensor(decay4[:, :], by_step(a3)[:, :, 3], by_step(a1)[:, :, 0], ALU.mult))
                dve.wait_ge(qk_squared, n + 1)
                dve.tensor_reduce(norms[:, :, :], qk_sq.rearrange("p s i t -> p s t i"), AX.X,
                                  ALU.add).then_inc(qk_ssq, 1)
                dve.wait_ge(ang_in, n + 1)
                link(dve.tensor_scalar(cos_a, ang, 1.0 / TWO_PI, ROUND, ALU.mult, ALU.add))
                link(dve.tensor_scalar(cos_a, cos_a, ROUND, None, ALU.subtract))
                link(dve.scalar_tensor_tensor(ang, cos_a, -TWO_PI_HI, ang, ALU.mult, ALU.add))
                link(dve.scalar_tensor_tensor(ang, cos_a, -TWO_PI_LO, ang, ALU.mult, ALU.add))
                link(dve.tensor_scalar(ang, ang, PI_DOWN, -PI_DOWN, ALU.min, ALU.max))
                link(dve.scalar_tensor_tensor(cos_a, ang, -1.0, ang, ALU.mult, ALU.min))
                dve.tensor_scalar(cos_a, cos_a, np.pi / 2, None, ALU.add).then_inc(ang_reduced, 1)
                dve.wait_ge(ctrl_ready, 2 * B * (n + 1))
                dve.tensor_copy(xnT[:, :, 0:KT - 1], xnT[:, :, P:])
                link(dve.memset(tap_in[:, :], 1.0))
                dve.sem_inc(halo_ready, 1)
                dve.tensor_tensor(gate_raw, gate_raw, over(lc[:, L_BOG:L_BOG + D], 1, B), ALU.add).then_inc(
                    og_biased, 1)
                dve.tensor_copy(z[:, :, HD:].rearrange("p t j -> p j t"), qkv[:, 2])
                dve.wait_ge(qk_std, n + 1)
                link(dve.reciprocal(norms[:, :, :], norms[:, :, :]))
                dve.tensor_tensor(kn.rearrange("p t i -> p i t"), qkv[:, 1], over(norms[:, 1, :], 1, HD), ALU.mult)
                link(dve.tensor_tensor(qn.rearrange("p t i -> p i t"), qkv[:, 0], over(norms[:, 0, :], 1, HD),
                                       ALU.mult))
                link(dve.tensor_tensor(kb, kn, over(beta[:, :], 2, HD), ALU.mult))
                kn_c, qn_c, kb_c, z_c, ke_c, qs_c = (by_step(a) for a in (kn, qn, kb, z, kb_end, q_state))
                now = [by_step(decay[:, d, 1:]) for d in range(3)]
                prev = [by_step(decay[:, d, 0:P]) for d in range(3)]

                def wide(a):
                    return over(a, 2, HD)

                for r in range(CK):
                    dve.tensor_tensor(qs_c[:, :, r], qn_c[:, :, r], wide(now[r][:, :, r] if r < 3 else decay4[:, :]),
                                      ALU.mult)
                    if r == CK - 1:
                        dve.tensor_copy(ke_c[:, :, r], kb_c[:, :, r])
                    else:
                        dve.tensor_tensor(ke_c[:, :, r], kb_c[:, :, r], wide(now[CK - 2 - r][:, :, CK - 1]), ALU.mult)
                    if r == 0:
                        dve.tensor_scalar(z_c[:, :, r, 0:HD], kn_c[:, :, r], -1.0, None, ALU.mult)
                    else:
                        dve.scalar_tensor_tensor(z_c[:, :, r, 0:HD], kn_c[:, :, r], -1.0,
                                                 wide(prev[r - 1][:, :, r]), ALU.mult, ALU.mult)
                kk_rows = kk[:, 0:3 * P].rearrange("p (d c r) -> p d c r", d=3, r=CK)
                qk_rows = qk.rearrange("p d (c r) -> p d c r", r=CK)

                def dots(a_c, d, out):
                    n_r = CK - d
                    buf = score[:, self_at[0]:self_at[0] + NC * n_r * HD].rearrange("p (c r i) -> p c r i", c=NC, i=HD)
                    self_at[0] += NC * n_r * HD
                    flat = "p c r i -> p c (r i)"
                    last = dve.tensor_tensor(buf.rearrange(flat), a_c[:, :, d:, :].rearrange(flat),
                                             kb_c[:, :, 0:n_r, :].rearrange(flat), ALU.mult)
                    return last, buf, out[:, :, d:]

                for a_c, rows_, d0 in ((kn_c, kk_rows, 1), (qn_c, qk_rows, 0)):
                    self_at = [0]
                    made = [dots(a_c, d, rows_[:, d - d0]) for d in range(d0, CK)]
                    link(made[-1][0])
                    for _, buf, dst in made:
                        last = dve.tensor_reduce(dst, buf, AX.X, ALU.add)
                    link(last)
                for d in range(1, CK):
                    if d > 1:
                        dve.tensor_tensor(kk_rows[:, d - 1, :, d:], kk_rows[:, d - 1, :, d:],
                                          prev[d - 2][:, :, d:], ALU.mult)
                    last = dve.tensor_tensor(qk_rows[:, d, :, d:], qk_rows[:, d, :, d:], now[d - 1][:, :, d:], ALU.mult)
                link(last)
                for s0 in range(CK - 1):
                    n_r = CK - 1 - s0
                    coef = kk[:, s0 + 1:s0 + 1 + n_r * (P + 1)].rearrange("p (r x) -> p r x", x=P + 1)
                    coef = coef[:, :, 0:P].rearrange("p r (c f) -> p r c f", f=CK)[:, :, :, 0]
                    tmp = fwd[:, 0:NC * n_r * 2 * HD].rearrange("p (c r x) -> p c r x", c=NC, x=2 * HD)
                    link(dve.tensor_tensor(tmp, over(z_c[:, :, s0, :], 2, n_r),
                                           over(coef.rearrange("p r c -> p c r"), 3, 2 * HD), ALU.mult))
                    last = dve.tensor_tensor(z_c[:, :, s0 + 1:, :], z_c[:, :, s0 + 1:, :], tmp, ALU.subtract)
                    link(last)
                dve.sem_inc(pre_done, 1)

            def recurrence(n):
                z_c, ke_c, de_c = (by_step(a) for a in (z, kb_end, delta))
                mark, reached = chain.mark, chain.reached

                def addend(c):
                    return dve.tensor_copy(pred[:, c % 2, :, :, HD], z_c[:, c, :, HD:])

                link(addend(0))
                for c in range(NC):
                    st = states[:, c, :]
                    k = mark(dve.tensor_tensor(
                        pred[:, c % 2, :, :, 0:HD], over(z_c[:, c, :, 0:HD], 2, HD),
                        over(st.rearrange("p (j i) -> p j i", i=HD), 1, CK), ALU.mult))
                    dve.tensor_scalar(outer[:, :, CK], st, decay4[:, c:c + 1], None, ALU.mult)
                    reached(k)
                    k = mark(dve.tensor_reduce(de_c[:, c], pred[:, c % 2], AX.X, ALU.add))
                    if c + 1 < NC:
                        addend(c + 1)
                    reached(k)
                    link(dve.tensor_tensor(
                        outer[:, :, 0:CK].rearrange("p (j i) s -> p s j i", i=HD),
                        over(ke_c[:, c], 2, HD), over(de_c[:, c], 3, HD), ALU.mult))
                    link(dve.tensor_reduce(states[:, c + 1, :], outer[:, :, :], AX.X, ALU.add))
                dve.sem_inc(chain_done, 1)

            def after_recurrence(n):
                re_c = by_step(reads)
                for r in range(CK):
                    dve.wait_ge(terms_ready, CK * n + r + 1)
                    dve.tensor_reduce(re_c[:, :, r, :], terms[:, r % 2, :, :, 0:HD + r + 1], AX.X,
                                      ALU.add).then_inc(terms_used, 1)
                dve.wait_ge(terms_used, CK * (n + 1) + 2)
                link(dve.tensor_copy(states[:, 0, :], states[:, NC, :]))
                dve.sem_inc(reads_ready, 1)
                dve.wait_ge(reads_squared, n + 1)
                dve.tensor_reduce(norms[:, 0, :], reads_sq, AX.X, ALU.add).then_inc(reads_ssq, 1)
                dve.wait_ge(reads_std, n + 1)
                link(dve.reciprocal(norms[:, 0, :], norms[:, 0, :]))
                dve.tensor_tensor(memT.rearrange("p j t -> p t j"), reads, over(norms[:, 0, :], 2, HD),
                                  ALU.mult).then_inc(mem_ready, 1)
                dve.wait_ge(vstd_ready, 2 * (n + 1))
                link(dve.reciprocal(rv[:, :], rv[:, :]))
                link(dve.tensor_scalar(vec_ss[:, :], vec_ss[:, :], VEC_OVER, VEC_DOWN, ALU.is_lt, ALU.mult))
                dve.tensor_tensor(rv[:, :], rv[:, :], vec_ss[:, :], ALU.mult).then_inc(rv_ready, 1)
                dve.wait_ge(y_ready, BB * (n + 1))
                link(dve.tensor_tensor(ym, ym, yv, ALU.add))
                link(dve.tensor_tensor(ym, ym, over(lc[:, L_BOUT:L_BOUT + D], 1, B), ALU.add))
                dve.wait_ge(gate_sig, n + 1)
                link(dve.tensor_tensor(ym, ym, gate, ALU.mult))
                xb = X[:, ds(n * B, B), :]
                link(dve.tensor_tensor(xb, xb, ym, ALU.add))
                dve.sem_inc(att_free, 1)

            def attention():
                block_layernorm(0)
                with dve.Fori(0, NB - 1) as n:
                    chain.restart()
                    before_recurrence(n)
                    block_layernorm(n + 1)
                    recurrence(n)
                    after_recurrence(n)
                chain.restart()
                before_recurrence(NB - 1)
                recurrence(NB - 1)
                after_recurrence(NB - 1)

            dve.memset(ones[:, :], 1.0)
            for k, v in enumerate((LN_EPS, RMS_EPS, NORM_EPS, RMS_EPS * VEC_DOWN ** 2)):
                dve.memset(epsv[:, k:k + 1], v)
            for e in range(E):
                dve.memset(order[:, e:e + 1], float(E - e))
            dve.memset(states[:, 0, :], 0.0)
            dve.memset(decay[:, :, :], 1.0)
            dve.memset(xnT[:, :, 0:KT - 1], 0.0)
            link(dve.memset(sums[:, :, :], 0.0))
            dve.sem_inc(halo_ready, 1)
            dve.sem_inc(terms_used, 2)
            dve.sem_inc(consts_ready, 1)
            dve.sem_inc(turn_free, RING_CREDIT)
            dve.sem_inc(x_turned, ROWS_CREDIT)
            dve.sem_inc(rows_added, ROWS_CREDIT)
            dve.sem_inc(xsT_ready, X_CREDIT)
            dve.sem_inc(up_ready, UP_CREDIT)
            dve.sem_inc(silu_ready, SILU_CREDIT)
            dve.sem_inc(h_ready, H_CREDIT)
            dve.sem_inc(h_turned, TURN_CREDIT)
            dve.sem_inc(hT_ready, HT_CREDIT)
            dve.sem_inc(down_done, DOWN_CREDIT)
            dve.sem_inc(eo_ready, EO_CREDIT)
            dve.sem_inc(onehot_used, 4)
            dve.sem_inc(xn_stored, 16)
            for k in range(STORES):
                dve.sem_inc(eo_stored[k], 16)

            dve.wait_ge(x_in, 16 * NB)
            router(RING_ROUTER1, 0, 0)
            dve.wait_ge(w_in, 16 * 7)
            dve.tensor_tensor(second_w[:, :, :], second_w[:, :, :], over(second_tmp, 1, KT), ALU.mult)
            dve.tensor_tensor(second_b[:, :], second_b[:, :], tap_rows[:, :], ALU.mult)
            dve.tensor_copy(tap_in[:, :], lc[0:KT, L_TAPS:L_END])
            for j in range(HD):
                dve.tensor_scalar(mem_w[:, j, :], mem_w[:, j, :], lc[:, L_RMSM + j:L_RMSM + j + 1], None, ALU.mult)
            for c in range(2):
                last = dve.tensor_scalar(vec_w[:, c, :], vec_w[:, c, :], lc[:, L_RMSV + c:L_RMSV + c + 1], None,
                                         ALU.mult)
            link(last)
            dve.sem_inc(att_free, 1)
            experts(0)
            attention()
            router(RING_ROUTER2, 2 * NB, 1)
            experts(1)

        @block.gpsimd
        def _(pool):
            chain = Chain(pool, pool_step)
            link = chain.link
            link(pool.memset(vec[:, 0, :], 0.0))

            def gathers(phase):
                loops0 = phase * (GATHER_LOOPS + ADD_LOOPS)
                pool.wait_ge(token_of_ready, phase + 1)
                pool.wait_ge(xn_stored, 16 * (NB * (phase + 1) + 1))
                if phase:
                    pool.wait_ge(rows_added, R * ADD_LOOPS * phase + ROWS_CREDIT)

                def all_rows_in(i, first):
                    for k in range(R):
                        pool.wait_ge(rows_in[k], 16 * (loops0 + first + i))
                        pool.nop(nofuse=True)

                def fetch(i, first, table, src, free, free0):
                    link(pool.tensor_copy(*table))
                    pool.nop(nofuse=True)
                    for k in range(R):
                        pool.wait_ge(free, free0 + i * R + k + 1)
                        pool.nop(nofuse=True)
                        pool.indirect_dma_start(
                            out=rows[:, k, :], out_offset=None, in_=src,
                            in_offset=bass.IndirectOffsetOnAxis(ap=ids_now[:, k:k + 1], axis=0),
                        ).then_inc(rows_in[k], 16)

                fetch(0, 0, (ids_now[:, :], token_of[:, 0:R]), xn_dram, x_turned, phase * SLOT_TILES)
                with pool.Fori(1, GATHER_LOOPS) as i:
                    chain.enter(i - 1, 1)
                    all_rows_in(i, 0)
                    fetch(i, 0, (ids_now[:, :], token_of[:, ds(i * R, R)]), xn_dram, x_turned, phase * SLOT_TILES)
                chain.leave(GATHER_LOOPS - 1, 1)
                for k in range(STORES):
                    pool.wait_ge(eo_stored[k], 16 * (SLOT_TILES // STORES * (phase + 1) + 1))
                with pool.Fori(0, ADD_LOOPS) as i:
                    chain.enter(i, 1)
                    all_rows_in(i, GATHER_LOOPS)
                    fetch(i, GATHER_LOOPS,
                          (ids_now[:, :].rearrange("p (c t) -> p c t", c=TOP_K),
                           slot_of[:, :, ds(i * ADD_TILES, ADD_TILES)]),
                          eo_dram, rows_added, phase * R * ADD_LOOPS)
                chain.leave(ADD_LOOPS, 1)

            def rotation(n):
                chain.restart()
                pool.wait_ge(sincos_ready, n + 1)
                pool.nop(nofuse=True)
                n_t = BB * P
                flat = rot.rearrange("p r c n t -> p r c (n t)")
                for c in range(2):
                    w = [lc[:, L_WB + 2 * c + k:L_WB + 2 * c + k + 1] for k in range(2)]
                    pool.tensor_scalar(part[:, 0, :], sin_a, w[1], None, ALU.mult)
                    pool.tensor_scalar(part[:, 1, :], sin_a, w[0], None, ALU.mult)
                    pool.tensor_scalar(flat[:, 0, c, :], cos_a, w[0], None, ALU.mult)
                    link(pool.tensor_scalar(flat[:, 1, c, :], cos_a, w[1], None, ALU.mult))
                    pool.tensor_tensor(flat[:, 0, c, :], flat[:, 0, c, :], part[:, 0, :], ALU.subtract)
                    link(pool.tensor_tensor(flat[:, 1, c, :], flat[:, 1, c, :], part[:, 1, :], ALU.add))
                    pool.tensor_tensor(flat[:, 0, c, :], flat[:, 0, c, :], upd[:, 0:n_t], ALU.mult)
                    pool.tensor_tensor(flat[:, 1, c, :], flat[:, 1, c, :], upd[:, n_t:], ALU.mult)
                link(pool.tensor_tensor(vprod[:, 0:2 * n_t], upd, cand, ALU.mult))
                by_time = lambda a: a.rearrange("p (c m l) -> p l c m", c=2, l=SEG)
                for c in range(2):
                    last = pool.tensor_tensor(run[:, :, c, 2, :], by_time(cand)[:, :, c],
                                              by_time(vprod[:, 0:2 * n_t])[:, :, c], ALU.subtract)
                link(last)
                pool.sem_inc(pairs_used, 1)
                A = rot.rearrange("p r c n (g l) -> p l r c (n g)", l=SEG)
                link(pool.tensor_copy(run[:, 0, :, 0:2, :], A[:, 0]))
                prod = [vprod[:, k * 6 * n_s:(k + 1) * 6 * n_s].rearrange("p (r c m) -> p r c m", r=2, c=3)
                        for k in range(2)]
                for l in range(1, SEG):
                    for k in range(2):
                        last = pool.tensor_tensor(prod[k], over(A[:, l, :, k], 2, 3),
                                                  over(run[:, l - 1, k], 1, 2), ALU.mult)
                    link(last)
                    pool.tensor_tensor(run[:, l, :, 0:2, :], prod[0][:, :, 0:2], prod[1][:, :, 0:2], ALU.add)
                    link(pool.tensor_tensor(prod[0][:, :, 2], prod[0][:, :, 2], prod[1][:, :, 2], ALU.add))
                    link(pool.tensor_tensor(run[:, l, :, 2, :], run[:, l, :, 2, :], prod[0][:, :, 2], ALU.add))
                last_map = run[:, SEG - 1].rearrange("p r c (n g) -> p r c n g", g=NG)
                for g in range(NG):
                    step = vprod[:, 0:4 * BB].rearrange("p (r c n) -> p r c n", r=2, c=2)
                    total = vprod[:, 4 * BB:6 * BB].rearrange("p (r n) -> p r n", r=2)
                    link(pool.tensor_tensor(step, last_map[:, :, 0:2, :, g],
                                            over(vec[:, g, :].rearrange("p (c n) -> p c n", c=2), 1, 2), ALU.mult))
                    link(pool.tensor_tensor(total, step[:, :, 0], step[:, :, 1], ALU.add))
                    link(pool.tensor_tensor(vec[:, g + 1, :].rearrange("p (r n) -> p r n", r=2), total,
                                            last_map[:, :, 2, :, g], ALU.add))
                halves = [vprod[:, k * 2 * n_t:(k + 1) * 2 * n_t] for k in range(2)]
                for c in range(2):
                    for k in range(2):
                        last = pool.tensor_tensor(
                            halves[c][:, k * n_t:(k + 1) * n_t].rearrange("p (l n g) -> p l n g", n=BB, g=NG),
                            run[:, :, k, c, :].rearrange("p l (n g) -> p l n g", g=NG),
                            over(vec[:, 0:NG, c * BB:(c + 1) * BB].rearrange("p g n -> p n g"), 1, SEG), ALU.mult)
                link(last)
                link(pool.tensor_tensor(halves[0], halves[0], halves[1], ALU.add))
                for k in range(2):
                    part_k = halves[0][:, k * n_t:(k + 1) * n_t].rearrange("p (l m) -> p l m", l=SEG)
                    last = pool.tensor_tensor(part_k, part_k, run[:, :, k, 2, :], ALU.add)
                link(last)
                pool.wait_ge(att_free, n + 1)
                pool.nop(nofuse=True)
                for k in range(2):
                    last = pool.tensor_scalar(
                        vec_cut[:, k * BB:(k + 1) * BB, :].rearrange("p n (g l) -> p (n g) l", l=SEG),
                        halves[0][:, k * n_t:(k + 1) * n_t].rearrange("p (l m) -> p m l", l=SEG),
                        VEC_CUT, -VEC_CUT, ALU.min, ALU.max)
                last.then_inc(vec_ready, 1)
                link(pool.tensor_copy(vec[:, 0, :], vec[:, NG, :]))

            def read_terms(n):
                pool.wait_ge(chain_done, n + 1)
                pool.nop(nofuse=True)
                before = states[:, 0:NC, :].rearrange("p c (j i) -> p c j i", i=HD)
                de_c = delta.rearrange("p (c r) j -> p c r j", r=CK)
                qk_c = qk.rearrange("p d (c r) -> p d c r", r=CK)
                qs_c = q_state.rearrange("p (c r) i -> p c r i", r=CK)
                for r in range(CK):
                    pool.wait_ge(terms_used, CK * n + r + 1)
                    pool.nop(nofuse=True)
                    last = pool.tensor_tensor(terms[:, r % 2, :, :, 0:HD], before, over(qs_c[:, :, r, :], 2, HD),
                                              ALU.mult)
                    for d in range(r + 1):
                        last = pool.tensor_tensor(terms[:, r % 2, :, :, HD + d], de_c[:, :, r - d, :],
                                                  over(qk_c[:, d, :, r], 2, HD), ALU.mult)
                    last.then_inc(terms_ready, 1)

            n_s = BB * NG
            gathers(0)
            with pool.Fori(0, NB) as n:
                rotation(n)
                read_terms(n)
            gathers(1)


def lane_constants(x):
    bc = x["L0_attn_b_ctrl"]
    lc = np.zeros((P, L_END), np.float32)
    lanes_bp = lambda a: np.tile(a, (2, 1))
    lc[:, L_BU:L_BC] = lanes_bp(bc[C_UG:C_ANG].reshape(NPAIR, 2))
    lc[:, L_BC:L_BANG] = lanes_bp(bc[C_CAND:C_Q].reshape(NPAIR, 2))
    lc[:, L_BANG:L_WB] = lanes_bp(bc[C_ANG:C_CAND].reshape(NPAIR, 1))
    lc[:, L_WB:L_RMSV] = lanes_bp(x["L0_attn_W_block"].reshape(NPAIR, 4))
    lc[:, L_RMSV:L_RMSM] = lanes_bp(x["L0_attn_rms_v_w"].reshape(NPAIR, 2))
    lc[:, L_RMSM:L_BOG] = x["L0_attn_rms_m_w"]
    lc[:, L_BOG:L_BOUT] = bc[C_OG:C_END]
    lc[:, L_BOUT:L_ID] = x["L0_attn_b_out"]
    lc[:, L_ID:L_PAIR] = np.eye(P, dtype=np.float32)
    lc[:, L_PAIR:L_IOTA] = np.repeat(np.eye(2, dtype=np.float32), NPAIR, axis=0)
    lc[:, L_IOTA:L_TOK] = np.arange(P)
    lc[:, L_TOK:L_TRI] = np.arange(TOK).reshape(TILES, P).T
    lc[:, L_TRI:L_TAPS] = np.triu(np.ones((P, P), np.float32), 1)
    lc[0:KT, L_TAPS:L_END] = np.arange(KT)[:, None] + np.arange(P)[None, :] >= KT - 1
    return lc


def control_columns():
    by_pair = lambda c0: c0 + np.arange(D).reshape(NPAIR, 2).T.ravel()
    by_head = lambda c0: c0 + np.arange(D).reshape(H, HD).T.ravel()
    return np.concatenate([by_pair(C_UG), np.arange(C_ANG, C_CAND), by_pair(C_CAND), np.arange(C_OG, C_END),
                           by_head(C_Q), by_head(C_K), by_head(C_V), np.arange(C_A, C_OG)])


def kernel(**inputs):
    import concourse.bacc as bacc
    from concourse.bass_utils import run_bass_kernel_spmd

    x = {k: np.asarray(v) for k, v in inputs.items()}
    w_out = x["L0_attn_W_out"]
    mem = w_out[:D].reshape(H, HD, D)
    w_ctrl = x["L0_attn_W_ctrl"][:, control_columns()]
    taps = np.zeros((KT, SECOND), np.float32)
    for s3, k in enumerate("qkv"):
        taps[:, s3 * D:(s3 + 1) * D] = x[f"L0_attn_{k}conv_w"].reshape(H, HD, KT).transpose(2, 1, 0).reshape(KT, D)
    taps[KT - 1, QKV:] = 1.0
    w_mem = np.zeros((B, H, HD, 2, D), np.float32)
    for b in range(B):
        w_mem[b, :, :, b % 2] = mem
    w_vec = np.zeros((2, NPAIR, 2, 2, D), np.float32)
    for b in range(2):
        w_vec[b, :, :, b] = w_out[D:].reshape(NPAIR, 2, D)
    arrays = {
        "hidden": x["L0_attn_hidden"],
        "w_first": w_ctrl[:, :FIRST],
        "w_second": w_ctrl[:, FIRST:],
        "taps": np.broadcast_to(taps, (P, KT, SECOND)),
        "tap_rows_in": taps,
        "bias_second": np.broadcast_to(x["L0_attn_b_ctrl"][control_columns()[FIRST:]], (KT, SECOND)),
        "lane_consts": lane_constants(x),
        "w_mem": w_mem.reshape(P, HD, 2 * D),
        "w_vec": w_vec.reshape(P, 2, 2 * D),
        "router_wt": x["L0_ffn_router_w"].T,
        "gate_wt": x["L0_ffn_gate_w"].transpose(2, 0, 1),
        "up_wt": x["L0_ffn_up_w"].transpose(2, 0, 1),
        "down_wt": x["L0_ffn_down_w"].reshape(E, D, CH, P).transpose(3, 0, 2, 1),
    }
    arrays = {k: np.ascontiguousarray(v) for k, v in arrays.items()}
    nc = bacc.Bacc("TRN2", target_bir_lowering=False, num_devices=1)
    args = [nc.dram_tensor(k, v.shape, F32, kind="ExternalInput").ap() for k, v in arrays.items()]
    out = nc.dram_tensor("out", (B, S, D), F32, kind="ExternalOutput").ap()
    macaron_kernel(nc, *args, out)
    r = run_bass_kernel_spmd(nc, [arrays], core_ids=[0])
    return r.results[0]["out"]
```

```python
from contextlib import ExitStack

import numpy as np
import concourse.bass as bass
from concourse import mybir

P = 128
B, S, D = 8, 512, 128
H, HD, KT = 16, 8, 4
E, I = 8, 512
CH = I // P
NB = S // P
TILES = NB * B
TOP_K = 2
TOK = TILES * P
SLOT_TILES = TOK * TOP_K // P + E
R = 8
GATHER_LOOPS = SLOT_TILES // R
OH = 8
GROUPS = TOP_K * TILES // OH
NPAIR = D // 2
BB = B // 2
C_UG, C_ANG, C_CAND, C_Q, C_K, C_V, C_A, C_BE, C_OG, C_END = np.cumsum(
    [0, D, D // 2, D, D, D, D, H, H, D]).tolist()
PAIR_ROWS = 5
HEAD_ROWS = 3 * HD + 2
FIRST = PAIR_ROWS * NPAIR + D
SECOND = HEAD_ROWS * H
QKV = 3 * D
CK = 4
NC = P // CK
PARTS = (0, 14, 26, NC)
PART = 14
READS = CK * (len(PARTS) - 1)
SEG = 8
NG = P // SEG

L_BU = 0
L_BC = L_BU + 2
L_BANG = L_BC + 2
L_WB = L_BANG + 1
L_RMSV = L_WB + 4
L_RMSM = L_RMSV + 2
L_BOG = L_RMSM + 1
L_BOUT = L_BOG + D
L_ID = L_BOUT + D
L_PAIR = L_ID + P
L_IOTA = L_PAIR + 2
L_TOK = L_IOTA + P
L_TRI = L_TOK + TOP_K * TILES
L_TAPS = L_TRI + P
L_END = L_TAPS + P

LN_EPS, RMS_EPS, NORM_EPS = 1e-5, 1e-6, 1e-12
TWO_PI = 2 * np.pi
TWO_PI_HI = 6.28125
TWO_PI_LO = TWO_PI - TWO_PI_HI
ROUND = 1.5 * 2 ** 23
PI_DOWN = 3.1415925
VEC_DOWN = 2.0 ** -20
VEC_CUT = 1e23
VEC_OVER = 2.0 ** 128 * VEC_DOWN ** 2
SCORE_FLOOR = -87.0

ALU = mybir.AluOpType
ACT = mybir.ActivationFunctionType
F32 = mybir.dt.float32
U32 = mybir.dt.uint32
I32 = mybir.dt.int32
AX = mybir.AxisListType
ds = bass.ds

RING_CREDIT = 2
ROWS_CREDIT = R
X_CREDIT, UP_CREDIT, SILU_CREDIT, H_CREDIT, DOWN_CREDIT, EO_CREDIT = 1, 2, 2, 2, 2, 1
ARENA = 37600
STORES = 4

ROUTER_ORDER = (("T", 0), ("T", 1), ("L", 0), ("T", 2), ("L", 1), ("T", 3), ("L", 2), ("L", 3))
ROUTER_TURNS = 3 * NB
ROUTER_USES = ROUTER_TURNS + 3
BLOCK_USES = 2 + 16 + 12 + 10
RING_ROUTER1 = 0
RING_ATT = ROUTER_USES
STAGE_USES = 2 + 16 + 12
RING_ROUTER2 = RING_ATT + NB * BLOCK_USES


def over(ap, axis, n):
    a = ap.unsqueeze(axis)
    shape = list(a.shape)
    shape[axis] = n
    return a.broadcast_to(shape)


class Chain:

    def __init__(self, eng, sem):
        self.eng, self.sem, self.base, self.k, self.saved = eng, sem, 0, 0, []

    def link(self, ins):
        ins.then_inc(self.sem, 1)
        self.k += 1
        self.eng.wait_ge(self.sem, self.base + self.k)

    def restart(self):
        self.eng.sem_clear(self.sem)
        self.base, self.k = 0, 0

    def mark(self, ins):
        ins.then_inc(self.sem, 1)
        self.k += 1
        return self.k

    def reached(self, k):
        self.eng.wait_ge(self.sem, k)

    def enter(self, i, per):
        self.saved.append((self.base, self.k))
        self.base, self.k = self.base + self.k + i * per, 0

    def leave(self, rounds, per):
        assert self.k == per, (self.k, per)
        self.base, k = self.saved.pop()
        self.k = k + rounds * per


def macaron_kernel(nc, hidden, w_first, w_second, taps, tap_rows_in, bias_second, lane_consts, w_mem, w_vec, router_wt, gate_wt, up_wt, down_wt, out):
    ctx = ExitStack()
    with ctx:
        def sb(name, shape):
            return ctx.enter_context(nc.sbuf_tensor(name, shape, F32))

        def sem(name):
            return ctx.enter_context(nc.semaphore(name))

        X = sb("X", [P, TILES, D])
        first_w = sb("first_w", [P, FIRST])
        second_w = sb("second_w", [P, KT, SECOND])
        second_b = sb("second_b", [KT, SECOND])
        tap_rows = sb("tap_rows", [KT, SECOND])
        tap_in = sb("tap_in", [KT, P])
        mem_w = sb("mem_w", [P, D])
        vec_w = sb("vec_w", [P, 2, 2 * D])
        rout_w = sb("rout_w", [P, E])
        lc = sb("lc", [P, L_END])
        ident = lc[:, L_ID:L_ID + P]
        ones = sb("ones", [P, P])
        arena = sb("arena", [P, ARENA])

        class Space:
            def __init__(self, at):
                self.at = at

            def take(self, size):
                self.at += size
                assert self.at <= ARENA, self.at
                return arena[:, self.at - size:self.at]

        ffn = Space(0)
        gate_w = ffn.take(E * I).rearrange("p (e i) -> p e i", e=E)
        up_w = ffn.take(E * I).rearrange("p (e i) -> p e i", e=E)
        down_w = ffn.take(E * CH * D).rearrange("p (e c d) -> p e c d", e=E, c=CH)
        xsT = ffn.take(2 * P).rearrange("p (k t) -> p k t", k=2)
        silu = ffn.take(2 * I).rearrange("p (k t) -> p k t", k=2)
        hid = ffn.take(2 * I).rearrange("p (k t) -> p k t", k=2)
        eo = ffn.take(STORES * D).rearrange("p (k t) -> p k t", k=STORES)
        onehot_space = ffn.take(2 * OH * (P + SLOT_TILES))
        onehot = onehot_space.rearrange("p (k m t) -> p k m t", k=2, m=OH)
        rsq = onehot_space[:, 0:2 * B * D].rearrange("p (k b d) -> p k b d", k=2, d=D)
        second_tmp = ffn.take(SECOND)
        router_tmp = ffn.take(13 * TILES * E).rearrange("p (k m e) -> p k m e", k=13, e=E)
        rx = ffn.take(TILES * D).rearrange("p (n b d) -> p n b d", n=NB, d=D)
        ys = rx.rearrange("p (k c) b d -> p k c (b d)", k=2)
        rxT_space = ffn.take(2 * B * P)
        rxT = rxT_space.rearrange("p (k b t) -> p k b t", k=2, t=P)
        gate_now = rxT_space[:, 0:2 * I].rearrange("p (k i) -> p k i", k=2)
        up_now = rxT_space[:, 2 * I:4 * I].rearrange("p (k i) -> p k i", k=2)
        att = Space(0)
        region = att.take(B * C_OG)
        pair_rows = region[:, 0:PAIR_ROWS * B * NPAIR].rearrange("p (r b m) -> p r b m", b=B, m=NPAIR)
        head_rows = region[:, PAIR_ROWS * B * NPAIR:].rearrange("p (r b h) -> p r b h", b=B, h=H)
        qkv = att.take(3 * HD * P).rearrange("p (s i t) -> p s i t", s=3, i=HD)
        gate_raw = att.take(B * D).rearrange("p (b d) -> p b d", d=D)
        gate = att.take(B * D).rearrange("p (b d) -> p b d", d=D)
        upd = att.take(2 * BB * P)
        cand = att.take(2 * BB * P)
        ang = att.take(BB * P)
        sin_a, cos_a = ang, att.take(BB * P)
        pre = Space(att.at)
        kn = pre.take(P * HD).rearrange("p (t i) -> p t i", i=HD)
        qn = pre.take(P * HD).rearrange("p (t i) -> p t i", i=HD)
        kb = pre.take(P * HD).rearrange("p (t i) -> p t i", i=HD)
        score = pre.take(10 * NC * HD)
        fwd = pre.take(3 * NC * 2 * HD)
        sq = score[:, 0:B * D].rearrange("p (b d) -> p b d", d=D)
        qk_sq = region[:, 0:2 * HD * P].rearrange("p (s i t) -> p s i t", s=2, i=HD)
        during = Space(att.at)
        pred = during.take(2 * CK * HD * (HD + 1)).rearrange("p (k t j i) -> p k t j i", k=2, t=CK, j=HD)
        outer = during.take(HD * HD * (CK + 1)).rearrange("p (x s) -> p x s", s=CK + 1)
        post = Space(max(att.at + B * D, during.at))
        terms = post.take(4 * PART * HD * 3 * CK).rearrange("p (k c j x) -> p k c j x", k=4, j=HD, x=3 * CK)
        reads = post.take(HD * P).rearrange("p (t j) -> p t j", j=HD)
        late = Space(att.at + 3 * HD * P)
        mem_tok = late.take(B * D)
        mem_sq = late.take(B * D)
        memT = late.take(B * P).rearrange("p (b t) -> p b t", t=P)
        ym = late.take(B * D).rearrange("p (b d) -> p b d", d=D)
        att.at = max(pre.at, post.at, late.at)
        z = att.take(P * 2 * HD).rearrange("p (t x) -> p t x", x=2 * HD)
        kb_end = att.take(P * HD).rearrange("p (t i) -> p t i", i=HD)
        q_state = att.take(P * HD).rearrange("p (t i) -> p t i", i=HD)
        kk = att.take(3 * (P + 1) + 1)
        qk = att.take(CK * P).rearrange("p (d t) -> p d t", d=CK)
        delta = att.take(P * HD).rearrange("p (t j) -> p t j", j=HD)
        rot = att.take(4 * BB * P).rearrange("p (r c n t) -> p r c n t", r=2, c=2, n=BB)
        rot_rows = rot.rearrange("p r c n t -> p r c (n t)")
        run_space = att.take(SEG * 6 * BB * NG)
        rows = run_space[:, 0:R * D].rearrange("p (r d) -> p r d", d=D)
        assert ffn.at <= att.at - SEG * 6 * BB * NG
        run = run_space.rearrange("p (l r c n) -> p l r c n", l=SEG, r=2, c=3)
        vprod = att.take(4 * BB * P)
        late_xn = arena[:, att.at:att.at + 2 * B * D].rearrange("p (k b d) -> p k b d", k=2, d=D)
        vec_cut = att.take(2 * BB * P).rearrange("p (c t) -> p c t", t=P)
        vec_sq = att.take(2 * BB * P).rearrange("p (c t) -> p c t", t=P)
        part = vprod.rearrange("p (k c n) -> p k c n", k=2, c=2)
        yv = z[:, 0:P // 2, :].rearrange("p t x -> p (t x)").rearrange("p (b d) -> p b d", d=D)
        states = sb("states", [P, NC + 1, HD * HD])
        decay = sb("decay", [P, 3, P + 1])
        decay4 = sb("decay4", [P, NC])
        beta = sb("beta", [P, P])
        norms = sb("norms", [P, 2, P])
        read_norms = sb("read_norms", [P, P])
        vec = sb("vec", [P, NG + 1, 2 * BB])
        vec_ss = sb("vec_ss", [P, B])
        rv = sb("rv", [P, B])
        epsv = sb("epsv", [P, 7])
        order = sb("order", [P, E])
        xn = sb("xn", [P, B, D])
        xnT = sb("xnT", [P, B, KT - 1 + P])
        stats = sb("stats", [P, 4, B])
        rstats = sb("rstats", [P, 4, TILES])
        tok_w = sb("tok_w", [P, TOP_K, TILES])
        place = sb("place", [P, 3, TOP_K, TILES])
        base_tile = sb("base_tile", [P, 4, E])
        dest_f = sb("dest_f", [P, 2, SLOT_TILES])
        dest_of = ctx.enter_context(nc.sbuf_tensor("dest_of", [P, SLOT_TILES], U32))
        token_of = ctx.enter_context(nc.sbuf_tensor("token_of", [P, SLOT_TILES], U32))
        ids_out = ctx.enter_context(nc.sbuf_tensor("ids_out", [P, 2, R // 2], U32))
        ids_now = ctx.enter_context(nc.sbuf_tensor("ids_now", [P, 2, R // 2], U32))
        expert_f = sb("expert_f", [P, SLOT_TILES])
        expert_of = ctx.enter_context(nc.sbuf_tensor("expert_of", [P, SLOT_TILES], I32))
        sums = sb("sums", [P, 4, 2 * E])
        gate_ps = ctx.enter_context(nc.psum_tensor("gate_ps", [P, 2, I], F32))
        up_ps = ctx.enter_context(nc.psum_tensor("up_ps", [P, 2, I], F32))
        xt_ps = ctx.enter_context(nc.psum_tensor("xt_ps", [P, 4 * P], F32))
        eo_ps = ctx.enter_context(nc.psum_tensor("eo_ps", [P, 4 * P], F32))
        turn = ctx.enter_context(nc.psum_tensor("turn", [P, 2, 4 * P], F32))

        c_in, w_in, e_in, x_out = sem("c_in"), sem("w_in"), sem("e_in"), sem("x_out")
        x_in = [sem(f"x_in{n}") for n in range(NB)]
        consts_ready = sem("consts_ready")
        dve_step, pool_step = sem("dve_step"), sem("pool_step")
        centered, squared, var_ready, std_ready, xn_ready = (
            sem(n) for n in ("centered", "squared", "var_ready", "std_ready", "xn_ready"))
        turned, turn_free = sem("turned"), sem("turn_free")
        xnT_ready = sem("xnT_ready")
        shifted, exps_ready, colsums_ready = (sem(n) for n in ("shifted", "exps_ready", "colsums_ready"))
        masks_ready, onehot_ready, onehot_used, token_of_ready, slots_ready = (
            sem(n) for n in ("masks_ready", "onehot_ready", "onehot_used", "token_of_ready",
                             "slots_ready"))
        x_turned, xsT_ready, gate_now_ready, up_now_ready, gate_ready, up_ready, silu_ready, h_ready = (
            sem(n) for n in ("x_turned", "xsT_ready", "gate_now_ready", "up_now_ready", "gate_ready", "up_ready",
                             "silu_ready", "h_ready"))
        down_done, eo_ready = sem("down_done"), sem("eo_ready")
        xn_stored = sem("xn_stored")
        r_centered, r_squared, r_var, r_std, rstd_ready, rxT_ready, rows_ready = (
            sem(n) for n in ("r_centered", "r_squared", "r_var", "r_std", "rstd_ready", "rxT_ready", "rows_ready"))
        rows_in = [sem(f"rows_in{k}") for k in range(R)]
        eo_stored = sem("eo_stored")
        block_added = sem("block_added")
        late_sums, late_std, late_ready, xn_loaded = (
            sem(n) for n in ("late_sums", "late_std", "late_ready", "xn_loaded"))
        y_in = [sem(f"y_in{k}") for k in range(2)]
        dest_ready = sem("dest_ready")
        att_free, ctrl_ready, og_biased, gate_sig = (
            sem(n) for n in ("att_free", "ctrl_ready", "og_biased", "gate_sig"))
        ang_reduced, sines_done, sincos_ready, qk_squared, qk_ssq, qk_std, pre_done = (
            sem(n) for n in ("ang_reduced", "sines_done", "sincos_ready", "qk_squared", "qk_ssq", "qk_std", "pre_done"))
        halo_ready, pairs_used, vec_ready, vec_squared, chain_done = (
            sem(n) for n in ("halo_ready", "pairs_used", "vec_ready", "vec_squared", "chain_done"))
        terms_ready, terms_used = sem("terms_ready"), sem("terms_used")
        lanes_in, ang_in, turns_in, v_placed = sem("lanes_in"), sem("ang_in"), sem("turns_in"), sem("v_placed")
        queries_ready, q_state_ready = sem("queries_ready"), sem("q_state_ready")
        reads_ready, mem_in, reads_squared, reads_ssq, reads_std, mem_ready, memT_ready = (
            sem(n) for n in ("reads_ready", "mem_in", "reads_squared", "reads_ssq", "reads_std", "mem_ready",
                             "memT_ready"))
        vstd_ready, rv_ready, yv_ready, y_taken, weights_ready = (
            sem(n) for n in ("vstd_ready", "rv_ready", "yv_ready", "y_taken", "weights_ready"))

        block = ctx.enter_context(nc.Block())

        xn_dram = nc.dram_tensor("xn_dram", [TOK, D], F32).ap()
        y_dram = nc.dram_tensor("y_dram", [1 + TOP_K * TOK, D], F32).ap()
        x_src = hidden.rearrange("b (n t) d -> t n b d", t=P)
        res = out.rearrange("b (n t) d -> t n b d", t=P)

        @block.sync
        def _(sp):
            def load_experts():
                sp.dma_start(gate_w, gate_wt).then_inc(e_in, 16)
                sp.dma_start(up_w, up_wt).then_inc(e_in, 16)
                sp.dma_start(down_w, down_wt).then_inc(e_in, 16)

            for n in range(NB):
                if n == 1:
                    sp.dma_start(lc[:, :], lane_consts).then_inc(c_in, 16)
                    sp.dma_start(rout_w[:, :], router_wt).then_inc(c_in, 16)
                sp.dma_start(X[:, n * B:(n + 1) * B, :], x_src[:, n]).then_inc(x_in[n], 16)
            load_experts()
            sp.dma_start(first_w[:, :], w_first).then_inc(w_in, 16)
            sp.dma_start(second_w[:, :, :], taps).then_inc(w_in, 16)
            sp.dma_start(second_tmp, w_second).then_inc(w_in, 16)
            sp.dma_start(tap_rows[:, :], tap_rows_in).then_inc(w_in, 16)
            sp.dma_start(second_b[:, :], bias_second).then_inc(w_in, 16)
            sp.dma_start(mem_w[:, :], w_mem).then_inc(w_in, 16)
            sp.dma_start(vec_w[:, :, :], w_vec).then_inc(w_in, 16)

            def experts(phase):
                for n in range(NB):
                    sp.wait_ge(rows_ready, NB * phase + n + 1)
                    sp.dma_start(xn_dram[n * B * P:(n + 1) * B * P, :].rearrange("(b t) d -> t b d", t=P),
                                 rx[:, n]).then_inc(xn_stored, 16)
                sp.wait_ge(eo_stored, 16 * SLOT_TILES * (phase + 1))
                for n in range(NB):
                    if n >= 2:
                        sp.wait_ge(block_added, NB * phase + n - 1)
                        if phase:
                            store_block(n - 2)
                    for c in range(TOP_K):
                        r0 = 1 + c * TOK + n * B * P
                        sp.dma_start(ys[:, n % 2, c].rearrange("p (b d) -> p b d", d=D),
                                     y_dram[r0:r0 + B * P, :].rearrange("(b t) d -> t b d", t=P)).then_inc(
                                         y_in[n % 2], 16)

            def store_block(n):
                sp.dma_start(res[:, n], X[:, n * B:(n + 1) * B, :]).then_inc(x_out, 16)

            experts(0)
            xn_rows = [xn_dram[n * B * P:(n + 1) * B * P, :].rearrange("(b t) d -> t b d", t=P) for n in range(NB)]
            sp.wait_ge(late_ready, NB - 2)
            for n in range(2, NB):
                sp.dma_start(xn_rows[n], late_xn[:, n - 2]).then_inc(xn_stored, 16)
            sp.wait_ge(xn_stored, 16 * (NB + 2))
            for n in range(2, NB):
                sp.wait_ge(xnT_ready, 2 * n)
                sp.dma_start(xn[:, :, :], xn_rows[n]).then_inc(xn_loaded, 16)
                sp.wait_ge(xn_loaded, 16 * (n - 1))
                sp.sem_inc(xn_ready, 1)
            sp.wait_ge(att_free, NB + 1)
            load_experts()
            experts(1)
            for n in range(NB - 2, NB):
                sp.wait_ge(block_added, NB + n + 1)
                store_block(n)
            sp.wait_ge(x_out, 16 * NB)

        @block.tensor
        def _(pe):
            def bank(u):
                return turn[:, u % 2, :]

            def ln_turns(u, layer):
                pe.wait_ge(xn_ready, layer + 1)
                for half in range(2):
                    pe.wait_ge(turn_free, u[0] + half + 1)
                    for b in range(4):
                        last = pe.transpose(turn[:, (u[1] + half) % 2, b * P:(b + 1) * P],
                                            xn[:, 4 * half + b, :], ident)
                    last.then_inc(turned, 1)

            def router(u0, phase):
                u = u0
                for kind, n in ROUTER_ORDER:
                    if kind == "T":
                        pe.wait_ge(r_centered, NB * phase + n + 1)
                        for half in range(2):
                            pe.wait_ge(turn_free, u + 1)
                            for b in range(4):
                                last = pe.transpose(turn[:, u % 2, b * P:(b + 1) * P], rx[:, n, 4 * half + b, :],
                                                    ident)
                            last.then_inc(turned, 1)
                            u += 1
                    else:
                        pe.wait_ge(rxT_ready, 2 * (NB * phase + n + 1))
                        pe.wait_ge(turn_free, u + 1)
                        for b in range(B):
                            last = pe.matmul(turn[:, u % 2, b * E:(b + 1) * E], rxT[:, n % 2, b, :], rout_w[:, :],
                                             start=True, stop=True)
                        last.then_inc(turned, 1)
                        u += 1
                pe.wait_ge(turn_free, u + 1)
                pe.wait_ge(masks_ready, phase + 1)
                masks = router_tmp[:, 5].rearrange("p m e -> p (m e)")
                pe.matmul(turn[:, u % 2, 0:TILES * E], lc[:, L_TRI:L_TRI + P], masks, start=True, stop=True)
                pe.matmul(turn[:, u % 2, TILES * E:2 * TILES * E], ones[:, :], masks,
                          start=True, stop=True).then_inc(turned, 1)
                u += 1
                pe.wait_ge(turn_free, u + 1)

                for i in range(GROUPS):
                    pe.wait_ge(onehot_ready, phase * GROUPS + i + 1)
                    for k in range(OH):
                        last = pe.matmul(turn[:, u % 2, 0:SLOT_TILES], onehot[:, i % 2, k, 0:P],
                                         onehot[:, i % 2, k, P:], start=i + k == 0,
                                         stop=i == GROUPS - 1 and k == OH - 1)
                    last.then_inc(onehot_used, 1)
                pe.wait_ge(onehot_used, (phase + 1) * GROUPS + 2)
                pe.sem_inc(turned, 1)
                u += 1
                pe.wait_ge(turn_free, u + 1)
                pe.wait_ge(colsums_ready, phase + 1)
                pe.matmul(turn[:, u % 2, 0:E], ones[:, :], sums[:, 0, 0:E],
                          start=True, stop=True).then_inc(turned, 1)

            def experts(phase):
                j0 = phase * SLOT_TILES
                pe.wait_ge(e_in, 48 * (phase + 1))
                pe.wait_ge(slots_ready, phase + 1)

                def turn_rows(i, k):
                    pe.wait_ge(rows_in[k % R], 16 * (phase * GATHER_LOOPS + i + k // R + 1))
                    pe.wait_ge(xsT_ready, j0 + i * R + k + X_CREDIT)
                    pe.transpose(xt_ps[:, 0:P], rows[:, k % R, :], ident).then_inc(x_turned, 1)

                def gate_up(i, k):
                    j = j0 + i * R + k
                    pe.wait_ge(xsT_ready, j + 1 + X_CREDIT)
                    for weights, weights_ready_, ps, read, done in (
                            (gate_now, gate_now_ready, gate_ps, silu_ready, gate_ready),
                            (up_now, up_now_ready, up_ps, h_ready, up_ready)):
                        pe.wait_ge(weights_ready_, j + 1)
                        pe.wait_ge(read, j + 1)
                        for c in range(CH):
                            last = pe.matmul(ps[:, k % 2, c * P:(c + 1) * P], weights[:, k % 2, c * P:(c + 1) * P],
                                             xsT[:, k % 2, :], start=True, stop=True)
                        last.then_inc(done, 1)

                def down(i, k):
                    e = pe.value_load(expert_of[0:1, ds(i * R + k, 1)], min_val=0, max_val=E - 1)
                    pe.wait_ge(h_ready, j0 + i * R + k + 1 + H_CREDIT)
                    pe.wait_ge(eo_ready, j0 + i * R + k + EO_CREDIT)
                    for c in range(CH):
                        last = pe.matmul(eo_ps[:, 0:D], hid[:, k % 2, c * P:(c + 1) * P],
                                         down_w[:, ds(e, 1), c, :].rearrange("p a d -> p (a d)"),
                                         start=(c == 0), stop=(c == CH - 1))
                    last.then_inc(down_done, 1)

                def body(i, last=False):
                    for k in range(R):
                        if not last or k + 2 < R:
                            turn_rows(i, k + 2)
                        if not last or k + 1 < R:
                            gate_up(i, k + 1)
                        down(i, k)

                turn_rows(0, 0)
                turn_rows(0, 1)
                gate_up(0, 0)
                with pe.Fori(0, GATHER_LOOPS - 1) as i:
                    body(i)
                body(GATHER_LOOPS - 1, last=True)

            def stage(n, U):
                par = (RING_ATT + STAGE_USES) % 2
                assert STAGE_USES % 2 == 0 and BLOCK_USES % 2 == 0 and RING_ATT % 2 == par
                ln_turns((U, RING_ATT), n)
                pe.wait_ge(xnT_ready, 2 * (n + 1))
                pe.wait_ge(halo_ready, n + 1)
                for b in range(B):
                    for half in range(2):
                        pe.wait_ge(turn_free, U + 2 + 2 * b + half + 1)
                        out_ps = turn[:, (par + half) % 2, :]
                        if half == 0:
                            pe.matmul(out_ps[:, 0:FIRST], xnT[:, b, KT - 1:], first_w[:, :],
                                      start=True, stop=True).then_inc(turned, 1)
                        else:
                            for j in reversed(range(KT)):
                                cols = SECOND if j == KT - 1 else QKV
                                pe.matmul(out_ps[:, 0:cols], xnT[:, b, j:j + P], second_w[:, j, 0:cols],
                                          start=(j == KT - 1), stop=False)
                            pe.matmul(out_ps[:, 0:SECOND], tap_in[:, :], second_b[:, :],
                                      start=False, stop=True).then_inc(turned, 1)
                pe.wait_ge(ctrl_ready, 2 * B * (n + 1))
                u = 2 + 2 * B

                def lane_group(u, cols):
                    pe.wait_ge(turn_free, U + u + 1)
                    for k, col in enumerate(cols):
                        last = pe.transpose(turn[0:P, (par + u) % 2, k * P:(k + 1) * P], col, ident)
                    last.then_inc(turned, 1)

                def heads(r):
                    return head_rows[:, r].rearrange("p b h -> p (b h)")

                def pairs(r, bb):
                    return pair_rows[:, r, 2 * bb:2 * bb + 2, :].rearrange("p b m -> p (b m)")

                lane_group(u, [pairs(2, bb) for bb in range(BB)])
                u += 1
                for r0 in range(0, 3 * HD, 4):
                    lane_group(u, [heads(r0 + r) for r in range(4)])
                    u += 1
                lane_group(u, [heads(3 * HD), heads(3 * HD + 1)])
                u += 1
                for r in (0, 1, 3, 4):
                    lane_group(u, [pairs(r, bb) for bb in range(BB)])
                    u += 1
                assert u == STAGE_USES

            def project(n, U):
                par = RING_ATT % 2
                u = 0
                pe.wait_ge(vec_squared, n + 1)
                for half in range(2):
                    pe.wait_ge(turn_free, U + u + 1)
                    for k in range(2):
                        for c in range(2):
                            last = pe.matmul(turn[:, (par + u) % 2, 2 * k:2 * k + 2],
                                             vec_sq[:, c * BB + 2 * half + k, :],
                                             lc[:, L_PAIR:L_PAIR + 2], start=(c == 0), stop=(c == 1))
                    last.then_inc(turned, 1)
                    u += 1
                for half in range(2):
                    pe.wait_ge(turn_free, U + u + 1)
                    for k in range(2):
                        for c in range(2):
                            last = pe.matmul(turn[:, (par + u) % 2, 2 * k * D:2 * (k + 1) * D],
                                             vec_cut[:, c * BB + 2 * half + k, :],
                                             vec_w[:, c, :], start=(c == 0), stop=(c == 1))
                    last.then_inc(turned, 1)
                    u += 1
                pe.wait_ge(reads_ready, n + 1)
                for half in range(2):
                    pe.wait_ge(turn_free, U + u + 1)
                    for k in range(4):
                        last = pe.transpose(turn[:, (par + u) % 2, k * P:(k + 1) * P],
                                            reads[:, :, 4 * half + k], ident)
                    last.then_inc(turned, 1)
                    u += 1
                pe.wait_ge(mem_ready, n + 1)
                for half in range(2):
                    pe.wait_ge(turn_free, U + u + 1)
                    for k in range(4):
                        b = 4 * half + k
                        last = pe.transpose(turn[:, (par + u) % 2, k * P:(k + 1) * P],
                                            mem_tok[:, b * D:(b + 1) * D], ident)
                    last.then_inc(turned, 1)
                    u += 1
                for half in range(2):
                    pe.wait_ge(memT_ready, 2 * n + half + 1)
                    pe.wait_ge(turn_free, U + u + 1)
                    for k in range(4):
                        last = pe.matmul(turn[:, (par + u) % 2, k * D:(k + 1) * D], memT[:, 4 * half + k, :],
                                         mem_w[:, :], start=True, stop=True)
                    last.then_inc(turned, 1)
                    u += 1
                assert u == BLOCK_USES - STAGE_USES

            def attention():
                pe.wait_ge(weights_ready, 1)
                stage(0, RING_ATT)
                with pe.Fori(0, NB - 1) as n:
                    stage(n + 1, RING_ATT + STAGE_USES + n * BLOCK_USES)
                    project(n, RING_ATT + 2 * STAGE_USES + n * BLOCK_USES)
                project(NB - 1, RING_ATT + STAGE_USES + (NB - 1) * BLOCK_USES)

            pe.wait_ge(c_in, 32)
            pe.wait_ge(consts_ready, 1)
            router(RING_ROUTER1, 0)
            experts(0)
            attention()
            router(RING_ROUTER2, 1)
            experts(1)

        @block.scalar
        def _(act):
            def ln_part(layer):
                act.wait_ge(centered, layer + 1)
                act.activation(sq, xn[:, :, :], ACT.Square).then_inc(squared, 1)
                act.wait_ge(var_ready, layer + 1)
                act.activation(stats[:, 1, :], stats[:, 0, :], ACT.Sqrt, bias=eps_ln,
                               scale=1.0 / D).then_inc(std_ready, 1)

            def router(u0, phase):
                u = u0
                for kind, n in ROUTER_ORDER:
                    if kind == "T":
                        act.wait_ge(r_centered, NB * phase + n + 1)
                        if n >= 2:
                            act.wait_ge(r_var, NB * phase + n - 1)
                        act.activation(rsq[:, n % 2], rx[:, n], ACT.Square).then_inc(r_squared, 1)
                        for half in range(2):
                            act.wait_ge(turned, u + 1)
                            act.activation(rxT[:, n % 2, 4 * half:4 * half + 4, :],
                                           turn[:, u % 2, :].rearrange("p (b t) -> p b t", t=P),
                                           ACT.Copy).then_inc(rxT_ready, 1)
                            act.wait_ge(rxT_ready, 2 * (NB * phase + n) + half + 1)
                            act.sem_inc(turn_free, 1)
                            u += 1
                    else:
                        act.wait_ge(turned, u + 1)
                        act.activation(router_tmp[:, 0, n * B:(n + 1) * B, :],
                                       turn[:, u % 2, 0:B * E].rearrange("p (b e) -> p b e", e=E),
                                       ACT.Copy).then_inc(turn_free, 1)
                        u += 1
                act.wait_ge(r_var, NB * (phase + 1))
                act.activation(rstats[:, 3, :], rstats[:, 2, :], ACT.Sqrt, bias=eps_ln,
                               scale=1.0 / D).then_inc(r_std, 1)
                act.wait_ge(shifted, phase + 1)
                act.activation(router_tmp[:, 2], router_tmp[:, 1], ACT.Exp).then_inc(exps_ready, 1)
                act.wait_ge(turned, u + 1)
                act.activation(router_tmp[:, 8:10].rearrange("p k m e -> p (k m e)"), turn[:, u % 2, :],
                               ACT.Copy).then_inc(turn_free, 1)
                act.wait_ge(turned, u + 2)
                act.activation(dest_f[:, 0, :], turn[:, (u + 1) % 2, 0:SLOT_TILES], ACT.Copy).then_inc(dest_ready, 1)
                act.wait_ge(dest_ready, phase + 1)
                act.sem_inc(turn_free, 1)
                act.wait_ge(turned, u + 3)
                act.activation(sums[:, 1, 0:E], turn[:, u % 2, 0:E], ACT.Copy).then_inc(turn_free, 1)

            def experts(phase):
                j0 = phase * SLOT_TILES

                def gate_silu(i, k):
                    act.wait_ge(gate_ready, j0 + i * R + k + 1)
                    act.wait_ge(h_ready, j0 + i * R + k + 1)
                    act.activation(silu[:, k % 2, :], gate_ps[:, k % 2, :], ACT.Silu).then_inc(silu_ready, 1)

                def place_gate(i, k):
                    e = act.value_load(expert_of[0:1, ds(i * R + k, 1)], min_val=0, max_val=E - 1)
                    act.wait_ge(up_ready, j0 + i * R + k + 1)
                    act.activation(gate_now[:, k % 2, :], gate_w[:, ds(e, 1), :].rearrange("p a i -> p (a i)"),
                                   ACT.Copy).then_inc(gate_now_ready, 1)

                def body(i, last=False):
                    for k in range(R):
                        if not last or k + 2 < R:
                            place_gate(i, k + 2)
                        if not last or k + 1 < R:
                            gate_silu(i, k + 1)

                act.wait_ge(e_in, 48 * (phase + 1))
                act.wait_ge(slots_ready, phase + 1)
                place_gate(0, 0)
                place_gate(0, 1)
                gate_silu(0, 0)
                with act.Fori(0, GATHER_LOOPS - 1) as i:
                    body(i)
                body(GATHER_LOOPS - 1, last=True)

            def src(par, u, k0, k1):
                return turn[:, (par + u) % 2, k0 * P:k1 * P]

            def stage(n, U, first=False):
                par = RING_ATT % 2
                if first:
                    ln_part(0)
                for half in range(2):
                    act.wait_ge(turned, U + half + 1)
                    if half == 0:
                        act.wait_ge(halo_ready, n + 1)
                    act.activation(xnT[:, 4 * half:4 * half + 4, KT - 1:],
                                   src(par, half, 0, 4).rearrange("p (b t) -> p b t", t=P),
                                   ACT.Copy).then_inc(xnT_ready, 1)
                    act.wait_ge(xnT_ready, 2 * n + half + 1)
                    act.sem_inc(turn_free, 1)
                for b in range(B):
                    for half in range(2):
                        act.wait_ge(turned, U + 2 + 2 * b + half + 1)
                        ps = turn[:, (par + half) % 2, :]
                        if half == 0:
                            act.activation(pair_rows[:, :, b, :], ps[:, 0:FIRST - D].rearrange(
                                "p (r m) -> p r m", m=NPAIR), ACT.Copy)
                            last = act.activation(gate_raw[:, b, :], ps[:, FIRST - D:FIRST], ACT.Copy)
                        else:
                            last = act.activation(head_rows[:, :, b, :], ps[:, 0:SECOND].rearrange(
                                "p (r h) -> p r h", h=H), ACT.Copy)
                        last.then_inc(ctrl_ready, 1)
                        act.wait_ge(ctrl_ready, 2 * (B * n + b) + half + 1)
                        act.sem_inc(turn_free, 1)
                if first:
                    act.wait_ge(late_sums, 1)
                    act.activation(rstats[:, 3, B:], rstats[:, 2, B:], ACT.Sqrt, bias=eps_ln,
                                   scale=1.0 / D).then_inc(late_std, 1)
                else:
                    act.wait_ge(pre_done, n)
                u = 2 + 2 * B
                if not first:
                    act.wait_ge(pairs_used, n)
                act.wait_ge(turned, U + u + 1)
                act.activation(ang, src(par, u, 0, 4), ACT.Identity,
                               bias=lc[:, L_BANG:L_BANG + 1]).then_inc(ang_in, 1)
                act.wait_ge(ang_in, n + 1)
                act.sem_inc(turn_free, 1)
                act.activation(cos_a, ang, ACT.Identity, bias=round_up, scale=1.0 / TWO_PI).then_inc(turns_in, 1)
                act.wait_ge(turns_in, 2 * n + 1)
                act.activation(cos_a, cos_a, ACT.Identity, bias=round_down).then_inc(turns_in, 1)
                u += 1
                for g in range(6):
                    act.wait_ge(turned, U + u + 1)
                    act.activation(qkv[:, g // 2, 4 * (g % 2):4 * (g % 2) + 4, :],
                                   src(par, u, 0, 4).rearrange("p (i t) -> p i t", t=P),
                                   ACT.Silu).then_inc(turn_free, 1)
                    u += 1
                if not first:
                    act.wait_ge(q_state_ready, n)
                act.wait_ge(turned, U + u + 1)
                act.activation(decay[:, 0, 1:], src(par, u, 0, 1), ACT.Sigmoid)
                act.activation(beta[:, :], src(par, u, 1, 2), ACT.Sigmoid).then_inc(lanes_in, 1)
                act.wait_ge(lanes_in, n + 1)
                act.sem_inc(turn_free, 1)
                u += 1
                for c in range(2):
                    act.wait_ge(turned, U + u + 1)
                    act.activation(upd[:, c * BB * P:(c + 1) * BB * P], src(par, u, 0, 4), ACT.Sigmoid,
                                   bias=lc[:, L_BU + c:L_BU + c + 1]).then_inc(turn_free, 1)
                    u += 1
                for c in range(2):
                    act.wait_ge(turned, U + u + 1)
                    act.activation(cand[:, c * BB * P:(c + 1) * BB * P], src(par, u, 0, 4), ACT.Silu,
                                   bias=lc[:, L_BC + c:L_BC + c + 1]).then_inc(turn_free, 1)
                    u += 1

            def sines(n, first=False):
                act.wait_ge(ang_reduced, n + 1)
                act.activation(sin_a, ang, ACT.Sin)
                act.activation(cos_a, cos_a, ACT.Sin, bias=quarter).then_inc(sines_done, 1)
                act.wait_ge(sines_done, n + 1)
                if not first:
                    act.wait_ge(vec_ready, n)
                for c in range(2):
                    for r in range(2):
                        w_r, w_other = (lc[:, L_WB + 2 * c + k:L_WB + 2 * c + k + 1] for k in (r, 1 - r))
                        act.activation(rot_rows[:, r, c, :], cos_a, ACT.Copy, scale=w_r)
                        last = act.activation(part[:, r, c, :], sin_a, ACT.Copy, scale=w_other)
                last.then_inc(sincos_ready, 1)

            def lane_squares(n):
                act.activation(qk_sq, qkv[:, 0:2], ACT.Square).then_inc(qk_squared, 1)

            def lane_roots(n):
                act.wait_ge(qk_ssq, n + 1)
                act.activation(norms[:, :, :], norms[:, :, :], ACT.Sqrt, bias=eps_norm).then_inc(qk_std, 1)

            def gates(n):
                act.wait_ge(att_free, n + 1)
                act.activation(z[:, :, HD:].rearrange("p t j -> p j t"), qkv[:, 2], ACT.Copy).then_inc(v_placed, 1)
                act.wait_ge(og_biased, n + 1)
                act.activation(gate, gate_raw, ACT.Sigmoid).then_inc(gate_sig, 1)

            def rotation_out(n, U):
                par = RING_ATT % 2
                u = 0
                act.wait_ge(vec_ready, n + 1)
                act.activation(vec_sq, vec_cut, ACT.Square, scale=VEC_DOWN).then_inc(vec_squared, 1)
                for half in range(2):
                    act.wait_ge(turned, U + u + 1)
                    act.activation(vec_ss[:, 4 * half:4 * half + 4], src(par, u, 0, 4)[:, 0:4], ACT.Copy)
                    act.activation(rv[:, 4 * half:4 * half + 4], src(par, u, 0, 4)[:, 0:4], ACT.Sqrt, bias=eps_vec,
                                   scale=1.0 / D).then_inc(vstd_ready, 1)
                    act.wait_ge(vstd_ready, 2 * n + half + 1)
                    act.sem_inc(turn_free, 1)
                    u += 1
                act.wait_ge(rv_ready, n + 1)
                for half in range(2):
                    act.wait_ge(turned, U + u + 1)
                    for k in range(4):
                        b = 4 * half + k
                        last = act.activation(yv[:, b, :], src(par, u, k, k + 1), ACT.Copy, scale=rv[:, b:b + 1])
                    last.then_inc(yv_ready, 1)
                    act.wait_ge(yv_ready, 2 * n + half + 1)
                    act.sem_inc(turn_free, 1)
                    u += 1

            def memory_out(n, U):
                par = RING_ATT % 2
                u = 4
                by_j = lambda a: a.rearrange("p (m j) -> p j m", j=HD)
                for half in range(2):
                    act.wait_ge(turned, U + u + 1)
                    ps = src(par, u, 0, 4).rearrange("p (j m) -> p j m", j=4)
                    act.activation(by_j(mem_sq)[:, 4 * half:4 * half + 4, :], ps, ACT.Square).then_inc(
                        reads_squared, 1)
                    act.activation(by_j(mem_tok)[:, 4 * half:4 * half + 4, :], ps, ACT.Copy).then_inc(mem_in, 1)
                    act.wait_ge(mem_in, 2 * n + half + 1)
                    act.sem_inc(turn_free, 1)
                    u += 1
                act.wait_ge(reads_ssq, n + 1)
                act.activation(read_norms[:, :], read_norms[:, :], ACT.Sqrt, bias=eps_rms,
                               scale=1.0 / HD).then_inc(reads_std, 1)
                for half in range(2):
                    act.wait_ge(turned, U + u + 1)
                    act.activation(memT[:, 4 * half:4 * half + 4, :],
                                   src(par, u, 0, 4).rearrange("p (b t) -> p b t", t=P),
                                   ACT.Copy).then_inc(memT_ready, 1)
                    act.wait_ge(memT_ready, 2 * n + half + 1)
                    act.sem_inc(turn_free, 1)
                    u += 1
                for half in range(2):
                    act.wait_ge(y_taken, 2 * n + half + 1)
                    act.sem_inc(turn_free, 1)
                    u += 1

            def attention():
                stage(0, RING_ATT, first=True)
                sines(0, first=True)
                lane_squares(0)
                lane_roots(0)
                gates(0)
                with act.Fori(0, NB - 1) as n:
                    stage(n + 1, RING_ATT + STAGE_USES + n * BLOCK_USES)
                    lane_squares(n + 1)
                    rotation_out(n, RING_ATT + 2 * STAGE_USES + n * BLOCK_USES)
                    sines(n + 1)
                    lane_roots(n + 1)
                    memory_out(n, RING_ATT + 2 * STAGE_USES + n * BLOCK_USES)
                    gates(n + 1)
                rotation_out(NB - 1, RING_ATT + STAGE_USES + (NB - 1) * BLOCK_USES)
                memory_out(NB - 1, RING_ATT + STAGE_USES + (NB - 1) * BLOCK_USES)

            eps_ln, eps_rms, eps_norm, eps_vec, round_up, round_down, quarter = (epsv[:, k:k + 1] for k in range(7))
            act.wait_ge(c_in, 32)
            act.wait_ge(consts_ready, 1)
            router(RING_ROUTER1, 0)
            experts(0)
            attention()
            router(RING_ROUTER2, 1)
            experts(1)

        @block.vector
        def _(dve):
            chain = Chain(dve, dve_step)
            link = chain.link

            def layernorm(layer, x_block):
                link(dve.tensor_reduce(stats[:, 0, :], x_block, AX.X, ALU.add))
                link(dve.tensor_scalar(stats[:, 2, :], stats[:, 0, :], 1.0 / D, None, ALU.mult))
                dve.tensor_tensor(xn[:, :, :], x_block, over(stats[:, 2, :], 2, D), ALU.subtract).then_inc(centered, 1)
                dve.wait_ge(squared, layer + 1)
                dve.tensor_reduce(stats[:, 0, :], sq, AX.X, ALU.add).then_inc(var_ready, 1)
                dve.wait_ge(std_ready, layer + 1)
                link(dve.reciprocal(stats[:, 3, :], stats[:, 1, :]))
                dve.tensor_tensor(xn[:, :, :], xn[:, :, :], over(stats[:, 3, :], 2, D), ALU.mult).then_inc(xn_ready, 1)

            def router(u0, phase):
                rsum, rmean, rssq, rstd = (rstats[:, k, :] for k in range(4))

                def squares(n):
                    dve.wait_ge(r_squared, NB * phase + n + 1)
                    dve.tensor_reduce(rssq[:, n * B:(n + 1) * B], rsq[:, n % 2], AX.X, ALU.add).then_inc(r_var, 1)

                for n in range(NB):
                    x_block, ts = X[:, n * B:(n + 1) * B, :], slice(n * B, (n + 1) * B)
                    if phase == 0:
                        dve.wait_ge(x_in[n], 16)
                    link(dve.tensor_reduce(rsum[:, ts], x_block, AX.X, ALU.add))
                    link(dve.tensor_scalar(rmean[:, ts], rsum[:, ts], 1.0 / D, None, ALU.mult))
                    dve.tensor_tensor(rx[:, n], x_block, over(rmean[:, ts], 2, D), ALU.subtract).then_inc(r_centered, 1)
                    if n > 0:
                        squares(n - 1)
                squares(NB - 1)
                dve.wait_ge(r_std, phase + 1)
                link(dve.reciprocal(rstd, rstd))
                dve.sem_inc(rstd_ready, 1)
                dve.wait_ge(turn_free, u0 + ROUTER_TURNS + RING_CREDIT)
                lg, z, ex, m1, m2, both, z2, w, before, whole, pos, ping, tmp = (router_tmp[:, k] for k in range(13))
                top = sums[:, 2:4, :].rearrange("p a e -> p (a e)")

                def per_tile(a):
                    return over(a, 2, E)

                link(dve.tensor_tensor(lg, lg, per_tile(rstd), ALU.mult))
                link(dve.tensor_reduce(top, lg, AX.X, ALU.max))
                link(dve.tensor_tensor(z, lg, per_tile(top), ALU.subtract))
                dve.tensor_scalar(z, z, SCORE_FLOOR, None, ALU.max).then_inc(shifted, 1)
                dve.wait_ge(shifted, phase + 1)

                def pick(m, scores):
                    link(dve.tensor_reduce(top, scores, AX.X, ALU.max))
                    link(dve.tensor_tensor(m, scores, per_tile(top), ALU.is_equal))
                    link(dve.tensor_tensor(m, m, over(order[:, :], 1, TILES), ALU.mult))
                    link(dve.tensor_reduce(top, m, AX.X, ALU.max))
                    link(dve.tensor_tensor(m, m, per_tile(top), ALU.is_equal))

                pick(m1, z)
                link(dve.scalar_tensor_tensor(z2, m1, -1e4, z, ALU.mult, ALU.add))
                pick(m2, z2)
                dve.tensor_tensor(both, m1, m2, ALU.add).then_inc(masks_ready, 1)
                dve.wait_ge(masks_ready, phase + 1)
                dve.wait_ge(exps_ready, phase + 1)
                link(dve.tensor_tensor(w, both, ex, ALU.mult))
                link(dve.tensor_reduce(top, w, AX.X, ALU.add))
                link(dve.reciprocal(top, top))
                dve.wait_ge(turn_free, u0 + ROUTER_TURNS + 1 + RING_CREDIT)
                link(dve.tensor_tensor(pos, before, whole, ALU.subtract))
                src, dst = whole, ping
                step = 1
                while step < TILES:
                    dve.tensor_copy(dst[:, 0:step, :], src[:, 0:step, :])
                    link(dve.tensor_tensor(dst[:, step:, :], src[:, step:, :], src[:, 0:TILES - step, :], ALU.add))
                    src, dst = dst, (tmp if dst is ping else ping)
                    step *= 2
                link(dve.tensor_tensor(pos, pos, src, ALU.add))
                need, first, acc, count = (base_tile[:, k, :] for k in range(4))
                dve.tensor_scalar(count, src[:, TILES - 1, :], 1.0, None, ALU.max)
                link(dve.tensor_scalar(need, src[:, TILES - 1, :], P / 2 - 0.5, 1.0 / P, ALU.add, ALU.mult))
                link(dve.tensor_scalar(need, need, ROUND, None, ALU.add))
                link(dve.tensor_scalar(need, need, ROUND, None, ALU.subtract))
                link(dve.memset(first, 0.0))
                for e in range(1, E):
                    link(dve.tensor_tensor(first[:, e:e + 1], first[:, e - 1:e], need[:, e - 1:e], ALU.add))
                link(dve.tensor_scalar(acc, first, float(P), None, ALU.mult))
                link(dve.tensor_tensor(pos, pos, over(acc, 1, TILES), ALU.add))
                for k, m in enumerate((m1, m2)):
                    link(dve.tensor_tensor(tmp, m, pos, ALU.mult))
                    link(dve.tensor_reduce(place[:, 0, k, :], tmp, AX.X, ALU.add))
                num, tile, row = (place[:, k] for k in range(3))
                link(dve.tensor_scalar(tile, num, P / 2 - 0.5, 1.0 / P, ALU.subtract, ALU.mult))
                link(dve.tensor_scalar(tile, tile, ROUND, None, ALU.add))
                link(dve.tensor_scalar(tile, tile, ROUND, None, ALU.subtract))
                link(dve.scalar_tensor_tensor(row, tile, -float(P), num, ALU.mult, ALU.add))
                tiles = lc[:, L_IOTA:L_IOTA + SLOT_TILES]
                for i in range(GROUPS):
                    c, m = i * OH // TILES, i * OH % TILES
                    dve.wait_ge(onehot_used, phase * GROUPS + i + 1)
                    dve.tensor_tensor(onehot[:, i % 2, :, 0:P], over(lc[:, L_IOTA:L_IOTA + P], 1, OH),
                                      over(row[:, c, m:m + OH], 2, P), ALU.is_equal)
                    for k in range(OH):
                        last = dve.tensor_scalar(onehot[:, i % 2, k, P:], tiles, tile[:, c, m + k:m + k + 1],
                                                 lc[:, L_TOK + i * OH + k:L_TOK + i * OH + k + 1], ALU.is_equal, ALU.mult)
                    last.then_inc(onehot_ready, 1)
                link(dve.tensor_scalar(expert_f[:, :], tiles, first[:, 1:2], None, ALU.is_ge))
                for e in range(2, E):
                    link(dve.scalar_tensor_tensor(expert_f[:, :], tiles, first[:, e:e + 1], expert_f[:, :],
                                                  ALU.is_ge, ALU.add))
                dve.tensor_copy(expert_of[:, :], expert_f[:, :]).then_inc(slots_ready, 1)
                dve.wait_ge(dest_ready, phase + 1)
                dest, token = dest_f[:, 0, :], dest_f[:, 1, :]
                dve.tensor_copy(dest_of[:, :], dest)
                link(dve.tensor_scalar(token, dest, TOK + 0.5, -float(TOK), ALU.is_gt, ALU.mult))
                link(dve.scalar_tensor_tensor(token, dest, -1.0, token, ALU.add, ALU.add))
                dve.tensor_scalar(token_of[:, :], token, 0.0, None, ALU.max).then_inc(token_of_ready, 1)
                link(dve.tensor_tensor(w, w, per_tile(top), ALU.mult))
                dve.tensor_reduce(sums[:, 0, 0:E], w.rearrange("p m e -> p e m"), AX.X, ALU.add).then_inc(
                    colsums_ready, 1)
                link(dve.reciprocal(count, count))
                dve.wait_ge(turn_free, u0 + ROUTER_USES + RING_CREDIT)
                link(dve.scalar_tensor_tensor(count, sums[:, 1, 0:E], 0.5, count, ALU.mult, ALU.mult))
                for k, m in enumerate((m1, m2)):
                    link(dve.tensor_tensor(tmp, m, over(count, 1, TILES), ALU.mult))
                    link(dve.tensor_reduce(tok_w[:, k, :], tmp, AX.X, ALU.add))

            def experts(phase):
                j0 = phase * SLOT_TILES

                def copy_rows(i, k):
                    dve.wait_ge(x_turned, j0 + i * R + k + 1 + ROWS_CREDIT)
                    dve.wait_ge(up_ready, j0 + i * R + k + 1)
                    dve.tensor_copy(xsT[:, k % 2, :], xt_ps[:, 0:P]).then_inc(xsT_ready, 1)

                def hidden_product(i, k):
                    dve.wait_ge(silu_ready, j0 + i * R + k + 1 + SILU_CREDIT)
                    dve.wait_ge(up_ready, j0 + i * R + k + 1 + UP_CREDIT)
                    dve.wait_ge(down_done, j0 + i * R + k + 1)
                    dve.tensor_tensor(hid[:, k % 2, :], silu[:, k % 2, :], up_ps[:, k % 2, :],
                                      ALU.mult).then_inc(h_ready, 1)

                def copy_out(i, k):
                    dve.wait_ge(down_done, j0 + i * R + k + 1 + DOWN_CREDIT)
                    if not isinstance(i, int) or j0 + i * R + k >= STORES:
                        dve.wait_ge(eo_stored, 16 * (j0 + i * R + k - STORES + 1))
                    dve.tensor_copy(eo[:, k % STORES, :], eo_ps[:, 0:D]).then_inc(eo_ready, 1)

                def place_up(i, k):
                    e = dve.value_load(expert_of[0:1, ds(i * R + k, 1)], min_val=0, max_val=E - 1)
                    dve.wait_ge(up_ready, j0 + i * R + k + 1)
                    dve.tensor_copy(up_now[:, k % 2, :], up_w[:, ds(e, 1), :].rearrange("p a i -> p (a i)")).then_inc(
                        up_now_ready, 1)

                def body(i, last=False):
                    for k in range(R):
                        if not last or k + 2 < R:
                            place_up(i, k + 2)
                            copy_rows(i, k + 2)
                        if not last or k + 1 < R:
                            hidden_product(i, k + 1)
                        copy_out(i, k)

                dve.wait_ge(e_in, 48 * (phase + 1))
                dve.wait_ge(slots_ready, phase + 1)
                for k in range(2):
                    place_up(0, k)
                    copy_rows(0, k)
                hidden_product(0, 0)
                body(0)
                with dve.Fori(1, GATHER_LOOPS - 1) as i:
                    body(i)
                body(GATHER_LOOPS - 1, last=True)

            def combine(phase, n):
                dve.wait_ge(y_in[n % 2], 16 * TOP_K * (phase * NB // 2 + n // 2 + 1))
                for c in range(TOP_K):
                    for m in range(n * B, (n + 1) * B):
                        y = ys[:, n % 2, c, (m - n * B) * D:(m - n * B + 1) * D]
                        last = dve.scalar_tensor_tensor(X[:, m, :], y, tok_w[:, c, m:m + 1], X[:, m, :],
                                                        ALU.mult, ALU.add)
                    link(last)
                dve.sem_inc(block_added, 1)

            def late_layernorms():
                dve.wait_ge(xnT_ready, 2)
                lsum, lmean, lssq, lstd = (rstats[:, k, :] for k in range(4))
                places = (xn[:, :, :], late_xn[:, 0], late_xn[:, 1])
                for n in range(1, NB):
                    x_block, ts, to = X[:, n * B:(n + 1) * B, :], slice(n * B, (n + 1) * B), places[n - 1]
                    link(dve.tensor_reduce(lsum[:, ts], x_block, AX.X, ALU.add))
                    link(dve.tensor_scalar(lmean[:, ts], lsum[:, ts], 1.0 / D, None, ALU.mult))
                    link(dve.tensor_tensor(to, x_block, over(lmean[:, ts], 2, D), ALU.subtract))
                    link(dve.tensor_tensor(sq, to, to, ALU.mult))
                    link(dve.tensor_reduce(lssq[:, ts], sq, AX.X, ALU.add))
                dve.sem_inc(late_sums, 1)
                dve.wait_ge(late_std, 1)
                link(dve.reciprocal(lstd[:, B:], lstd[:, B:]))
                for n in range(1, NB):
                    last = dve.tensor_tensor(places[n - 1], places[n - 1], over(lstd[:, n * B:(n + 1) * B], 2, D),
                                             ALU.mult)
                    last.then_inc(xn_ready if n == 1 else late_ready, 1)

            def by_step(a):
                if len(a.shape) == 2:
                    return a.rearrange("p (c r) -> p c r", r=CK)
                return a.rearrange("p (c r) x -> p c r x", r=CK)

            def lane_sums(n):
                dve.wait_ge(lanes_in, n + 1)
                a1, a2, a3 = (decay[:, d, 1:] for d in range(3))
                link(dve.tensor_tensor(decay[:, 1, 1:], a1, decay[:, 0, 0:P], ALU.mult))
                link(dve.tensor_tensor(decay[:, 2, 2:], decay[:, 1, 2:], decay[:, 0, 0:P - 1], ALU.mult))
                link(dve.tensor_tensor(decay4[:, :], by_step(a3)[:, :, 3], by_step(a1)[:, :, 0], ALU.mult))
                dve.wait_ge(qk_squared, n + 1)
                dve.tensor_reduce(norms[:, :, :], qk_sq.rearrange("p s i t -> p s t i"), AX.X,
                                  ALU.add).then_inc(qk_ssq, 1)

            def keep_halo(n):
                dve.wait_ge(ctrl_ready, 2 * B * (n + 1))
                dve.tensor_copy(xnT[:, :, 0:KT - 1], xnT[:, :, P:])
                link(dve.memset(tap_in[:, :], 1.0))
                dve.sem_inc(halo_ready, 1)

            def normalise_keys(n):
                dve.wait_ge(qk_std, n + 1)
                link(dve.reciprocal(norms[:, :, :], norms[:, :, :]))
                link(dve.tensor_tensor(kn.rearrange("p t i -> p i t"), qkv[:, 1], over(norms[:, 1, :], 1, HD),
                                       ALU.mult))

            def normalise_queries(n):
                link(dve.tensor_tensor(qn.rearrange("p t i -> p i t"), qkv[:, 0], over(norms[:, 0, :], 1, HD),
                                       ALU.mult))
                dve.sem_inc(queries_ready, 1)

            def scale_keys(n):
                link(dve.tensor_tensor(kb, kn, over(beta[:, :], 2, HD), ALU.mult))

            def keys_to_end(n):
                kb_c, ke_c = by_step(kb), by_step(kb_end)
                now = [by_step(decay[:, d, 1:]) for d in range(3)]
                for r in range(CK - 1):
                    dve.tensor_tensor(ke_c[:, :, r], kb_c[:, :, r], over(now[CK - 2 - r][:, :, CK - 1], 2, HD), ALU.mult)
                link(dve.tensor_copy(ke_c[:, :, CK - 1], kb_c[:, :, CK - 1]))

            def before_recurrence(n):
                kn_c, qn_c, kb_c, z_c = (by_step(a) for a in (kn, qn, kb, z))
                now = [by_step(decay[:, d, 1:]) for d in range(3)]
                prev = [by_step(decay[:, d, 0:P]) for d in range(3)]

                def wide(a):
                    return over(a, 2, HD)

                for r in range(CK):
                    if r == 0:
                        dve.tensor_scalar(z_c[:, :, r, 0:HD], kn_c[:, :, r], -1.0, None, ALU.mult)
                    else:
                        dve.scalar_tensor_tensor(z_c[:, :, r, 0:HD], kn_c[:, :, r], -1.0,
                                                 wide(prev[r - 1][:, :, r]), ALU.mult, ALU.mult)
                kk_rows = kk[:, 0:3 * P].rearrange("p (d c r) -> p d c r", d=3, r=CK)
                qk_rows = qk.rearrange("p d (c r) -> p d c r", r=CK)

                def dots(a_c, d, out):
                    n_r = CK - d
                    buf = score[:, self_at[0]:self_at[0] + NC * n_r * HD].rearrange("p (c r i) -> p c r i", c=NC, i=HD)
                    self_at[0] += NC * n_r * HD
                    flat = "p c r i -> p c (r i)"
                    last = dve.tensor_tensor(buf.rearrange(flat), a_c[:, :, d:, :].rearrange(flat),
                                             kb_c[:, :, 0:n_r, :].rearrange(flat), ALU.mult)
                    return last, buf, out[:, :, d:]

                for a_c, rows_, d0 in ((kn_c, kk_rows, 1), (qn_c, qk_rows, 0)):
                    self_at = [0]
                    made = [dots(a_c, d, rows_[:, d - d0]) for d in range(d0, CK)]
                    link(made[-1][0])
                    for _, buf, dst in made:
                        last = dve.tensor_reduce(dst, buf, AX.X, ALU.add)
                    link(last)
                for d in range(1, CK):
                    if d > 1:
                        dve.tensor_tensor(kk_rows[:, d - 1, :, d:], kk_rows[:, d - 1, :, d:],
                                          prev[d - 2][:, :, d:], ALU.mult)
                    last = dve.tensor_tensor(qk_rows[:, d, :, d:], qk_rows[:, d, :, d:], now[d - 1][:, :, d:], ALU.mult)
                link(last)
                dve.wait_ge(v_placed, n + 1)
                for s0 in range(CK - 1):
                    n_r = CK - 1 - s0
                    coef = kk[:, s0 + 1:s0 + 1 + n_r * (P + 1)].rearrange("p (r x) -> p r x", x=P + 1)
                    coef = coef[:, :, 0:P].rearrange("p r (c f) -> p r c f", f=CK)[:, :, :, 0]
                    tmp = fwd[:, 0:NC * n_r * 2 * HD].rearrange("p (c r x) -> p c r x", c=NC, x=2 * HD)
                    link(dve.tensor_tensor(tmp, over(z_c[:, :, s0, :], 2, n_r),
                                           over(coef.rearrange("p r c -> p c r"), 3, 2 * HD), ALU.mult))
                    last = dve.tensor_tensor(z_c[:, :, s0 + 1:, :], z_c[:, :, s0 + 1:, :], tmp, ALU.subtract)
                    link(last)
                dve.sem_inc(pre_done, 1)

            def angles(n, first=False):
                if not first:
                    dve.wait_ge(pairs_used, n)
                dve.wait_ge(turns_in, 2 * (n + 1))
                link(dve.scalar_tensor_tensor(ang, cos_a, -TWO_PI_HI, ang, ALU.mult, ALU.add))
                link(dve.scalar_tensor_tensor(ang, cos_a, -TWO_PI_LO, ang, ALU.mult, ALU.add))
                link(dve.tensor_scalar(ang, ang, PI_DOWN, -PI_DOWN, ALU.min, ALU.max))
                dve.scalar_tensor_tensor(cos_a, ang, -1.0, ang, ALU.mult, ALU.min).then_inc(ang_reduced, 1)

            def sum_terms(n, k):
                part_k, r = k // CK, k % CK
                cs = slice(PARTS[part_k], PARTS[part_k + 1])
                dve.wait_ge(terms_ready, READS * n + k + 1)
                dve.tensor_reduce(by_step(reads)[:, cs, r, :], terms[:, k % 4, 0:cs.stop - cs.start, :, 0:HD + r + 1],
                                  AX.X, ALU.add).then_inc(terms_used, 1)

            SUM_AT = (20, 21, 22, 24, 28, 29, 30, 31)

            def rotation_norms(n):
                dve.wait_ge(vstd_ready, 2 * (n + 1))
                link(dve.reciprocal(rv[:, :], rv[:, :]))
                link(dve.tensor_scalar(vec_ss[:, :], vec_ss[:, :], VEC_OVER, VEC_DOWN, ALU.is_lt, ALU.mult))
                dve.tensor_tensor(rv[:, :], rv[:, :], vec_ss[:, :], ALU.mult).then_inc(rv_ready, 1)

            NORMS_AT = 21

            def recurrence(n, more=True):
                z_c, ke_c, de_c = (by_step(a) for a in (z, kb_end, delta))
                mark, reached = chain.mark, chain.reached

                def addend(c):
                    return dve.tensor_copy(pred[:, c % 2, :, :, HD], z_c[:, c, :, HD:])

                link(addend(0))
                for c in range(NC):
                    st = states[:, c, :]
                    k = mark(dve.tensor_tensor(
                        pred[:, c % 2, :, :, 0:HD], over(z_c[:, c, :, 0:HD], 2, HD),
                        over(st.rearrange("p (j i) -> p j i", i=HD), 1, CK), ALU.mult))
                    dve.tensor_scalar(outer[:, :, CK], st, decay4[:, c:c + 1], None, ALU.mult)
                    reached(k)
                    k = mark(dve.tensor_reduce(de_c[:, c], pred[:, c % 2], AX.X, ALU.add))
                    if c + 1 < NC:
                        addend(c + 1)
                    reached(k)
                    link(dve.tensor_tensor(
                        outer[:, :, 0:CK].rearrange("p (j i) s -> p s j i", i=HD),
                        over(ke_c[:, c], 2, HD), over(de_c[:, c], 3, HD), ALU.mult))
                    link(dve.tensor_reduce(states[:, c + 1, :], outer[:, :, :], AX.X, ALU.add))
                    if c + 1 in PARTS:
                        dve.sem_inc(chain_done, 1)
                    if c == NORMS_AT:
                        rotation_norms(n)
                        if more:
                            angles(n + 1)
                    if c in SUM_AT:
                        sum_terms(n, SUM_AT.index(c))

            def after_recurrence(n, U, more=True):
                for k in range(READS - CK, READS):
                    sum_terms(n, k)
                dve.wait_ge(terms_used, READS * (n + 1) + 4)
                dve.sem_inc(reads_ready, 1)
                link(dve.tensor_copy(states[:, 0, :], states[:, NC, :]))
                dve.wait_ge(yv_ready, 2 * (n + 1))
                link(dve.tensor_tensor(yv, yv, over(lc[:, L_BOUT:L_BOUT + D], 1, B), ALU.add))
                if more:
                    normalise_queries(n + 1)
                dve.wait_ge(reads_squared, 2 * (n + 1))
                dve.tensor_reduce(read_norms[:, :], mem_sq.rearrange("p (m j) -> p m j", j=HD), AX.X,
                                  ALU.add).then_inc(reads_ssq, 1)
                if more:
                    scale_keys(n + 1)
                dve.wait_ge(reads_std, n + 1)
                link(dve.reciprocal(read_norms[:, :], read_norms[:, :]))
                dve.wait_ge(mem_in, 2 * (n + 1))
                mem3 = mem_tok.rearrange("p (m j) -> p m j", j=HD)
                dve.tensor_tensor(mem3, mem3, over(read_norms[:, :], 2, HD), ALU.mult).then_inc(mem_ready, 1)
                if more:
                    keys_to_end(n + 1)
                    keep_halo(n + 1)
                dve.wait_ge(gate_sig, n + 1)
                for half in range(2):
                    dve.wait_ge(turned, U + 8 + half + 1)
                    bs = slice(4 * half, 4 * half + 4)
                    dve.tensor_tensor(ym[:, bs], turn[:, (RING_ATT + half) % 2, :].rearrange("p (b d) -> p b d", d=D),
                                      yv[:, bs], ALU.add).then_inc(y_taken, 1)
                dve.wait_ge(y_taken, 2 * (n + 1))
                link(dve.tensor_tensor(ym, ym, gate, ALU.mult))
                xb = X[:, ds(n * B, B), :]
                link(dve.tensor_tensor(xb, xb, ym, ALU.add))
                dve.sem_inc(att_free, 1)

            def attention():
                combine(0, 0)
                layernorm(0, X[:, 0:B, :])
                for n in range(1, NB):
                    combine(0, n)
                late_layernorms()
                angles(0, first=True)
                lane_sums(0)
                normalise_keys(0)
                normalise_queries(0)
                scale_keys(0)
                keys_to_end(0)
                keep_halo(0)
                with dve.Fori(0, NB - 1) as n:
                    chain.restart()
                    before_recurrence(n)
                    recurrence(n)
                    lane_sums(n + 1)
                    normalise_keys(n + 1)
                    after_recurrence(n, RING_ATT + 2 * STAGE_USES + n * BLOCK_USES)
                chain.restart()
                before_recurrence(NB - 1)
                recurrence(NB - 1, more=False)
                after_recurrence(NB - 1, RING_ATT + STAGE_USES + (NB - 1) * BLOCK_USES, more=False)

            dve.memset(ones[:, :], 1.0)
            for k, v in enumerate((LN_EPS, RMS_EPS, NORM_EPS, RMS_EPS * VEC_DOWN ** 2, ROUND, -ROUND, np.pi / 2)):
                dve.memset(epsv[:, k:k + 1], v)
            for e in range(E):
                dve.memset(order[:, e:e + 1], float(E - e))
            dve.memset(states[:, 0, :], 0.0)
            dve.memset(decay[:, :, :], 1.0)
            dve.memset(xnT[:, :, 0:KT - 1], 0.0)
            link(dve.memset(sums[:, :, :], 0.0))
            dve.sem_inc(halo_ready, 1)
            dve.sem_inc(terms_used, 4)
            dve.sem_inc(consts_ready, 1)
            dve.sem_inc(turn_free, RING_CREDIT)
            dve.sem_inc(x_turned, ROWS_CREDIT)
            dve.sem_inc(xsT_ready, X_CREDIT)
            dve.sem_inc(up_ready, UP_CREDIT)
            dve.sem_inc(silu_ready, SILU_CREDIT)
            dve.sem_inc(h_ready, H_CREDIT)
            dve.sem_inc(down_done, DOWN_CREDIT)
            dve.sem_inc(eo_ready, EO_CREDIT)
            dve.sem_inc(onehot_used, 2)

            router(RING_ROUTER1, 0)
            dve.sem_inc(att_free, 1)
            experts(0)
            attention()
            router(RING_ROUTER2, 1)
            experts(1)
            for n in range(NB):
                combine(1, n)

        @block.gpsimd
        def _(pool):
            chain = Chain(pool, pool_step)
            link = chain.link
            link(pool.memset(vec[:, 0, :], 0.0))

            def normalise(phase):
                pool.wait_ge(rstd_ready, phase + 1)
                pool.wait_ge(rxT_ready, 2 * NB * (phase + 1))
                pool.nop(nofuse=True)
                for n in range(NB):
                    pool.tensor_tensor(rx[:, n], rx[:, n], over(rstats[:, 3, n * B:(n + 1) * B], 2, D),
                                       ALU.mult).then_inc(rows_ready, 1)

            def gathers(phase):
                loops0 = phase * GATHER_LOOPS
                pool.wait_ge(token_of_ready, phase + 1)
                pool.wait_ge(xn_stored, 16 * (NB + (NB + 2) * phase))

                def fetch(i, k, before=True):
                    half, column = k // (R // 2), k % (R // 2)
                    if column == 0:
                        if before:
                            for k2 in range(k, k + R // 2):
                                pool.wait_ge(rows_in[k2], 16 * (loops0 + i))
                                pool.nop(nofuse=True)
                        link(pool.tensor_copy(ids_now[:, half, :], token_of[:, ds(i * R + k, R // 2)]))
                        pool.nop(nofuse=True)
                    pool.wait_ge(x_turned, phase * SLOT_TILES + i * R + k + 1)
                    pool.nop(nofuse=True)
                    pool.indirect_dma_start(
                        out=rows[:, k, :], out_offset=None, in_=xn_dram,
                        in_offset=bass.IndirectOffsetOnAxis(ap=ids_now[:, half, column:column + 1], axis=0),
                    ).then_inc(rows_in[k], 16)

                def put(i, k):
                    half, column = k // (R // 2), k % (R // 2)
                    j = phase * SLOT_TILES + i * R + k
                    if not isinstance(j, int) or j > 0:
                        pool.wait_ge(eo_stored, 16 * j)
                        pool.nop(nofuse=True)
                    if column == 0:
                        link(pool.tensor_copy(ids_out[:, half, :], dest_of[:, ds(i * R + k, R // 2)]))
                        pool.nop(nofuse=True)
                    pool.wait_ge(eo_ready, j + 1 + EO_CREDIT)
                    pool.nop(nofuse=True)
                    pool.indirect_dma_start(
                        out=y_dram, out_offset=bass.IndirectOffsetOnAxis(ap=ids_out[:, half, column:column + 1], axis=0),
                        in_=eo[:, k % STORES, :], in_offset=None,
                    ).then_inc(eo_stored, 16)

                for k in range(R):
                    fetch(0, k, before=False)
                for k in range(R):
                    fetch(1, k)
                    put(0, k)
                with pool.Fori(2, GATHER_LOOPS) as i:
                    chain.enter(i - 2, 4)
                    for k in range(R):
                        fetch(i, k)
                        put(i - 1, k)
                chain.leave(GATHER_LOOPS - 2, 4)
                for k in range(R):
                    put(GATHER_LOOPS - 1, k)

            def rotation(n):
                chain.restart()
                pool.wait_ge(ctrl_ready, 2 * B * (n + 1))
                pool.nop(nofuse=True)
                pool.tensor_tensor(gate_raw, gate_raw, over(lc[:, L_BOG:L_BOG + D], 1, B), ALU.add).then_inc(
                    og_biased, 1)
                pool.wait_ge(sincos_ready, n + 1)
                pool.nop(nofuse=True)
                n_t = BB * P
                pool.tensor_tensor(rot_rows[:, 0], rot_rows[:, 0], part[:, 0], ALU.subtract)
                link(pool.tensor_tensor(rot_rows[:, 1], rot_rows[:, 1], part[:, 1], ALU.add))
                for r in range(2):
                    pool.tensor_tensor(rot_rows[:, r], rot_rows[:, r], over(upd[:, r * n_t:(r + 1) * n_t], 1, 2),
                                       ALU.mult)
                link(pool.tensor_tensor(vprod[:, 0:2 * n_t], upd, cand, ALU.mult))
                by_time = lambda a: a.rearrange("p (c m l) -> p l c m", c=2, l=SEG)
                for c in range(2):
                    last = pool.tensor_tensor(run[:, :, c, 2, :], by_time(cand)[:, :, c],
                                              by_time(vprod[:, 0:2 * n_t])[:, :, c], ALU.subtract)
                link(last)
                pool.sem_inc(pairs_used, 1)
                A = rot.rearrange("p r c n (g l) -> p l r c (n g)", l=SEG)
                link(pool.tensor_copy(run[:, 0, :, 0:2, :], A[:, 0]))
                prod = [vprod[:, k * 6 * n_s:(k + 1) * 6 * n_s].rearrange("p (r c m) -> p r c m", r=2, c=3)
                        for k in range(2)]
                for l in range(1, SEG):
                    for k in range(2):
                        last = pool.tensor_tensor(prod[k], over(A[:, l, :, k], 2, 3),
                                                  over(run[:, l - 1, k], 1, 2), ALU.mult)
                    link(last)
                    pool.tensor_tensor(run[:, l, :, 0:2, :], prod[0][:, :, 0:2], prod[1][:, :, 0:2], ALU.add)
                    link(pool.tensor_tensor(prod[0][:, :, 2], prod[0][:, :, 2], prod[1][:, :, 2], ALU.add))
                    link(pool.tensor_tensor(run[:, l, :, 2, :], run[:, l, :, 2, :], prod[0][:, :, 2], ALU.add))
                pool.wait_ge(queries_ready, n + 1)
                pool.nop(nofuse=True)
                qn_c = qn.rearrange("p (c r) i -> p c r i", r=CK)
                qs_c = q_state.rearrange("p (c r) i -> p c r i", r=CK)
                for r in range(CK):
                    since = decay4[:, :] if r == CK - 1 else decay[:, r, 1:].rearrange("p (c r) -> p c r", r=CK)[:, :, r]
                    last = pool.tensor_tensor(qs_c[:, :, r], qn_c[:, :, r], over(since, 2, HD), ALU.mult)
                last.then_inc(q_state_ready, 1)
                last_map = run[:, SEG - 1].rearrange("p r c (n g) -> p r c n g", g=NG)
                for g in range(NG):
                    step = vprod[:, 0:4 * BB].rearrange("p (r c n) -> p r c n", r=2, c=2)
                    total = vprod[:, 4 * BB:6 * BB].rearrange("p (r n) -> p r n", r=2)
                    link(pool.tensor_tensor(step, last_map[:, :, 0:2, :, g],
                                            over(vec[:, g, :].rearrange("p (c n) -> p c n", c=2), 1, 2), ALU.mult))
                    link(pool.tensor_tensor(total, step[:, :, 0], step[:, :, 1], ALU.add))
                    link(pool.tensor_tensor(vec[:, g + 1, :].rearrange("p (r n) -> p r n", r=2), total,
                                            last_map[:, :, 2, :, g], ALU.add))
                halves = [vprod[:, k * 2 * n_t:(k + 1) * 2 * n_t] for k in range(2)]
                for c in range(2):
                    for k in range(2):
                        last = pool.tensor_tensor(
                            halves[c][:, k * n_t:(k + 1) * n_t].rearrange("p (l n g) -> p l n g", n=BB, g=NG),
                            run[:, :, k, c, :].rearrange("p l (n g) -> p l n g", g=NG),
                            over(vec[:, 0:NG, c * BB:(c + 1) * BB].rearrange("p g n -> p n g"), 1, SEG), ALU.mult)
                link(last)
                link(pool.tensor_tensor(halves[0], halves[0], halves[1], ALU.add))
                for k in range(2):
                    part_k = halves[0][:, k * n_t:(k + 1) * n_t].rearrange("p (l m) -> p l m", l=SEG)
                    last = pool.tensor_tensor(part_k, part_k, run[:, :, k, 2, :], ALU.add)
                link(last)
                pool.wait_ge(att_free, n + 1)
                pool.nop(nofuse=True)
                pool.wait_ge(xn_stored, 16 * (NB + 2))
                pool.nop(nofuse=True)
                for k in range(2):
                    last = pool.tensor_scalar(
                        vec_cut[:, k * BB:(k + 1) * BB, :].rearrange("p n (g l) -> p (n g) l", l=SEG),
                        halves[0][:, k * n_t:(k + 1) * n_t].rearrange("p (l m) -> p m l", l=SEG),
                        VEC_CUT, -VEC_CUT, ALU.min, ALU.max)
                last.then_inc(vec_ready, 1)
                link(pool.tensor_copy(vec[:, 0, :], vec[:, NG, :]))

            def read_terms(n):
                de_c = delta.rearrange("p (c r) j -> p c r j", r=CK)
                qk_c = qk.rearrange("p d (c r) -> p d c r", r=CK)
                qs_c = q_state.rearrange("p (c r) i -> p c r i", r=CK)
                for k in range(READS):
                    part_k, r = k // CK, k % CK
                    cs = slice(PARTS[part_k], PARTS[part_k + 1])
                    n_c = cs.stop - cs.start
                    before = states[:, cs, :].rearrange("p c (j i) -> p c j i", i=HD)
                    if r == 0:
                        pool.wait_ge(chain_done, (len(PARTS) - 1) * n + part_k + 1)
                        pool.nop(nofuse=True)
                    pool.wait_ge(terms_used, READS * n + k + 1)
                    pool.nop(nofuse=True)
                    last = pool.tensor_tensor(terms[:, k % 4, 0:n_c, :, 0:HD], before, over(qs_c[:, cs, r, :], 2, HD),
                                              ALU.mult)
                    for d in range(r + 1):
                        last = pool.tensor_tensor(terms[:, k % 4, 0:n_c, :, HD + d], de_c[:, cs, r - d, :],
                                                  over(qk_c[:, d, cs, r], 2, HD), ALU.mult)
                    last.then_inc(terms_ready, 1)

            n_s = BB * NG
            normalise(0)
            pool.wait_ge(c_in, 32)
            pool.wait_ge(w_in, 16 * 7)
            pool.tensor_tensor(second_w[:, :, :], second_w[:, :, :], over(second_tmp, 1, KT), ALU.mult)
            pool.tensor_tensor(second_b[:, :], second_b[:, :], tap_rows[:, :], ALU.mult)
            pool.tensor_copy(tap_in[:, :], lc[0:KT, L_TAPS:L_END])
            pool.tensor_scalar(mem_w[:, :], mem_w[:, :], lc[:, L_RMSM:L_RMSM + 1], None, ALU.mult)
            for c in range(2):
                last = pool.tensor_scalar(vec_w[:, c, :], vec_w[:, c, :], lc[:, L_RMSV + c:L_RMSV + c + 1], None,
                                          ALU.mult)
            last.then_inc(weights_ready, 1)
            gathers(0)
            with pool.Fori(0, NB) as n:
                rotation(n)
                read_terms(n)
            normalise(1)
            gathers(1)


def lane_constants(x):
    bc = x["L0_attn_b_ctrl"]
    lc = np.zeros((P, L_END), np.float32)
    lanes_bp = lambda a: np.tile(a, (2, 1))
    lc[:, L_BU:L_BC] = lanes_bp(bc[C_UG:C_ANG].reshape(NPAIR, 2))
    lc[:, L_BC:L_BANG] = lanes_bp(bc[C_CAND:C_Q].reshape(NPAIR, 2))
    lc[:, L_BANG:L_WB] = lanes_bp(bc[C_ANG:C_CAND].reshape(NPAIR, 1))
    lc[:, L_WB:L_RMSV] = lanes_bp(x["L0_attn_W_block"].reshape(NPAIR, 4))
    lc[:, L_RMSV:L_RMSM] = lanes_bp(x["L0_attn_rms_v_w"].reshape(NPAIR, 2))
    lc[:, L_RMSM] = np.tile(x["L0_attn_rms_m_w"], H)
    lc[:, L_BOG:L_BOUT] = bc[C_OG:C_END]
    lc[:, L_BOUT:L_ID] = x["L0_attn_b_out"]
    lc[:, L_ID:L_PAIR] = np.eye(P, dtype=np.float32)
    lc[:, L_PAIR:L_IOTA] = np.repeat(np.eye(2, dtype=np.float32), NPAIR, axis=0)
    lc[:, L_IOTA:L_TOK] = np.arange(P)
    lc[:, L_TOK:L_TRI] = 1 + np.arange(TOP_K * TOK).reshape(TOP_K * TILES, P).T
    lc[:, L_TRI:L_TAPS] = np.triu(np.ones((P, P), np.float32), 1)
    lc[0:KT, L_TAPS:L_END] = np.arange(KT)[:, None] + np.arange(P)[None, :] >= KT - 1
    return lc


def control_columns():
    by_pair = lambda c0: c0 + np.arange(D).reshape(NPAIR, 2).T.ravel()
    by_head = lambda c0: c0 + np.arange(D).reshape(H, HD).T.ravel()
    return np.concatenate([by_pair(C_UG), np.arange(C_ANG, C_CAND), by_pair(C_CAND), np.arange(C_OG, C_END),
                           by_head(C_Q), by_head(C_K), by_head(C_V), np.arange(C_A, C_OG)])


def kernel(**inputs):
    import concourse.bacc as bacc
    from concourse.bass_utils import run_bass_kernel_spmd

    x = {k: np.asarray(v) for k, v in inputs.items()}
    w_out = x["L0_attn_W_out"]
    w_ctrl = x["L0_attn_W_ctrl"][:, control_columns()]
    taps = np.zeros((KT, SECOND), np.float32)
    for s3, k in enumerate("qkv"):
        taps[:, s3 * D:(s3 + 1) * D] = x[f"L0_attn_{k}conv_w"].reshape(H, HD, KT).transpose(2, 1, 0).reshape(KT, D)
    taps[KT - 1, QKV:] = 1.0
    w_vec = np.zeros((2, NPAIR, 2, 2, D), np.float32)
    for b in range(2):
        w_vec[b, :, :, b] = w_out[D:].reshape(NPAIR, 2, D)
    arrays = {
        "hidden": x["L0_attn_hidden"],
        "w_first": w_ctrl[:, :FIRST],
        "w_second": w_ctrl[:, FIRST:],
        "taps": np.broadcast_to(taps, (P, KT, SECOND)),
        "tap_rows_in": taps,
        "bias_second": np.broadcast_to(x["L0_attn_b_ctrl"][control_columns()[FIRST:]], (KT, SECOND)),
        "lane_consts": lane_constants(x),
        "w_mem": w_out[:D],
        "w_vec": w_vec.reshape(P, 2, 2 * D),
        "router_wt": x["L0_ffn_router_w"].T,
        "gate_wt": x["L0_ffn_gate_w"].transpose(2, 0, 1),
        "up_wt": x["L0_ffn_up_w"].transpose(2, 0, 1),
        "down_wt": x["L0_ffn_down_w"].reshape(E, D, CH, P).transpose(3, 0, 2, 1),
    }
    arrays = {k: np.ascontiguousarray(v) for k, v in arrays.items()}
    nc = bacc.Bacc("TRN2", target_bir_lowering=False, num_devices=1)
    args = [nc.dram_tensor(k, v.shape, F32, kind="ExternalInput").ap() for k, v in arrays.items()]
    out = nc.dram_tensor("out", (B, S, D), F32, kind="ExternalOutput").ap()
    macaron_kernel(nc, *args, out)
    r = run_bass_kernel_spmd(nc, [arrays], core_ids=[0])
    return r.results[0]["out"]
```
